# Optimizing a Trainium2 kernel written in Bass

```python
import numpy as np
import jax
import jax.numpy as jnp

def _softmax(x, axis=-1):
    return jax.nn.softmax(x, axis=axis)

def _gelu(x):
    return jax.nn.gelu(x, approximate=True)

def _silu(x):
    return jax.nn.silu(x)

def _sigmoid(x):
    return jax.nn.sigmoid(x)

def _layernorm(x, axis=-1, eps=1e-05):
    m = jnp.mean(x, axis=axis, keepdims=True)
    v = jnp.var(x, axis=axis, keepdims=True)
    return (x - m) / jnp.sqrt(v + eps)

def _scatter_add(tgt, idx, src, axis=0):
    return tgt.at[idx].add(src)

def _segment_sum(src, seg, n):
    return jax.ops.segment_sum(src, seg, n)
kernel_name = 'mk_seq_preln_d2_jaxref_r4_515e0a'

def setup_inputs(seed: int=0):
    np.random.seed(seed)
    _w = jnp.asarray

    def _L0_attn_setup():
        import jax, jax.numpy as jnp
        import numpy as np
        B, T, D_MODEL, N = (4, 512, 256, 16)
        D_INNER = 2 * D_MODEL

        def _ssm_scan(x_in, A, B_ssm, C_ssm):

            def step(state, ins):
                x_t, a_t, b_t, c_t = ins
                decay = jnp.exp(a_t)
                state = state * decay[:, None, :] + x_t[:, :, None] * b_t[:, None, :]
                out_t = (state * c_t[:, None, :]).sum(-1)
                return (state, out_t)
            b, t, d = x_in.shape
            n = A.shape[-1]
            init = jnp.zeros((b, d, n), dtype=x_in.dtype)
            xs = (jnp.swapaxes(x_in, 0, 1), jnp.swapaxes(A, 0, 1), jnp.swapaxes(B_ssm, 0, 1), jnp.swapaxes(C_ssm, 0, 1))
            _, outs = jax.lax.scan(step, init, xs)
            return jnp.swapaxes(outs, 0, 1)
        key = jax.random.key(seed)
        ks = jax.random.split(key, 7)
        s = 0.02
        return {'x': jax.random.normal(ks[0], (B, T, D_MODEL), dtype=jnp.float32), 'W_in': jax.random.normal(ks[1], (D_MODEL, 2 * D_INNER), dtype=jnp.float32) * s, 'W_A': jax.random.normal(ks[2], (D_INNER, N), dtype=jnp.float32) * s, 'W_B': jax.random.normal(ks[3], (D_INNER, N), dtype=jnp.float32) * s, 'W_C': jax.random.normal(ks[4], (D_INNER, N), dtype=jnp.float32) * s, 'W_out': jax.random.normal(ks[5], (D_INNER, D_MODEL), dtype=jnp.float32) * s, 'norm_w': jnp.ones((D_INNER,), dtype=jnp.float32)}
    _L0_attn_in = _L0_attn_setup()

    def _L0_ffn_setup():
        import jax, jax.numpy as jnp
        import numpy as np
        B, S, D, H, O, E, K = (4, 512, 256, 512, 256, 8, 2)
        key = jax.random.key(seed)
        ks = jax.random.split(key, 8)
        x = jax.random.normal(ks[0], (B, S, D), dtype=jnp.float32)
        gate_w = jax.random.uniform(ks[1], (E, D), dtype=jnp.float32, minval=-1, maxval=1) * np.sqrt(6.0 / D)
        gate_b = jnp.zeros((E,), dtype=jnp.float32)
        w1 = jax.random.uniform(ks[2], (E, D, H), dtype=jnp.float32, minval=-1, maxval=1) * np.sqrt(6.0 / D)
        b1 = jnp.zeros((E, H), dtype=jnp.float32)
        w2 = jax.random.uniform(ks[3], (E, H, O), dtype=jnp.float32, minval=-1, maxval=1) * np.sqrt(6.0 / H)
        b2 = jnp.zeros((E, O), dtype=jnp.float32)
        return {'x': x, 'gate_w': gate_w, 'gate_b': gate_b, 'w1': w1, 'b1': b1, 'w2': w2, 'b2': b2}
    _L0_ffn_in = _L0_ffn_setup()

    def _L1_attn_setup():
        import jax, jax.numpy as jnp
        import numpy as np
        D_MODEL = 256
        NUM_HEADS = 16
        HEAD_DIM = D_MODEL // NUM_HEADS
        ROPE_THETA = 10000.0

        def apply_rope(x):
            S, d_k = (x.shape[-2], x.shape[-1])
            inv_freq = ROPE_THETA ** (jnp.arange(0, d_k, 2, dtype=jnp.float32) / d_k)
            ang = jnp.arange(S, dtype=jnp.float32)[:, None] / inv_freq[None, :]
            cos, sin = (jnp.cos(ang), jnp.sin(ang))
            xp = x.reshape(x.shape[:-1] + (d_k // 2, 2))
            x0, x1 = (xp[..., 0], xp[..., 1])
            out = jnp.stack([x0 * cos - x1 * sin, x0 * sin + x1 * cos], axis=-1)
            return out.reshape(x.shape)
        key = jax.random.key(seed)
        k1, k2, k3 = jax.random.split(key, 3)
        B, S = (2, 512)
        std = 2.0 / (D_MODEL + 3 * D_MODEL)
        std_o = 2.0 / (D_MODEL + D_MODEL)
        return {'x': jax.random.normal(k1, (B, S, D_MODEL), dtype=jnp.float32), 'W_qkv': jax.random.normal(k2, (3 * D_MODEL, D_MODEL), dtype=jnp.float32) * std, 'W_o': jax.random.normal(k3, (D_MODEL, D_MODEL), dtype=jnp.float32) * std_o}
    _L1_attn_in = _L1_attn_setup()

    def _L1_ffn_setup():
        import jax, jax.numpy as jnp
        import numpy as np
        B, S, D = (2, 512, 256)
        E, K, F = (16, 2, 128)
        FS = 256
        key = jax.random.key(seed)
        ks = jax.random.split(key, 8)

        def w(k, shape, fan_in):
            return jax.random.normal(k, shape, jnp.float32) / np.sqrt(fan_in).astype(np.float32)
        return {'x': jax.random.normal(ks[0], (B, S, D), jnp.float32), 'Wr': w(ks[1], (D, E), D), 'Wg': w(ks[2], (E, D, F), D), 'Wu': w(ks[3], (E, D, F), D), 'Wd': w(ks[4], (E, F, D), F), 'Sg': w(ks[5], (D, FS), D), 'Su': w(ks[6], (D, FS), D), 'Sd': w(ks[7], (FS, D), FS)}
    _L1_ffn_in = _L1_ffn_setup()
    _d = {'L0_attn_x': _L0_attn_in['x'], 'L0_attn_W_in': _L0_attn_in['W_in'], 'L0_attn_W_A': _L0_attn_in['W_A'], 'L0_attn_W_B': _L0_attn_in['W_B'], 'L0_attn_W_C': _L0_attn_in['W_C'], 'L0_attn_W_out': _L0_attn_in['W_out'], 'L0_attn_norm_w': _L0_attn_in['norm_w'], 'L0_ffn_gate_w': _L0_ffn_in['gate_w'], 'L0_ffn_gate_b': _L0_ffn_in['gate_b'], 'L0_ffn_w1': _L0_ffn_in['w1'], 'L0_ffn_b1': _L0_ffn_in['b1'], 'L0_ffn_w2': _L0_ffn_in['w2'], 'L0_ffn_b2': _L0_ffn_in['b2'], 'L1_attn_W_qkv': _L1_attn_in['W_qkv'], 'L1_attn_W_o': _L1_attn_in['W_o'], 'L1_ffn_Wr': _L1_ffn_in['Wr'], 'L1_ffn_Wg': _L1_ffn_in['Wg'], 'L1_ffn_Wu': _L1_ffn_in['Wu'], 'L1_ffn_Wd': _L1_ffn_in['Wd'], 'L1_ffn_Sg': _L1_ffn_in['Sg'], 'L1_ffn_Su': _L1_ffn_in['Su'], 'L1_ffn_Sd': _L1_ffn_in['Sd']}
    _x0 = _d['L0_attn_x']
    _d['L0_attn_x'] = jax.random.normal(jax.random.fold_in(jax.random.key(seed), 1), (4, 1024, 256), dtype=_x0.dtype)
    del _x0
    return _d

def reference(L0_attn_x, L0_attn_W_in, L0_attn_W_A, L0_attn_W_B, L0_attn_W_C, L0_attn_W_out, L0_attn_norm_w, L0_ffn_gate_w, L0_ffn_gate_b, L0_ffn_w1, L0_ffn_b1, L0_ffn_w2, L0_ffn_b2, L1_attn_W_qkv, L1_attn_W_o, L1_ffn_Wr, L1_ffn_Wg, L1_ffn_Wu, L1_ffn_Wd, L1_ffn_Sg, L1_ffn_Su, L1_ffn_Sd):

    def _L0_attn_ref(x, W_in, W_A, W_B, W_C, W_out, norm_w):
        import jax, jax.numpy as jnp
        import numpy as np
        B, T, D_MODEL, N = (4, 512, 256, 16)
        D_INNER = 2 * D_MODEL

        def _ssm_scan(x_in, A, B_ssm, C_ssm):

            def step(state, ins):
                x_t, a_t, b_t, c_t = ins
                decay = jnp.exp(a_t)
                state = state * decay[:, None, :] + x_t[:, :, None] * b_t[:, None, :]
                out_t = (state * c_t[:, None, :]).sum(-1)
                return (state, out_t)
            b, t, d = x_in.shape
            n = A.shape[-1]
            init = jnp.zeros((b, d, n), dtype=x_in.dtype)
            xs = (jnp.swapaxes(x_in, 0, 1), jnp.swapaxes(A, 0, 1), jnp.swapaxes(B_ssm, 0, 1), jnp.swapaxes(C_ssm, 0, 1))
            _, outs = jax.lax.scan(step, init, xs)
            return jnp.swapaxes(outs, 0, 1)
        D = W_A.shape[0]
        xz = jnp.einsum('btm,md->btd', x, W_in)
        x_in = jax.nn.silu(xz[..., :D]) * jax.nn.sigmoid(xz[..., D:])
        A = -jnp.exp(jnp.clip(jnp.einsum('btd,dn->btn', x_in, W_A), -5.0, 0.0))
        B_ssm = jnp.einsum('btd,dn->btn', x_in, W_B)
        C_ssm = jnp.einsum('btd,dn->btn', x_in, W_C)
        out = _ssm_scan(x_in.astype(jnp.float32), A.astype(jnp.float32), B_ssm.astype(jnp.float32), C_ssm.astype(jnp.float32))
        out = out.astype(x.dtype)
        eps = jnp.finfo(jnp.float32).eps
        out = out * jax.lax.rsqrt(jnp.mean(out * out, axis=-1, keepdims=True) + eps) * norm_w
        return jnp.einsum('btd,dm->btm', out, W_out)

    def _L0_ffn_ref(x, gate_w, gate_b, w1, b1, w2, b2):
        import jax, jax.numpy as jnp
        import numpy as np
        B, S, D, H, O, E, K = (4, 512, 256, 512, 256, 8, 2)
        logits = jnp.einsum('bsd,ed->bse', x, gate_w) + gate_b
        probs = jax.nn.softmax(logits, axis=-1)
        topk_vals, topk_idx = jax.lax.top_k(probs, K)
        h = jax.nn.relu(jnp.einsum('bsd,edh->bseh', x, w1) + b1)
        expert_out = jnp.einsum('bseh,eho->bseo', h, w2) + b2
        sel = jnp.take_along_axis(expert_out, topk_idx[..., None], axis=2)
        return jnp.sum(sel * topk_vals[..., None], axis=2)

    def _L1_attn_ref(x, W_qkv, W_o):
        import jax, jax.numpy as jnp
        import numpy as np
        D_MODEL = 256
        NUM_HEADS = 16
        HEAD_DIM = D_MODEL // NUM_HEADS
        ROPE_THETA = 10000.0

        def apply_rope(x):
            S, d_k = (x.shape[-2], x.shape[-1])
            inv_freq = ROPE_THETA ** (jnp.arange(0, d_k, 2, dtype=jnp.float32) / d_k)
            ang = jnp.arange(S, dtype=jnp.float32)[:, None] / inv_freq[None, :]
            cos, sin = (jnp.cos(ang), jnp.sin(ang))
            xp = x.reshape(x.shape[:-1] + (d_k // 2, 2))
            x0, x1 = (xp[..., 0], xp[..., 1])
            out = jnp.stack([x0 * cos - x1 * sin, x0 * sin + x1 * cos], axis=-1)
            return out.reshape(x.shape)
        B, S, d_model = x.shape
        H, d_k = (NUM_HEADS, HEAD_DIM)
        qkv = jnp.einsum('bsi,oi->bso', x, W_qkv)
        Q, K, V = jnp.split(qkv, 3, axis=-1)

        def to_heads(t):
            return t.reshape(B, S, H, d_k).transpose(0, 2, 1, 3)
        Q, K, V = (to_heads(Q), to_heads(K), to_heads(V))
        Q, K = (apply_rope(Q), apply_rope(K))
        scores = jnp.einsum('bhqd,bhkd->bhqk', Q, K) / jnp.sqrt(jnp.float32(d_k))
        causal = jnp.tril(jnp.ones((S, S), dtype=bool))
        scores = jnp.where(causal, scores, -jnp.inf)
        attn = jax.nn.softmax(scores, axis=-1)
        out = jnp.einsum('bhqk,bhkd->bhqd', attn, V)
        out = out.transpose(0, 2, 1, 3).reshape(B, S, d_model)
        return jnp.einsum('bsi,oi->bso', out, W_o)

    def _L1_ffn_ref(x, Wr, Wg, Wu, Wd, Sg, Su, Sd):
        import jax, jax.numpy as jnp
        import numpy as np
        B, S, D = (2, 512, 256)
        E, K, F = (16, 2, 128)
        FS = 256
        b, s, d = x.shape
        T = b * s
        xf = x.reshape(T, d)
        shared = jax.nn.silu(xf @ Sg) * (xf @ Su) @ Sd
        probs = jax.nn.softmax(xf @ Wr, axis=-1)
        topk_p, topk_i = jax.lax.top_k(probs, K)
        n_exp = Wr.shape[1]
        cw = jnp.zeros((T, n_exp), x.dtype).at[jnp.arange(T)[:, None], topk_i].add(topk_p)

        def step(acc, ew):
            wg, wu, wd, c = ew
            y = jax.nn.silu(xf @ wg) * (xf @ wu) @ wd
            return (acc + y * c[:, None], None)
        routed, _ = jax.lax.scan(step, jnp.zeros_like(xf), (Wg, Wu, Wd, cw.T))
        return (routed + shared).reshape(b, s, d)
    x = L0_attn_x
    x = x + _L0_attn_ref(_layernorm(x, axis=-1), L0_attn_W_in, L0_attn_W_A, L0_attn_W_B, L0_attn_W_C, L0_attn_W_out, L0_attn_norm_w)
    x = x + _L0_ffn_ref(_layernorm(x, axis=-1), L0_ffn_gate_w, L0_ffn_gate_b, L0_ffn_w1, L0_ffn_b1, L0_ffn_w2, L0_ffn_b2)
    x = x + _L1_attn_ref(_layernorm(x, axis=-1), L1_attn_W_qkv, L1_attn_W_o)
    x = x + _L1_ffn_ref(_layernorm(x, axis=-1), L1_ffn_Wr, L1_ffn_Wg, L1_ffn_Wu, L1_ffn_Wd, L1_ffn_Sg, L1_ffn_Su, L1_ffn_Sd)
    return x

_drawn_inputs = setup_inputs


def setup_inputs(seed=0):
    import zlib

    import numpy as np

    out = dict(_drawn_inputs(seed))
    spreads = {'L0_attn_norm_w': (1.0, 0.2),
     'L0_ffn_gate_b': (0.0, 0.1),
     'L0_ffn_b1': (0.0, 0.1),
     'L0_ffn_b2': (0.0, 0.1)}
    factors = {'L0_attn_W_A': 3.454, 'L1_attn_W_qkv': 21.958, 'L1_attn_W_o': 8.0}
    for name, (base, spread) in spreads.items():
        noise = np.random.default_rng([zlib.crc32(name.encode()), seed]).standard_normal(out[name].shape)
        drawn = base * np.exp(spread * noise) if base else spread * noise
        out[name] = jnp.asarray(drawn.astype(out[name].dtype))
    for name, factor in factors.items():
        out[name] = (out[name] * factor).astype(out[name].dtype)
    return out
```

```python
import concourse.bass as bass
from concourse import mybir
from contextlib import ExitStack

FP32 = mybir.dt.float32
FP32R = mybir.dt.float32r
BF16 = mybir.dt.bfloat16
U32 = mybir.dt.uint32
ALU = mybir.AluOpType
ACT = mybir.ActivationFunctionType
AXX = mybir.AxisListType.X

P = 128
H = P // 2
BATCH, SEQ, DM = 4, 1024, 256
TOK = BATCH * SEQ
NT = TOK // P
TPB = SEQ // P
KD = DM // P
LN_EPS = 1e-5

DI, NS = 512, 16
KI = DI // P
NH, HD = 16, 16
RMS_EPS = 1.1920929e-07


class Chain:

    def __init__(self, eng, sem, per_tile):
        self.eng, self.sem, self.per, self.k, self.base = eng, sem, per_tile, 0, 0

    def at(self, t):
        assert self.k in (0, self.per), (self.k, self.per)
        self.base, self.k = t * self.per, 0

    def step(self, ins):
        ins.then_inc(self.sem, 1)
        self.k += 1
        return ins

    def wait(self):
        self.eng.wait_ge(self.sem, self.base + self.k)

    def link(self, ins):
        self.step(ins)
        self.wait()


def wait_apart(eng, const_ready, *waits):
    values = [(s, v if isinstance(v, int) else eng.compute_val(v)) for s, v in waits if not isinstance(v, int) or v > 0]
    eng.wait_ge(const_ready, 6)
    for s, v in values:
        eng.wait_ge(s, v)


def wait(eng, sem, value):
    if not isinstance(value, int) or value > 0:
        eng.wait_ge(sem, value)


def pipeline(eng, tiles, stages, unroll=2, order=None):
    n = len(stages)
    order = order or range(n)
    first = -(-(n + 1) // unroll) * unroll

    def at(tau):
        for s in order:
            if 0 <= tau - s < tiles:
                stages[s](tau - s, (tau - s) // unroll, (tau - s) % unroll)

    for tau in range(first):
        at(tau)
    with eng.Fori(first // unroll, tiles // unroll) as turn:
        for r in range(unroll):
            for s in order:
                d = r - s
                stages[s](turn * unroll + d, turn + d // unroll, d % unroll)
    for tau in range(tiles, tiles + n - 1):
        at(tau)


def constants(nc, sb, sem):
    c = {}
    c["ident"] = ident = sb("ident", [P, P])
    c["neg_tri"] = neg_tri = sb("neg_tri", [P, P])
    c["neg_suf"] = neg_suf = sb("neg_suf", [P, P])
    c["neg_mid0"] = neg_mid0 = sb("neg_mid0", [P, P])
    c["neg_mid1"] = neg_mid1 = sb("neg_mid1", [P, P])
    c["neg_own"] = neg_own = sb("neg_own", [P, P])
    c["neg_one"] = neg_one = sb("neg_one", [P, 1])
    c["one"] = one = sb("one", [P, 1])
    c["ones_row"] = ones_row = sb("ones_row", [1, P])
    c["mhalf"] = mhalf = sb("mhalf", [P, 4])
    c["causal4"] = causal4 = sb("causal4", [P, 4, P])
    made = sem("const_filled")
    ready = sem("const_ready")
    c["ready"] = ready
    with nc.Block() as block:
        @block.gpsimd
        def _(pool):
            fills = ((ident, 0.0), (neg_tri, -1.0), (neg_suf, -1.0), (neg_one, -1.0), (one, 1.0),
                     (ones_row, 1.0), (mhalf, -0.5), (causal4, 1.0), (neg_mid1, 0.0))
            for tile, value in fills:
                nc.gpsimd.memset(tile[:], value).then_inc(made, 1)
            pool.wait_ge(made, len(fills))
            nc.gpsimd.affine_select(out=ident[:], in_=ident[:], compare_op=ALU.not_equal, fill=1.0, base=0,
                                    pattern=[[-1, P]], channel_multiplier=1).then_inc(ready, 1)
            nc.gpsimd.affine_select(out=neg_tri[:], in_=neg_tri[:], compare_op=ALU.is_ge, fill=0.0, base=0,
                                    pattern=[[1, P]], channel_multiplier=-1).then_inc(ready, 1)
            nc.gpsimd.affine_select(out=neg_suf[:], in_=neg_suf[:], compare_op=ALU.is_gt, fill=0.0, base=0,
                                    pattern=[[-1, P]], channel_multiplier=1).then_inc(ready, 1)
            nc.gpsimd.affine_select(out=causal4[:], in_=causal4[:], compare_op=ALU.is_ge, fill=0.0, base=0,
                                    pattern=[[0, 4], [1, P]], channel_multiplier=-1).then_inc(ready, 1)
            pool.wait_ge(ready, 4)
            nc.gpsimd.tensor_copy(neg_mid0[:], neg_tri[:]).then_inc(made, 1)
            nc.gpsimd.tensor_copy(neg_mid1[:, H:P], neg_tri[:, H:P]).then_inc(made, 1)
            pool.wait_ge(made, len(fills) + 2)
            nc.gpsimd.tensor_scalar(neg_mid0[0:32, :], neg_tri[0:32, :], 1.0, None, ALU.add).then_inc(made, 1)
            for p0, p1 in ((0, 32), (32, 64), (64, 96)):
                nc.gpsimd.tensor_scalar(neg_mid1[p0:p1, H:P], neg_tri[p0:p1, H:P], 1.0, None, ALU.add).then_inc(made, 1)
            pool.wait_ge(made, len(fills) + 6)
            nc.gpsimd.tensor_copy(neg_own[:, 0:H], neg_mid0[:, 0:H]).then_inc(ready, 1)
            nc.gpsimd.tensor_copy(neg_own[:, H:P], neg_mid1[:, H:P]).then_inc(ready, 1)
            pool.wait_ge(ready, 6)
    return c


def ssm_project(nc, sb, pb, sem, c, x_in, xi_dram, abc_dram, w_in_dram, w_abc_dram):
    ident, mhalf = c["ident"], c["mhalf"]
    w_in = sb("w_in", [P, KD, 2 * DI])
    w_abc = sb("w_abc", [P, KI, 3 * NS])
    x_t = sb("x_t", [P, 2, DM])
    stats = sb("stats", [P, 2, 6])
    mean_var = sb("mean_var", [P, 2, 2])
    var_eps = sb("var_eps", [P, 2])
    rstd = sb("rstd", [P, 2])
    xn = sb("xn", [P, 2, DM])
    xnt = sb("xnt", [P, 2, KD, P])
    sig = sb("sig", [P, 2, 2 * DI])
    gated = sb("gated", [P, 2, DI])
    xi = sb("xi", [P, 2, DI])
    xit = sb("xit", [P, 2, KI, P])
    abc = sb("abc", [P, 2, 3 * NS])
    ps_xnt = [pb(f"ps_xnt{s}", [P, KD, P]) for s in range(2)]
    ps_xz = [pb(f"ps_xz{s}", [P, 2 * DI]) for s in range(2)]
    ps_xit = pb("ps_xit", [P, KI, P])
    ps_abc = pb("ps_abc", [P, 3 * NS])

    w_loaded = sem("a_w_loaded")
    x_loaded = [sem(f"a_x_loaded{s}") for s in range(2)]
    ln_steps, var_ready, rstd_ready, xn_ready = (sem("a_" + n) for n in ("ln_steps", "var_ready", "rstd_ready", "xn_ready"))
    xnt_done, xnt_ready, xz_done, sig_ready = (sem("a_" + n) for n in ("xnt_done", "xnt_ready", "xz_done", "sig_ready"))
    gated_ready, xi_ready, xit_done, xit_ready = (sem("a_" + n) for n in ("gated_ready", "xi_ready", "xit_done", "xit_ready"))
    abc_done, abc_ready = sem("a_abc_done"), sem("a_abc_ready")
    stored = [sem(f"a_stored{s}") for s in range(2)]

    with nc.Block() as block:
        @block.sync
        def _(sp):
            sp.dma_start(w_in[:], w_in_dram.rearrange("(k p) n -> p k n", p=P)).then_inc(w_loaded, 16)
            sp.dma_start(w_abc[:], w_abc_dram.rearrange("(k p) n -> p k n", p=P)).then_inc(w_loaded, 16)

            def load(t, k, s):
                wait(sp, xn_ready, t - 1)
                sp.dma_start(x_t[:, s, :], x_in[bass.ts(t, P), :]).then_inc(x_loaded[s], 16)

            pipeline(sp, NT, [load])

        @block.vector
        def _(dve):
            chain = Chain(dve, ln_steps, 2)

            def norm(t, k, s):
                dve.wait_ge(x_loaded[s], 16 * k + 16)
                chain.at(t)
                chain.step(nc.vector.bn_stats(stats[:, s, :], x_t[:, s, :]))
                wait_apart(dve, c["ready"], (ln_steps, chain.base + chain.k))
                chain.link(nc.vector.bn_aggr(mean_var[:, s, :], stats[:, s, :]))
                nc.vector.tensor_scalar(var_eps[:, s:s + 1], mean_var[:, s, 1:2], LN_EPS, None,
                                        ALU.add).then_inc(var_ready, 1)
                dve.wait_ge(rstd_ready, t + 1)
                wait(dve, xnt_done, t - 1)
                nc.vector.tensor_scalar(xn[:, s, :], x_t[:, s, :], mean_var[:, s, 0:1], rstd[:, s:s + 1],
                                        ALU.subtract, ALU.mult).then_inc(xn_ready, 1)

            def gate(t, k, s):
                dve.wait_ge(sig_ready, t + 1)
                wait(dve, xi_ready, t - 1)
                nc.vector.tensor_tensor(gated[:, s, :], ps_xz[s][:, 0:DI], sig[:, s, 0:DI],
                                        ALU.mult).then_inc(gated_ready, 1)

            pipeline(dve, NT, [norm, gate])

        @block.gpsimd
        def _(pool):
            def rsqrt(t, k, s):
                pool.wait_ge(var_ready, t + 1)
                nc.gpsimd.tensor_tensor(rstd[:, s:s + 1], var_eps[:, s:s + 1], mhalf[:, 0:1],
                                        ALU.pow).then_inc(rstd_ready, 1)

            def gate(t, k, s):
                pool.wait_ge(gated_ready, t + 1)
                wait(pool, xit_done, t - 1)
                wait(pool, stored[s], 32 * k)
                nc.gpsimd.tensor_tensor(xi[:, s, :], gated[:, s, :], sig[:, s, DI:2 * DI],
                                        ALU.mult).then_inc(xi_ready, 1)

            pipeline(pool, NT, [rsqrt, gate])

        @block.tensor
        def _(pe):
            pe.wait_ge(w_loaded, 32)

            def project(t, k, s):
                pe.wait_ge(xn_ready, t + 1)
                wait(pe, xnt_ready, t - 1)
                for j in range(KD):
                    last = nc.tensor.transpose(ps_xnt[s][:, j, :], xn[:, s, j * P:(j + 1) * P], ident[:])
                last.then_inc(xnt_done, 1)
                pe.wait_ge(xnt_ready, t + 1)
                wait(pe, gated_ready, t - 1)
                for h in range(2):
                    for j in range(KD):
                        last = nc.tensor.matmul(ps_xz[s][:, h * DI:(h + 1) * DI], xnt[:, s, j, :],
                                                w_in[:, j, h * DI:(h + 1) * DI], start=(j == 0), stop=(j == KD - 1))
                last.then_inc(xz_done, 1)

            def states(t, k, s):
                pe.wait_ge(xi_ready, t + 1)
                wait(pe, xit_ready, t)
                for j in range(KI):
                    last = nc.tensor.transpose(ps_xit[:, j, :], xi[:, s, j * P:(j + 1) * P], ident[:])
                last.then_inc(xit_done, 1)
                pe.wait_ge(xit_ready, t + 1)
                wait(pe, abc_ready, t)
                for j in range(KI):
                    last = nc.tensor.matmul(ps_abc[:], xit[:, s, j, :], w_abc[:, j, :], start=(j == 0), stop=(j == KI - 1))
                last.then_inc(abc_done, 1)

            pipeline(pe, NT, [project, states])

        @block.scalar
        def _(act):
            def project(t, k, s):
                act.wait_ge(xnt_done, t + 1)
                wait(act, xz_done, t - 1)
                nc.scalar.activation(xnt[:, s], ps_xnt[s][:], ACT.Copy).then_inc(xnt_ready, 1)

            def gate(t, k, s):
                act.wait_ge(xz_done, t + 1)
                wait(act, xi_ready, t - 1)
                nc.scalar.activation(sig[:, s, :], ps_xz[s][:], ACT.Sigmoid).then_inc(sig_ready, 1)
                act.wait_ge(xit_done, t + 1)
                wait(act, abc_done, t - 1)
                nc.scalar.activation(xit[:, s], ps_xit[:], ACT.Copy).then_inc(xit_ready, 1)
                act.wait_ge(abc_done, t + 1)
                wait(act, stored[s], 32 * k)
                nc.scalar.activation(abc[:, s, :], ps_abc[:], ACT.Copy).then_inc(abc_ready, 1)
                act.dma_start(xi_dram[bass.ts(t, P), :], xi[:, s, :]).then_inc(stored[s], 16)
                act.wait_ge(abc_ready, t + 1)
                act.dma_start(abc_dram[bass.ts(t, P), :], abc[:, s, :]).then_inc(stored[s], 16)

            pipeline(act, NT, [project, gate])
            for s in range(2):
                act.wait_ge(stored[s], 32 * (NT // 2))


def ssm_scan(nc, sb, pb, sem, c, x_in, xi_dram, abc_dram, w_out_dram, norm_w_dram, x1_dram):
    ident, mhalf, one, neg_one, causal4 = c["ident"], c["mhalf"], c["one"], c["neg_one"], c["causal4"]
    B4 = BATCH
    NP = P // B4
    xi = sb("b_xi", [P, 2, B4, DI])
    abc = sb("b_abc", [P, 2, B4, 3 * NS])
    x_t = sb("b_x", [P, 2, B4, DM])
    a_clip = sb("a_clip", [P, B4, NS])
    ea = sb("ea", [P, B4, NP])
    e_inv = sb("e_inv", [P, B4, NS])
    e_all = sb("e_all", [P, 4, B4, NS])
    decay = sb("decay", [P, 2])
    bx = sb("bx", [P, B4, NP])
    diag = {n: sb("diag_" + n, [P, B4 * (P + NP)]) for n in ("c0", "c1", "p")}
    bxt = sb("bxt", [P, P])
    c0t = sb("c0t", [P, B4, P])
    c1t = sb("c1t", [P, B4, H])
    cpt = sb("cpt", [P, 2, B4, P])
    bsm = sb("bsm", [P, 2, B4 * (P + NP)])
    scores = sb("scores", [P, 2, B4, P])
    state = sb("state", [P, DI])
    ys = sb("ys", [P, 2, KI, P])
    sq = sb("sq", [P, 2, KI, P])
    ms = sb("ms", [P, 2])
    rms = sb("rms", [P, 2])
    x1 = sb("x1", [P, 2, B4, DM])
    w_out = sb("w_out", [P, KI, DM])
    norm_w = sb("norm_w", [P, KI])
    ps_cum = pb("ps_cum", [P, 5 * B4 * NS + 1])
    ps_s = pb("ps_s", [P, B4, P])
    ps_tr = pb("ps_tr", [P, B4, P])
    ps_y = [pb(f"ps_y{i}", [P, KI, P]) for i in range(2)]
    ps_o = [pb(f"ps_o{i}", [P, DM + 1]) for i in range(2)]
    ps_st = pb("ps_st", [P, DI])

    w_loaded, w_steps, zeroed = sem("b_w_loaded"), sem("b_w_steps"), sem("b_zeroed")
    loaded = [sem(f"b_loaded{s}") for s in range(2)]
    (clipped, ea_ready, cum_done, exps_ready, bx_ready, bxt_done, bxt_ready, c0t_done, c0t_ready, c1t_done, c1t_ready, cpt_done,
     cpt_ready, s_done, scores_ready, y_done, ys_ready, sq_ready, o_done, ms_ready, rms_ready, x1_ready,
     st_done, state_ready) = (sem("b_" + n) for n in (
        "clipped", "ea_ready", "cum_done", "exps_ready", "bx_ready", "bxt_done", "bxt_ready", "c0t_done",
        "c0t_ready", "c1t_done", "c1t_ready", "cpt_done", "cpt_ready", "s_done", "scores_ready", "y_done", "ys_ready", "sq_ready",
        "o_done", "ms_ready", "rms_ready", "x1_ready", "st_done", "state_ready"))
    stored = [sem(f"b_stored{s}") for s in range(2)]
    S4 = B4 * NS
    W = P + NP

    def own(tile):
        return tile.rearrange("p (b w) -> p b w", w=W)[:, :, 0:NS]

    def masked(tile, b):
        return tile[:, b * P:(b + 1) * P]

    with nc.Block() as block:
        @block.sync
        def _(sp):
            sp.dma_start(w_out[:], w_out_dram.rearrange("(k p) n -> p k n", p=P)).then_inc(w_loaded, 16)
            sp.dma_start(norm_w[:], norm_w_dram).then_inc(w_loaded, 16)

            def chunk(dram, ch):
                return dram.rearrange("(b t) n -> t b n", b=B4)[bass.ts(ch, P)]

            def load(ch, k, s):
                wait_apart(sp, c["ready"], (st_done, ch - 1), (x1_ready, B4 * (ch - 1)))
                sp.dma_start(xi[:, s], chunk(xi_dram, ch)).then_inc(loaded[s], 16)
                sp.dma_start(abc[:, s], chunk(abc_dram, ch)).then_inc(loaded[s], 16)
                sp.dma_start(x_t[:, s], chunk(x_in, ch)).then_inc(loaded[s], 16)

            def store(ch, k, s):
                wait_apart(sp, c["ready"], (x1_ready, B4 * (ch + 1)))
                sp.dma_start(chunk(x1_dram, ch), x1[:, s]).then_inc(stored[s], 16)

            pipeline(sp, TPB, [load, lambda *a: None, store])
            for s in range(2):
                sp.wait_ge(stored[s], 16 * (TPB // 2))

        @block.gpsimd
        def _(pool):
            nc.gpsimd.memset(ea[:], 0.0).then_inc(zeroed, 1)
            nc.gpsimd.memset(bx[:], 0.0).then_inc(zeroed, 1)
            nc.gpsimd.memset(diag["c0"][:], 0.0).then_inc(zeroed, 1)
            nc.gpsimd.memset(diag["c1"][:], 0.0).then_inc(zeroed, 1)
            nc.gpsimd.memset(diag["p"][:], 0.0).then_inc(zeroed, 1)
            nc.gpsimd.memset(bsm[:], 0.0).then_inc(zeroed, 1)
            nc.gpsimd.memset(scores[:], 0.0).then_inc(zeroed, 1)
            nc.gpsimd.memset(state[:], 0.0).then_inc(zeroed, 1)

            def rsqrt(ch, k, s):
                for b in range(B4):
                    pool.wait_ge(ms_ready, B4 * ch + b + 1)
                    nc.gpsimd.tensor_tensor(rms[:, b % 2:b % 2 + 1], ms[:, b % 2:b % 2 + 1], mhalf[:, 0:1],
                                            ALU.pow).then_inc(rms_ready, 1)

            pipeline(pool, TPB, [lambda *a: None, rsqrt])

        @block.vector
        def _(dve):
            dve.wait_ge(zeroed, 8)
            dve.wait_ge(w_loaded, 32)
            for j in range(KI):
                nc.vector.tensor_scalar(w_out[:, j, :], w_out[:, j, :], norm_w[:, j:j + 1], None,
                                        ALU.mult).then_inc(w_steps, 1)

            def prepare(ch, k, s):
                dve.wait_ge(loaded[s], 48 * k + 48)
                wait(dve, ea_ready, ch)
                nc.vector.tensor_scalar(a_clip[:], abc[:, s, :, 0:NS], -5.0, 0.0, ALU.max,
                                        ALU.min).then_inc(clipped, 1)
                dve.wait_ge(exps_ready, 3 * ch + 2)
                b_part, c_part = abc[:, s, :, NS:2 * NS], abc[:, s, :, 2 * NS:3 * NS]

                wait(dve, bxt_done, ch)
                nc.vector.tensor_tensor(bx[:, :, 0:NS], b_part, e_inv[:], ALU.mult).then_inc(bx_ready, 1)
                wait(dve, cpt_done, ch)
                for i, n in ((0, "c0"), (1, "c1"), (3, "p")):
                    nc.vector.tensor_tensor(own(diag[n][:]), c_part, e_all[:, i], ALU.mult).then_inc(bx_ready, 1)
                wait(dve, st_done, ch - 1)
                nc.vector.tensor_tensor(own(bsm[:, s, :]), b_part, e_all[:, 2], ALU.mult).then_inc(bx_ready, 1)
                wait_apart(dve, c["ready"], (s_done, ch + 1))
                nc.vector.copy_predicated(scores[0:H, s], causal4[0:H].bitcast(U32), ps_s[0:H]).then_inc(scores_ready, 1)
                nc.vector.copy_predicated(scores[H:P, s, :, H:P], causal4[H:P, :, H:P].bitcast(U32),
                                          ps_s[H:P, :, H:P]).then_inc(scores_ready, 1)
                dve.wait_ge(cpt_done, ch + 1)
                wait(dve, st_done, ch - 1)
                nc.vector.tensor_copy(cpt[:, s], ps_tr[:]).then_inc(cpt_ready, 1)

            def outputs(ch, k, s):
                def take(b):
                    n = B4 * ch + b
                    dve.wait_ge(y_done, n + 1)
                    wait(dve, o_done, n - 1)
                    nc.vector.tensor_copy(ys[:, b % 2], ps_y[b % 2][:]).then_inc(ys_ready, 1)

                def finish(b):
                    n = B4 * ch + b
                    i = b % 2
                    dve.wait_ge(o_done, n + 1)
                    wait(dve, rms_ready, n - 1)
                    nc.vector.tensor_scalar(ms[:, i:i + 1], ps_o[i][:, DM:DM + 1], 1.0 / DI, RMS_EPS, ALU.mult,
                                            ALU.add).then_inc(ms_ready, 1)
                    dve.wait_ge(rms_ready, n + 1)
                    wait(dve, stored[s], 16 * k)
                    nc.vector.scalar_tensor_tensor(out=x1[:, s, b, :], in0=ps_o[i][:, 0:DM], scalar=rms[:, i:i + 1],
                                                   in1=x_t[:, s, b, :], op0=ALU.mult, op1=ALU.add).then_inc(x1_ready, 1)

                take(0)
                take(1)
                finish(0)
                take(2)
                finish(1)
                take(3)
                dve.wait_ge(st_done, ch + 1)
                nc.vector.scalar_tensor_tensor(out=state[:], in0=state[:], scalar=decay[:, s:s + 1], in1=ps_st[:],
                                               op0=ALU.mult, op1=ALU.add).then_inc(state_ready, 1)
                finish(2)
                finish(3)

            pipeline(dve, TPB, [prepare, outputs])

        @block.scalar
        def _(act):
            act.wait_ge(zeroed, 2)

            def prepare(ch, k, s):
                act.wait_ge(clipped, ch + 1)
                wait(act, cum_done, ch)
                nc.scalar.activation(ea[:, :, 0:NS], a_clip[:], ACT.Exp).then_inc(ea_ready, 1)
                act.wait_ge(cum_done, ch + 1)
                wait(act, bx_ready, 5 * ch)
                wait(act, state_ready, ch - 1)
                nc.scalar.activation(e_inv[:].rearrange("p b n -> p (b n)"), ps_cum[:, 0:S4], ACT.Exp,
                                     scale=-1.0).then_inc(exps_ready, 1)
                nc.scalar.activation(e_all[:].rearrange("p i b n -> p (i b n)"), ps_cum[:, S4:5 * S4],
                                     ACT.Exp).then_inc(exps_ready, 1)
                nc.scalar.activation(decay[:, s:s + 1], ps_cum[:, 5 * S4:5 * S4 + 1], ACT.Exp).then_inc(exps_ready, 1)
                act.wait_ge(bxt_done, ch + 1)
                wait(act, s_done, ch)
                nc.scalar.activation(bxt[:], ps_s[:, 0, :], ACT.Copy).then_inc(bxt_ready, 1)
                act.wait_ge(c0t_done, ch + 1)
                nc.scalar.activation(c0t[:], ps_tr[:], ACT.Copy).then_inc(c0t_ready, 1)
                act.wait_ge(c1t_done, ch + 1)
                nc.scalar.activation(c1t[:], ps_tr[:, :, H:P], ACT.Copy).then_inc(c1t_ready, 1)

            def outputs(ch, k, s):
                for b in range(B4):
                    n = B4 * ch + b
                    act.wait_ge(ys_ready, n + 1)
                    wait(act, o_done, n - 1)
                    nc.scalar.activation(sq[:, b % 2], ys[:, b % 2], ACT.Square).then_inc(sq_ready, 1)

            pipeline(act, TPB, [prepare, outputs])

        @block.tensor
        def _(pe):
            pe.wait_ge(w_steps, KI)
            pe.wait_ge(zeroed, 8)

            def prepare(ch, k, s):
                pe.wait_ge(ea_ready, ch + 1)
                wait(pe, exps_ready, 3 * ch)
                for i, m in enumerate(("neg_own", "neg_mid0", "neg_mid1", "neg_suf", "neg_tri")):
                    nc.tensor.matmul(ps_cum[:, i * S4:(i + 1) * S4], c[m][:], ea[:, :, 0:NS], start=True, stop=True)
                nc.tensor.matmul(ps_cum[:, 5 * S4:5 * S4 + 1], ea[:].rearrange("p b n -> p (b n)"), neg_one[:],
                                 start=True, stop=True).then_inc(cum_done, 1)
                pe.wait_ge(bx_ready, 5 * ch + 1)
                wait(pe, scores_ready, 2 * ch)
                nc.tensor.transpose(ps_s[:, 0, :], bx[:].rearrange("p b n -> p (b n)"), ident[:]).then_inc(bxt_done, 1)
                pe.wait_ge(bx_ready, 5 * ch + 4)
                wait(pe, cpt_ready, ch)
                for b in range(B4):
                    last = nc.tensor.transpose(ps_tr[:, b, :], masked(diag["c0"], b), ident[:])
                last.then_inc(c0t_done, 1)
                pe.wait_ge(c0t_ready, ch + 1)
                for b in range(B4):
                    last = nc.tensor.transpose(ps_tr[:, b, :], masked(diag["c1"], b), ident[:])
                last.then_inc(c1t_done, 1)
                pe.wait_ge(bxt_ready, ch + 1)
                nc.tensor.matmul(ps_s[0:H], bxt[:, 0:H], c0t[:], start=True, stop=True)
                pe.wait_ge(c1t_ready, ch + 1)
                nc.tensor.matmul(ps_s[H:P, :, H:P], bxt[:, H:P], c1t[:], start=True, stop=True).then_inc(s_done, 1)
                for b in range(B4):
                    last = nc.tensor.transpose(ps_tr[:, b, :], masked(diag["p"], b), ident[:])
                last.then_inc(cpt_done, 1)

            def outputs(ch, k, s):
                def scan(b):
                    wait(pe, ys_ready, B4 * ch + b - 1)
                    for j in range(KI):
                        d = slice(j * P, (j + 1) * P)
                        nc.tensor.matmul(ps_y[b % 2][:, j, :], xi[:, s, b, d], scores[:, s, b, :], start=True, stop=False)
                        last = nc.tensor.matmul(ps_y[b % 2][:, j, :], state[:, d], cpt[:, s, b, :], start=False, stop=True)
                    last.then_inc(y_done, 1)

                def project(b):
                    i = b % 2
                    pe.wait_ge(sq_ready, B4 * ch + b + 1)
                    wait(pe, x1_ready, B4 * ch + b - 1)
                    for j in range(KI):
                        nc.tensor.matmul(ps_o[i][:, 0:DM], ys[:, i, j, :], w_out[:, j, :], start=(j == 0), stop=(j == KI - 1))
                    for j in range(KI):
                        last = nc.tensor.matmul(ps_o[i][:, DM:DM + 1], sq[:, i, j, :], one[:], start=(j == 0), stop=(j == KI - 1))
                    last.then_inc(o_done, 1)

                pe.wait_ge(scores_ready, 2 * ch + 2)
                pe.wait_ge(cpt_ready, ch + 1)
                wait(pe, state_ready, ch)
                scan(0)
                scan(1)
                project(0)
                scan(2)
                project(1)
                scan(3)
                for b in range(B4):
                    last = nc.tensor.matmul(ps_st[:], masked(bsm[:, s, :], b), xi[:, s, b, :], start=(b == 0), stop=(b == B4 - 1))
                last.then_inc(st_done, 1)
                project(2)
                project(3)

            pipeline(pe, TPB, [prepare, outputs])


CAP = TOK + P


G = 4
NG = NT // G


def route(nc, sb, pb, sem, c, name, E, x_dram, xn_dram, gathered, w_gate_dram, gate_b_dram, kept, attn=None):
    ident, mhalf, ones_row = c["ident"], c["mhalf"], c["ones_row"]
    pos_all, prob_all, tile_list = kept["pos"], kept["prob"], kept["tiles"]
    n_list = 2 * NT + E
    biased = gate_b_dram is not None
    w_gate = sb(name + "w_gate", [P, KD, E])
    gate_b = sb(name + "gate_b", [1, E])
    x_t = sb(name + "x_t", [P, 2, G, DM])
    stats = sb(name + "stats", [P, G, 6])
    mean_var = sb(name + "mean_var", [P, G, 2])
    var_eps = sb(name + "var_eps", [P, G])
    rstd = sb(name + "rstd", [P, G])
    xn = sb(name + "xn", [P, 2, G, DM])
    xs = sb(name + "xs", [P, 2, G, DM])
    xnt = sb(name + "xnt", [P, KD, G * P])
    top = sb(name + "top", [P, G])
    shifted = sb(name + "shifted", [P, G, E])
    expd = sb(name + "expd", [P, G, E])
    total = sb(name + "total", [P, G])
    inv = sb(name + "inv", [P, G])
    probs = sb(name + "probs", [P, G, E])
    best = sb(name + "best", [P, G, 8])
    best_at = sb(name + "best_at", [P, G, 8], U32)
    best_f = sb(name + "best_f", [P, G, 2])
    hot = sb(name + "hot", [P, 2, G, 2, E])
    both = sb(name + "both", [P, 2, G, E])
    free_row = sb(name + "free_row", [P, E])
    row = sb(name + "row", [P, G, E])
    hot_row = sb(name + "hot_row", [P, G, 2, E])
    pos_f = sb(name + "pos_f", [P, G, 2])
    pos = sb(name + "pos", [P, 2, G, 2], U32)
    experts = sb(name + "experts", [P, E])
    zeros = sb(name + "zeros", [P, DM])
    before = sb(name + "before", [P, P])
    all_ones = sb(name + "all_ones", [P, P])
    region = sb(name + "region", [P, E])
    count = sb(name + "count", [P, E])
    count_i = sb(name + "count_i", [P, E], U32)
    n_tiles = sb(name + "n_tiles", [P, E])
    one_e = sb(name + "one_e", [P, E])
    end = sb(name + "end", [P, E])
    moved = sb(name + "moved", [P, E])
    best_all = sb(name + "best_all", [P, NT, 2])
    pos_f_all = sb(name + "pos_f_all", [P, NT, 2])
    hot_all = sb(name + "hot_all", [P, 2 * NT, E])
    shift = sb(name + "shift", [P, NT, 2])
    index = sb(name + "index", [1, n_list])
    passed = sb(name + "passed", [1, n_list, E])
    passed_n = sb(name + "passed_n", [1, n_list, E])
    which = sb(name + "which", [1, n_list])
    start = sb(name + "start", [1, n_list])
    first_row = sb(name + "first_row", [1, n_list])
    pad_row = sb(name + "pad_row", [1, E], U32)
    if attn:
        headst_dram, inv_dram, wo_dram, res_dram, sum_dram = attn
        w_o = sb(name + "w_o", [P, KD, DM])
        headst = sb(name + "headst", [P, 2, KD, G * P])
        inv_t = sb(name + "inv_t", [P, 2, KD, G * P])
        scaled = sb(name + "scaled", [P, 2, KD, G * P])
        res = sb(name + "res", [P, 2, G, DM])
        ps_wo = pb(name + "ps_wo", [P, G, DM])
    ps_xnt = pb(name + "ps_xnt", [P, KD, G * P])
    ps_logits = pb(name + "ps_logits", [P, G, E])
    ps_rank = pb(name + "ps_rank", [P, G + 1, E])

    w_loaded, set_up = sem(name + "w_loaded"), sem(name + "set_up")
    x_loaded = [sem(f"{name}x_loaded{s}") for s in range(2)]
    (scaled_ready, wo_done, x_ready, ln_steps, var_ready, rstd_ready, xn_ready, xnt_done, xnt_ready,
     logits_done, shifted_ready, exp_ready, top_steps, both_ready, rank_done, row_ready, place_steps, pos_ready,
     kept_ready, xs_ready, list_steps, list_ready) = (sem(name + n) for n in (
        "scaled_ready", "wo_done", "x_ready", "ln_steps", "var_ready", "rstd_ready", "xn_ready",
        "xnt_done", "xnt_ready", "logits_done", "shifted_ready", "exp_ready", "top_steps", "both_ready", "rank_done",
        "row_ready", "place_steps", "pos_ready", "kept_ready", "xs_ready", "list_steps", "list_ready"))
    x_stored = [sem(f"{name}x_stored{s}") for s in range(2)]
    xn_stored = [sem(f"{name}xn_stored{s}") for s in range(2)]
    scattered = c["moved"][name + "scattered"]
    padded = sem(name + "padded")

    def rows(dram, g):
        return dram[bass.ts(g, G * P), :].rearrange("(j p) n -> p j n", p=P)

    def nothing(g, k, s):
        pass

    with nc.Block() as block:
        @block.sync
        def _(sp):
            sp.dma_start(w_gate[:], w_gate_dram.rearrange("(k p) n -> p k n", p=P)).then_inc(w_loaded, 16)
            if biased:
                sp.dma_start(gate_b[:], gate_b_dram).then_inc(w_loaded, 16)
            if attn:
                sp.dma_start(w_o[:], wo_dram.rearrange("(k p) n -> p k n", p=P)).then_inc(w_loaded, 16)

            def load(g, k, s):
                wait_apart(sp, c["ready"], (xn_ready, g - 1))
                if attn:
                    for kd in range(KD):
                        sp.dma_start(inv_t[:, s, kd, :], inv_dram[kd * (P // HD):(kd + 1) * (P // HD), bass.ts(g, G * P)]
                                     .unsqueeze(1).broadcast_to([P // HD, HD, G * P])).then_inc(x_loaded[s], 16)
                    sp.dma_start(headst[:, s], headst_dram[:, bass.ts(g, G * P)].rearrange("(k p) t -> p k t", p=P)).then_inc(x_loaded[s], 16)
                    sp.dma_start(res[:, s], rows(res_dram, g)).then_inc(x_loaded[s], 16)
                else:
                    sp.dma_start(x_t[:, s], rows(x_dram, g)).then_inc(x_loaded[s], 16)

            def store(g, k, s):
                if attn:
                    wait_apart(sp, c["ready"], (x_ready, g + 1), (xn_ready, g + 1))
                    sp.dma_start(rows(sum_dram, g), x_t[:, s]).then_inc(x_stored[s], 16)
                    sp.dma_start(rows(xn_dram, g), xn[:, s]).then_inc(xn_stored[s], 16)

            pipeline(sp, NG, [load, store])
            if attn:
                for s in range(2):
                    sp.wait_ge(x_stored[s], 16 * (NG // 2))
                    sp.wait_ge(xn_stored[s], 16 * (NG // 2))
            sp.wait_ge(set_up, 9)
            for e in range(E):
                sp.dma_start(gathered[E * CAP + e * P:E * CAP + (e + 1) * P, :], zeros[:]).then_inc(padded, 16)
            sp.wait_ge(list_ready, 1)
            for e in range(E):
                at = sp.value_load(pad_row[0:1, e:e + 1], min_val=e * CAP, max_val=e * CAP + TOK)
                sp.dma_start(gathered[bass.ds(at, P), :], zeros[:]).then_inc(padded, 16)
            sp.wait_ge(padded, 32 * E)

        @block.gpsimd
        def _(pool):
            for tile, value in ((zeros, 0.0), (one_e, 1.0), (before, 1.0), (all_ones, 1.0)):
                nc.gpsimd.memset(tile[:], value).then_inc(set_up, 1)
            for tile, step, n in ((experts, 1, E), (free_row, CAP, E), (region, CAP, E), (index, 1, n_list)):
                nc.gpsimd.iota(tile[:], pattern=[[step, n]], base=0, channel_multiplier=0,
                               allow_small_or_imprecise_dtypes=True).then_inc(set_up, 1)
            pool.wait_ge(set_up, 8)
            nc.gpsimd.affine_select(out=before[:], in_=before[:], compare_op=ALU.is_gt, fill=0.0, base=0,
                                    pattern=[[1, P]], channel_multiplier=-1).then_inc(set_up, 1)

            def scale(g, k, s):
                if attn:
                    wait_apart(pool, c["ready"], (x_loaded[s], 64 * k + 64), (wo_done, g - 1))
                    nc.gpsimd.tensor_tensor(scaled[:, s], headst[:, s], inv_t[:, s], ALU.mult).then_inc(scaled_ready, 1)

            def rsqrt(g, k, s):
                pool.wait_ge(var_ready, g + 1)
                nc.gpsimd.tensor_tensor(rstd[:], var_eps[:], mhalf[:], ALU.pow).then_inc(rstd_ready, 1)

            def scatter(g, k, s):
                wait_apart(pool, c["ready"], (pos_ready, g + 1), (xs_ready, g + 1))
                for j in range(G):
                    for i in range(2):
                        nc.gpsimd.indirect_dma_start(
                            out=gathered[:, :], out_offset=bass.IndirectOffsetOnAxis(ap=pos[:, s, j, i:i + 1], axis=0),
                            in_=xs[:, s, j, :], in_offset=None).then_inc(scattered[s], 16)

            pipeline(pool, NG, [scale, rsqrt, nothing, scatter])
            for s in range(2):
                pool.wait_ge(scattered[s], 32 * G * (NG // 2))

        @block.vector
        def _(dve):
            norm_chain = Chain(dve, ln_steps, 2 * G)
            top_chain = Chain(dve, top_steps, 4 * G + 5)
            place_chain = Chain(dve, place_steps, 2)

            def add(g, k, s):
                if attn:
                    dve.wait_ge(wo_done, g + 1)
                    dve.wait_ge(x_loaded[s], 64 * k + 64)
                    wait(dve, x_stored[s], 16 * k)
                    nc.vector.tensor_tensor(x_t[:, s], res[:, s], ps_wo[:], ALU.add).then_inc(x_ready, 1)

            def norm(g, k, s):
                if attn:
                    dve.wait_ge(x_ready, g + 1)
                else:
                    dve.wait_ge(x_loaded[s], 16 * k + 16)
                norm_chain.at(g)
                for j in range(G):
                    norm_chain.step(nc.vector.bn_stats(stats[:, j, :], x_t[:, s, j, :]))
                wait_apart(dve, c["ready"], (ln_steps, norm_chain.base + norm_chain.k))
                for j in range(G):
                    norm_chain.step(nc.vector.bn_aggr(mean_var[:, j, :], stats[:, j, :]))
                norm_chain.wait()
                nc.vector.tensor_scalar(var_eps[:], mean_var[:, :, 1], LN_EPS, None, ALU.add).then_inc(var_ready, 1)
                dve.wait_ge(rstd_ready, g + 1)
                wait(dve, xs_ready, g - 1)
                if xn_dram is not None:
                    wait(dve, xn_stored[s], 16 * k)
                for j in range(G):
                    last = nc.vector.tensor_scalar(xn[:, s, j, :], x_t[:, s, j, :], mean_var[:, j, 0:1], rstd[:, j:j + 1],
                                                   ALU.subtract, ALU.mult)
                last.then_inc(xn_ready, 1)

            def choose(g, k, s):
                top_chain.at(g)
                dve.wait_ge(logits_done, g + 1)
                top_chain.link(nc.vector.reduce_max(top[:], ps_logits[:], AXX))
                nc.vector.tensor_tensor(shifted[:], ps_logits[:], top[:].unsqueeze(2).broadcast_to([P, G, E]),
                                        ALU.subtract).then_inc(shifted_ready, 1)
                dve.wait_ge(exp_ready, g + 1)
                top_chain.link(nc.vector.reduce_sum(total[:], expd[:], AXX))
                top_chain.link(nc.vector.reciprocal(inv[:], total[:]))
                top_chain.step(nc.vector.tensor_tensor(probs[:], expd[:], inv[:].unsqueeze(2).broadcast_to([P, G, E]), ALU.mult))
                wait_apart(dve, c["ready"], (top_steps, top_chain.base + top_chain.k))
                for j in range(G):
                    top_chain.step(nc.vector.max(best[:, j, :], probs[:, j, :]))
                wait_apart(dve, c["ready"], (top_steps, top_chain.base + top_chain.k))
                for j in range(G):
                    top_chain.step(nc.vector.max_index(best_at[:, j, :], best[:, j, :], probs[:, j, :]))
                top_chain.wait()
                top_chain.link(nc.vector.tensor_copy(best_f[:], best_at[:, :, 0:2]))
                nc.vector.tensor_copy(prob_all[:, bass.ts(g, G), :], best[:, :, 0:2]).then_inc(kept_ready, 1)
                nc.vector.tensor_copy(best_all[:, bass.ts(g, G), :], best_f[:]).then_inc(kept_ready, 1)
                for j in range(G):
                    for i in range(2):
                        top_chain.step(nc.vector.tensor_scalar(hot[:, s, j, i, :], experts[:], best_f[:, j, i:i + 1],
                                                               None, ALU.is_equal))
                top_chain.wait()
                nc.vector.tensor_tensor(both[:, s], hot[:, s, :, 0, :], hot[:, s, :, 1, :], ALU.add).then_inc(both_ready, 1)

            def place(g, k, s):
                place_chain.at(g)
                dve.wait_ge(rank_done, g + 1)
                wait(dve, row_ready, 2 * g)
                nc.vector.tensor_tensor(row[:], free_row[:].unsqueeze(1).broadcast_to([P, G, E]), ps_rank[:, 0:G, :],
                                        ALU.add).then_inc(row_ready, 1)
                dve.wait_ge(row_ready, 2 * g + 1)
                nc.vector.tensor_tensor(free_row[:], free_row[:], ps_rank[:, G, :], ALU.add).then_inc(row_ready, 1)
                place_chain.link(nc.vector.tensor_tensor(hot_row[:], hot[:, s], row[:].unsqueeze(2).broadcast_to([P, G, 2, E]), ALU.mult))
                place_chain.link(nc.vector.reduce_sum(pos_f[:], hot_row[:], AXX))
                wait(dve, scattered[s], 32 * G * k)
                nc.vector.tensor_copy(pos[:, s], pos_f[:]).then_inc(pos_ready, 1)
                nc.vector.tensor_copy(pos_f_all[:, bass.ts(g, G), :], pos_f[:]).then_inc(kept_ready, 1)

            dve.wait_ge(set_up, 9)
            pipeline(dve, NG, [add, norm, choose, place])

            chain = Chain(dve, list_steps, 19)
            chain.at(0)
            dve.wait_ge(row_ready, 2 * NG)
            dve.wait_ge(kept_ready, 3 * NG)
            nc.vector.tensor_copy(pad_row[:], free_row[0:1, :]).then_inc(list_ready, 1)
            chain.link(nc.vector.tensor_tensor(count[:], free_row[:], region[:], ALU.subtract))
            chain.link(nc.vector.tensor_scalar(count_i[:], count[:], float(P - 1), None, ALU.add))
            chain.link(nc.vector.tensor_scalar(count_i[:], count_i[:], P.bit_length() - 1, None, ALU.logical_shift_right))
            chain.link(nc.vector.tensor_copy(n_tiles[:], count_i[:]))
            chain.link(nc.vector.tensor_tensor_scan(end[:], one_e[:], n_tiles[:], 0.0, ALU.mult, ALU.add))
            chain.link(nc.vector.tensor_tensor(passed[:], index[:].unsqueeze(2).broadcast_to([1, n_list, E]),
                                               end[0:1].unsqueeze(1).broadcast_to([1, n_list, E]), ALU.is_ge))
            chain.link(nc.vector.reduce_sum(which[:], passed[:], AXX))
            chain.link(nc.vector.tensor_tensor(passed_n[:], passed[:], n_tiles[0:1].unsqueeze(1).broadcast_to([1, n_list, E]), ALU.mult))
            chain.link(nc.vector.reduce_sum(start[:], passed_n[:], AXX))
            chain.link(nc.vector.tensor_tensor(start[:], index[:], start[:], ALU.subtract))
            chain.link(nc.vector.tensor_scalar(start[:], start[:], float(P), None, ALU.mult))
            chain.link(nc.vector.scalar_tensor_tensor(out=first_row[:], in0=which[:], scalar=float(CAP), in1=start[:],
                                                      op0=ALU.mult, op1=ALU.add))
            nc.vector.tensor_scalar(tile_list[0:1, 0, :], which[:], float(E - 1), None, ALU.min).then_inc(list_ready, 1)
            nc.vector.tensor_copy(tile_list[0:1, 1, :], first_row[:]).then_inc(list_ready, 1)
            chain.link(nc.vector.tensor_tensor(moved[:], end[:], n_tiles[:], ALU.subtract))
            chain.link(nc.vector.tensor_scalar(moved[:], moved[:], float(P), None, ALU.mult))
            chain.link(nc.vector.tensor_tensor(moved[:], moved[:], region[:], ALU.subtract))
            chain.link(nc.vector.tensor_tensor(hot_all[:], experts[:].unsqueeze(1).broadcast_to([P, 2 * NT, E]),
                                               best_all[:].rearrange("p t i -> p (t i)").unsqueeze(2).broadcast_to([P, 2 * NT, E]),
                                               ALU.is_equal))
            chain.link(nc.vector.tensor_tensor(hot_all[:], hot_all[:], moved[:].unsqueeze(1).broadcast_to([P, 2 * NT, E]), ALU.mult))
            chain.link(nc.vector.reduce_sum(shift[:].rearrange("p t i -> p (t i)"), hot_all[:], AXX))
            chain.link(nc.vector.tensor_tensor(shift[:], shift[:], pos_f_all[:], ALU.add))
            nc.vector.tensor_copy(pos_all[:], shift[:]).then_inc(list_ready, 1)
            dve.wait_ge(list_ready, 4)

        @block.tensor
        def _(pe):
            pe.wait_ge(set_up, 9)
            pe.wait_ge(w_loaded, 16 * (1 + biased + (attn is not None)))

            def attend(g, k, s):
                if attn:
                    pe.wait_ge(scaled_ready, g + 1)
                    wait(pe, x_ready, g)
                    for j in range(G):
                        for kd in range(KD):
                            last = nc.tensor.matmul(ps_wo[:, j, :], scaled[:, s, kd, j * P:(j + 1) * P], w_o[:, kd, :],
                                                    start=(kd == 0), stop=(kd == KD - 1))
                    last.then_inc(wo_done, 1)

            def gate(g, k, s):
                pe.wait_ge(xn_ready, g + 1)
                wait(pe, xnt_ready, g)
                for kd in range(KD):
                    for j in range(G):
                        last = nc.tensor.transpose(ps_xnt[:, kd, j * P:(j + 1) * P], xn[:, s, j, kd * P:(kd + 1) * P], ident[:])
                last.then_inc(xnt_done, 1)
                pe.wait_ge(xnt_ready, g + 1)
                wait(pe, shifted_ready, g)
                for j in range(G):
                    for kd in range(KD):
                        last = nc.tensor.matmul(ps_logits[:, j, :], xnt[:, kd, j * P:(j + 1) * P], w_gate[:, kd, :],
                                                start=(kd == 0), stop=(kd == KD - 1 and not biased))
                    if biased:
                        last = nc.tensor.matmul(ps_logits[:, j, :], ones_row[:], gate_b[:], start=False, stop=True)
                last.then_inc(logits_done, 1)

            def rank(g, k, s):
                pe.wait_ge(both_ready, g + 1)
                wait(pe, row_ready, 2 * g)
                for j in range(G + 1):
                    for i in range(min(j + 1, G)):
                        last = nc.tensor.matmul(ps_rank[:, j, :], before[:] if i == j else all_ones[:], both[:, s, i, :],
                                                start=(i == 0), stop=(i == min(j, G - 1)))
                last.then_inc(rank_done, 1)

            pipeline(pe, NG, [attend, gate, rank])

        @block.scalar
        def _(act):
            def gate(g, k, s):
                act.wait_ge(xnt_done, g + 1)
                wait(act, logits_done, g)
                nc.scalar.activation(xnt[:], ps_xnt[:], ACT.Copy).then_inc(xnt_ready, 1)

            def soften(g, k, s):
                act.wait_ge(shifted_ready, g + 1)
                nc.scalar.activation(expd[:], shifted[:], ACT.Exp).then_inc(exp_ready, 1)
                wait(act, scattered[s], 32 * G * k)
                nc.scalar.activation(xs[:, s], xn[:, s], ACT.Copy).then_inc(xs_ready, 1)

            pipeline(act, NG, [nothing, gate, soften])


def run_experts(nc, sb, pb, sem, c, name, E, gathered, outputs, kept, up, down):
    ident = c["ident"]
    n_list = 2 * NT + E
    width, w_up, b_up = up
    blocks, w_down, b_down = down
    hidden = blocks * P
    relu = b_up is not None
    tiles = kept["tiles"]
    x_t = sb(name + "x_t", [P, 2, DM])
    xt = sb(name + "xt", [P, 2, KD, P])
    h = sb(name + "h", [P, 2, hidden])
    ht = sb(name + "ht", [P, 2, blocks, P])
    y = sb(name + "y", [P, 2, DM])
    if not relu:
        sig = sb(name + "sig", [P, 2, hidden])
        act_g = sb(name + "act_g", [P, 2, hidden])
    ps_x = pb(name + "ps_x", [P, KD, P])
    ps_h = [pb(f"{name}ps_h{s}", [P, width]) for s in range(2)]
    ps_ht = pb(name + "ps_ht", [P, blocks, P])
    ps_y = pb(name + "ps_y", [P, DM])
    x_loaded = [sem(f"{name}x_loaded{s}") for s in range(2)]
    stored = [sem(f"{name}stored{s}") for s in range(2)]
    xt_done, xt_ready, h_done, sig_ready, gated, h_ready, ht_done, ht_ready, y_done, y_ready = (sem(name + n) for n in (
        "xt_done", "xt_ready", "h_done", "sig_ready", "gated", "h_ready", "ht_done", "ht_ready", "y_done", "y_ready"))

    def nothing(t, k, s):
        pass

    def entry(eng, t, what, top):
        return eng.value_load(tiles[0:1, what, bass.ds(t, 1)], min_val=0, max_val=top)

    with nc.Block() as block:
        @block.sync
        def _(sp):
            def load(t, k, s):
                wait_apart(sp, c["ready"], (xt_done, t - 1))
                row = entry(sp, t, 1, E * CAP + (E - 1) * P)
                sp.dma_start(x_t[:, s, :], gathered[bass.ds(row, P), :]).then_inc(x_loaded[s], 16)

            pipeline(sp, n_list, [load])

        @block.tensor
        def _(pe):
            def transpose_x(t, k, s):
                pe.wait_ge(x_loaded[s], 16 * k + 16)
                wait(pe, xt_ready, t)
                for j in range(KD):
                    last = nc.tensor.transpose(ps_x[:, j, :], x_t[:, s, j * P:(j + 1) * P], ident[:])
                last.then_inc(xt_done, 1)

            def go_up(t, k, s):
                e = entry(pe, t, 0, E - 1)
                pe.wait_ge(xt_ready, t + 1)
                wait(pe, h_ready, t - 1)
                for j in range(KD):
                    last = nc.tensor.matmul(ps_h[s][:], xt[:, s, j, :], w_up[:, j, bass.ts(e, width)], start=(j == 0), stop=(j == KD - 1))
                last.then_inc(h_done, 1)

            def transpose_h(t, k, s):
                pe.wait_ge(h_ready, t + 1)
                wait(pe, ht_ready, t)
                for j in range(blocks):
                    last = nc.tensor.transpose(ps_ht[:, j, :], h[:, s, j * P:(j + 1) * P], ident[:])
                last.then_inc(ht_done, 1)

            def go_down(t, k, s):
                e = entry(pe, t, 0, E - 1)
                pe.wait_ge(ht_ready, t + 1)
                wait(pe, y_ready, t)
                for j in range(blocks):
                    last = nc.tensor.matmul(ps_y[:], ht[:, s, j, :], w_down[:, j, bass.ts(e, DM)], start=(j == 0), stop=(j == blocks - 1))
                last.then_inc(y_done, 1)

            pipeline(pe, n_list, [transpose_x, go_up, transpose_h, go_down])

        @block.vector
        def _(dve):
            def hide(t, k, s):
                if relu:
                    e = entry(dve, t, 0, E - 1)
                dve.wait_ge(h_done, t + 1)
                wait(dve, ht_done, t - 1)
                if relu:
                    nc.vector.tensor_tensor(h[:, s, :], ps_h[s][:], b_up[:, bass.ts(e, width)], ALU.add).then_inc(h_ready, 1)
                else:
                    dve.wait_ge(sig_ready, t + 1)
                    nc.vector.tensor_tensor(act_g[:, s, :], ps_h[s][:, 0:hidden], sig[:, s, :], ALU.mult).then_inc(gated, 1)
                    dve.wait_ge(gated, t + 1)
                    nc.vector.tensor_tensor(h[:, s, :], ps_h[s][:, hidden:2 * hidden], act_g[:, s, :], ALU.mult).then_inc(h_ready, 1)

            def finish(t, k, s):
                if b_down is not None:
                    e = entry(dve, t, 0, E - 1)
                dve.wait_ge(y_done, t + 1)
                wait(dve, stored[s], 16 * k)
                if b_down is not None:
                    nc.vector.tensor_tensor(y[:, s, :], ps_y[:], b_down[:, bass.ts(e, DM)], ALU.add).then_inc(y_ready, 1)
                else:
                    nc.vector.tensor_copy(y[:, s, :], ps_y[:]).then_inc(y_ready, 1)

            pipeline(dve, n_list, [nothing, hide, nothing, finish])

        @block.scalar
        def _(act):
            def copy_x(t, k, s):
                act.wait_ge(xt_done, t + 1)
                wait(act, h_done, t - 1)
                nc.scalar.activation(xt[:, s], ps_x[:], ACT.Copy).then_inc(xt_ready, 1)

            def sigmoid(t, k, s):
                if not relu:
                    act.wait_ge(h_done, t + 1)
                    wait(act, gated, t - 1)
                    nc.scalar.activation(sig[:, s, :], ps_h[s][:, 0:hidden], ACT.Sigmoid).then_inc(sig_ready, 1)

            def copy_h(t, k, s):
                act.wait_ge(ht_done, t + 1)
                wait(act, y_done, t - 1)
                nc.scalar.activation(ht[:, s], ps_ht[:], ACT.Relu if relu else ACT.Copy).then_inc(ht_ready, 1)

            def store(t, k, s):
                act.wait_ge(y_ready, t + 1)
                act.dma_start(outputs[bass.ts(t, P), :], y[:, s, :]).then_inc(stored[s], 16)

            pipeline(act, n_list, [copy_x, sigmoid, copy_h, nothing, store])
            for s in range(2):
                act.wait_ge(stored[s], 16 * (n_list // 2))


SLOTS = 4


def project_qkv(nc, sb, pb, sem, c, x_dram, outputs, kept, sum_dram, w_qkv_dram, rope_dram, qkt_dram, v_dram):
    ident, mhalf = c["ident"], c["mhalf"]
    QK = 2 * DM
    w = sb("w_qkv", [P, KD, 3 * DM])
    x_t = sb("d_x", [P, 2, DM])
    idx = sb("d_idx", [P, 2, 2], U32)
    prob = sb("d_prob", [P, 2, 2])
    ye = [sb(f"d_ye{i}", [P, 2, DM]) for i in range(2)]
    part = sb("d_part", [P, 2, DM])
    x2 = sb("d_x2", [P, 2, DM])
    rope = sb("d_rope", [P, 2, 2, HD])
    stats = sb("d_stats", [P, 2, 6])
    mean_var = sb("d_mean_var", [P, 2, 2])
    var_eps = sb("d_var_eps", [P, 2])
    rstd = sb("d_rstd", [P, 2])
    xn = sb("d_xn", [P, 2, DM])
    xnt = sb("d_xnt", [P, 2, KD, P])
    by_cos = sb("d_by_cos", [P, 2, QK])
    by_sin = sb("d_by_sin", [P, 2, QK])
    qk = sb("d_qk", [P, 2, QK])
    hi = sb("d_hi", [P, 2, QK], FP32R)
    lo = sb("d_lo", [P, 2, QK])
    qkt = sb("d_qkt", [P, 2, 8, P])
    v_t = sb("d_v", [P, 2, DM])
    ps_xnt = pb("d_ps_xnt", [P, KD, P])
    ps_qkv = [pb(f"d_ps_qkv{s}", [P, 3 * DM]) for s in range(2)]
    ps_t = [pb(f"d_ps_t{i}", [P, 4, P]) for i in range(2)]
    w_loaded = sem("d_w_loaded")
    x_loaded = [sem(f"d_x_loaded{s}") for s in range(2)]
    (idx_ready, x2_steps, x2_ready, ln_steps, var_ready, rstd_ready, xn_ready, xnt_done, xnt_ready, qkv_done, roped,
     qk_ready, hi_ready, lo_ready, hit_done, lot_done, qkt_ready, v_ready) = (sem("d_" + n) for n in (
        "idx_ready", "x2_steps", "x2_ready", "ln_steps", "var_ready", "rstd_ready", "xn_ready", "xnt_done", "xnt_ready",
        "qkv_done", "roped", "qk_ready", "hi_ready", "lo_ready", "hit_done", "lot_done", "qkt_ready", "v_ready"))
    gathered = c["moved"]["d_gathered"]
    x2_stored = [sem(f"d_x2_stored{s}") for s in range(2)]
    qkv_stored = [sem(f"d_qkv_stored{s}") for s in range(2)]

    def nothing(t, k, s):
        pass

    with nc.Block() as block:
        @block.sync
        def _(sp):
            sp.dma_start(w[:], w_qkv_dram.rearrange("(k p) n -> p k n", p=P)).then_inc(w_loaded, 16)

            def load(t, k, s):
                wait_apart(sp, c["ready"], (x2_ready, t - 1), (roped, 3 * (t - 1)))
                sp.dma_start(x_t[:, s, :], x_dram[bass.ts(t, P), :]).then_inc(x_loaded[s], 16)
                sp.dma_start(rope[:, s], rope_dram[bass.ts(t, P), :].rearrange("p (a d) -> p a d", a=2)).then_inc(x_loaded[s], 16)

            def store_x2(t, k, s):
                wait_apart(sp, c["ready"], (x2_ready, t + 1))
                sp.dma_start(sum_dram[bass.ts(t, P), :], x2[:, s, :]).then_inc(x2_stored[s], 16)

            def store_qkv(t, k, s):
                wait_apart(sp, c["ready"], (qkt_ready, 2 * t + 2), (v_ready, t + 1))
                sp.dma_start(qkt_dram[:, bass.ts(t, P)].rearrange("(j p) t -> p j t", p=P), qkt[:, s]).then_inc(qkv_stored[s], 16)
                sp.dma_start(v_dram[bass.ts(t, P), :], v_t[:, s, :]).then_inc(qkv_stored[s], 16)

            pipeline(sp, NT, [load, store_x2, nothing, nothing, store_qkv])
            for s in range(2):
                sp.wait_ge(x2_stored[s], 16 * (NT // 2))
                sp.wait_ge(qkv_stored[s], 32 * (NT // 2))

        @block.gpsimd
        def _(pool):
            def gather(t, k, s):
                wait(pool, x2_ready, t - 1)
                nc.gpsimd.tensor_copy(idx[:, s:s + 1, :], kept["pos"][:, bass.ds(t, 1), :]).then_inc(idx_ready, 1)
                nc.gpsimd.tensor_copy(prob[:, s:s + 1, :], kept["prob"][:, bass.ds(t, 1), :]).then_inc(idx_ready, 1)
                wait_apart(pool, c["ready"], (idx_ready, 2 * t + 2))
                for i in range(2):
                    nc.gpsimd.indirect_dma_start(
                        out=ye[i][:, s, :], out_offset=None, in_=outputs[:, :],
                        in_offset=bass.IndirectOffsetOnAxis(ap=idx[:, s, i:i + 1], axis=0)).then_inc(gathered[s], 16)

            def rsqrt(t, k, s):
                pool.wait_ge(var_ready, t + 1)
                nc.gpsimd.tensor_tensor(rstd[:, s:s + 1], var_eps[:, s:s + 1], mhalf[:, 0:1], ALU.pow).then_inc(rstd_ready, 1)

            def split(t, k, s):
                pool.wait_ge(roped, 3 * t + 3)
                wait(pool, lo_ready, t - 1)
                wait(pool, hi_ready, t - 1)
                nc.gpsimd.tensor_tensor(qk[:, s, :], by_cos[:, s, :], by_sin[:, s, :], ALU.add).then_inc(qk_ready, 1)
                pool.wait_ge(hi_ready, t + 1)
                wait(pool, lot_done, t - 1)
                nc.gpsimd.tensor_tensor(lo[:, s, :], qk[:, s, :], hi[:, s, :].bitcast(FP32), ALU.subtract).then_inc(lo_ready, 1)

            pipeline(pool, NT, [gather, rsqrt, split])

        @block.vector
        def _(dve):
            norm_chain = Chain(dve, ln_steps, 2)

            def norm(t, k, s):
                dve.wait_ge(x_loaded[s], 32 * k + 32)
                dve.wait_ge(gathered[s], 32 * k + 32)
                wait(dve, x2_stored[s], 16 * k)
                nc.vector.scalar_tensor_tensor(out=part[:, s, :], in0=ye[0][:, s, :], scalar=prob[:, s, 0:1], in1=x_t[:, s, :],
                                               op0=ALU.mult, op1=ALU.add).then_inc(x2_steps, 1)
                dve.wait_ge(x2_steps, t + 1)
                nc.vector.scalar_tensor_tensor(out=x2[:, s, :], in0=ye[1][:, s, :], scalar=prob[:, s, 1:2], in1=part[:, s, :],
                                               op0=ALU.mult, op1=ALU.add).then_inc(x2_ready, 1)
                dve.wait_ge(x2_ready, t + 1)
                norm_chain.at(t)
                norm_chain.step(nc.vector.bn_stats(stats[:, s, :], x2[:, s, :]))
                wait_apart(dve, c["ready"], (ln_steps, norm_chain.base + norm_chain.k))
                norm_chain.link(nc.vector.bn_aggr(mean_var[:, s, :], stats[:, s, :]))
                nc.vector.tensor_scalar(var_eps[:, s:s + 1], mean_var[:, s, 1:2], LN_EPS, None, ALU.add).then_inc(var_ready, 1)
                dve.wait_ge(rstd_ready, t + 1)
                wait(dve, xnt_done, t - 1)
                nc.vector.tensor_scalar(xn[:, s, :], x2[:, s, :], mean_var[:, s, 0:1], rstd[:, s:s + 1],
                                        ALU.subtract, ALU.mult).then_inc(xn_ready, 1)

            def turn(t, k, s):
                dve.wait_ge(qkv_done, t + 1)
                wait(dve, qk_ready, t - 1)
                heads = ps_qkv[s][:, 0:QK].rearrange("p (h d) -> p h d", d=HD)
                pairs = ps_qkv[s][:, 0:QK].rearrange("p (h d two) -> p h d two", two=2, d=HD // 2)
                out = by_sin[:, s, :].rearrange("p (h d two) -> p h d two", two=2, d=HD // 2)
                sin = rope[:, s, 1, :].rearrange("p (d two) -> p d two", two=2)
                nc.vector.tensor_tensor(by_cos[:, s, :].rearrange("p (h d) -> p h d", d=HD), heads,
                                        rope[:, s, 0, :].unsqueeze(1).broadcast_to([P, 2 * NH, HD]), ALU.mult).then_inc(roped, 1)
                for i in range(2):
                    nc.vector.tensor_tensor(out[:, :, :, i], pairs[:, :, :, 1 - i],
                                            sin[:, :, i].unsqueeze(1).broadcast_to([P, 2 * NH, HD // 2]), ALU.mult).then_inc(roped, 1)

            def copy_lo(t, k, s):
                dve.wait_ge(lot_done, t + 1)
                wait(dve, qkv_stored[s], 32 * k)
                nc.vector.tensor_copy(qkt[:, s, 4:8, :], ps_t[1][:]).then_inc(qkt_ready, 1)

            pipeline(dve, NT, [nothing, norm, turn, copy_lo])

        @block.scalar
        def _(act):
            def copy_xn(t, k, s):
                act.wait_ge(xnt_done, t + 1)
                wait(act, qkv_done, t - 1)
                nc.scalar.activation(xnt[:, s], ps_xnt[:], ACT.Copy).then_inc(xnt_ready, 1)

            def split(t, k, s):
                act.wait_ge(qkv_done, t + 1)
                act.wait_ge(roped, 3 * t + 3)
                wait(act, qkv_stored[s], 32 * k)
                nc.scalar.activation(v_t[:, s, :], ps_qkv[s][:, QK:], ACT.Copy).then_inc(v_ready, 1)
                act.wait_ge(qk_ready, t + 1)
                wait(act, hit_done, t - 1)
                wait(act, lo_ready, t - 1)
                nc.scalar.activation(hi[:, s, :], qk[:, s, :], ACT.Copy).then_inc(hi_ready, 1)

            def copy_hi(t, k, s):
                act.wait_ge(hit_done, t + 1)
                wait(act, qkv_stored[s], 32 * k)
                nc.scalar.activation(qkt[:, s, 0:4, :], ps_t[0][:], ACT.Copy).then_inc(qkt_ready, 1)

            pipeline(act, NT, [nothing, copy_xn, split, copy_hi])

        @block.tensor
        def _(pe):
            pe.wait_ge(w_loaded, 16)

            def project(t, k, s):
                pe.wait_ge(xn_ready, t + 1)
                wait(pe, xnt_ready, t)
                for j in range(KD):
                    last = nc.tensor.transpose(ps_xnt[:, j, :], xn[:, s, j * P:(j + 1) * P], ident[:])
                last.then_inc(xnt_done, 1)
                pe.wait_ge(xnt_ready, t + 1)
                wait(pe, roped, 3 * (t - 1))
                wait(pe, v_ready, t - 1)
                for n0, n1 in ((0, QK), (QK, 3 * DM)):
                    for j in range(KD):
                        last = nc.tensor.matmul(ps_qkv[s][:, n0:n1], xnt[:, s, j, :], w[:, j, n0:n1], start=(j == 0), stop=(j == KD - 1))
                last.then_inc(qkv_done, 1)

            def transpose_qk(t, k, s):
                pe.wait_ge(hi_ready, t + 1)
                wait(pe, qkt_ready, 2 * t)
                for j in range(4):
                    last = nc.tensor.transpose(ps_t[0][:, j, :], hi[:, s, j * P:(j + 1) * P].bitcast(FP32), ident[:])
                last.then_inc(hit_done, 1)
                pe.wait_ge(lo_ready, t + 1)
                for j in range(4):
                    last = nc.tensor.transpose(ps_t[1][:, j, :], lo[:, s, j * P:(j + 1) * P], ident[:])
                last.then_inc(lot_done, 1)

            pipeline(pe, NT, [nothing, project, nothing, transpose_qk])


def attention(nc, sb, pb, sem, c, qkt_dram, v_dram, headst_dram, sums_dram):
    ident = c["ident"]
    heads = BATCH * NH
    VR = HD + 1
    NC = SEQ // P
    KS = 4 * HD
    HALF = 4
    ks = sb("t_ks", [KS + 2, SLOTS, SEQ], FP32R)
    qs = sb("t_qs", [KS + 2, SLOTS, SEQ], FP32R)
    v_raw = sb("t_v_raw", [P, NC, SLOTS * HD])
    vs = sb("t_vs", [P, SLOTS, NC, VR])
    later = sb("t_later", [P, P], BF16)
    ident_b = sb("t_ident_b", [P, P], BF16)
    maxes = sb("t_maxes", [P, 2, NC, 2])
    row_max = sb("t_row_max", [P, 2, NC])
    neg_max = sb("t_neg_max", [NC, 2, P], FP32R)
    packs, at = [], 0
    for half in range(2):
        regions = [(kc, max(kc, HALF * half) * P, (HALF * (half + 1) - max(kc, HALF * half)) * P)
                   for kc in range(HALF * (half + 1))]
        for i in range(0, len(regions), 2):
            pack = []
            base = at
            for kc, q0, width in regions[i:i + 2]:
                pack.append((kc, q0, width, at - base, at))
                at += width
            packs.append((half, base, at - base, pack))
    probs = sb("t_probs", [P, at])
    att = sb("t_att", [VR, SLOTS, 2, HALF * P])
    ps_s = [pb(f"t_ps_s{i}", [P, 4 * P]) for i in range(2)]
    ps_st = [pb(f"t_ps_st{i}", [P, 8 * P]) for i in range(2)]
    ps_max = pb("t_ps_max", [NC, P])
    ps_o = pb("t_ps_o", [32 + VR, HALF * P])
    even = sb("t_even", [VR, HALF * P])
    pieces = [(qc, k0, min(k0 + 4 * P, (qc + 1) * P)) for qc in range(NC) for k0 in range(0, (qc + 1) * P, 4 * P)]
    NPC, NPK = len(pieces), len(packs)
    NP0 = sum(p[0] == 0 for p in packs)
    diagonal = [any(q0 == kc * P for kc, q0, *_ in p[3]) for p in packs]
    ND = sum(diagonal)
    filled, set_up = sem("t_filled"), sem("t_set_up")
    qk_loaded = [sem(f"t_qk_loaded{s}") for s in range(SLOTS)]
    row_loaded = [sem(f"t_row_loaded{s}") for s in range(SLOTS)]
    (v_loaded, vs_ready, s_done, piece_ready, max_ready, maxt_done, neg_ready, st_done, exp_ready, masked, av_done,
     even_ready, att_ready) = (sem("t_" + n) for n in (
        "v_loaded", "vs_ready", "s_done", "piece_ready", "max_ready", "maxt_done", "neg_ready", "st_done", "exp_ready",
        "masked", "av_done", "even_ready", "att_ready"))
    stored = [sem(f"t_stored{s}") for s in range(SLOTS)]

    def nothing(n, k, s):
        pass

    with nc.Block() as block:
        @block.sync
        def _(sp):
            def place(k):
                if isinstance(k, int):
                    return k // (NH // SLOTS), k % (NH // SLOTS)
                batch = sp.snap(k // (NH // SLOTS))
                return batch, nc.s_assert_within(k - batch * (NH // SLOTS), 0, NH // SLOTS - 1,
                                                 skip_runtime_bounds_check_because="it is a remainder")

            def load(n, k, s):
                batch, group = place(k)
                wait_apart(sp, c["ready"], (st_done, NPK * (n - SLOTS) + NPK), (vs_ready, n if s == 0 else 0))
                if s == 0:
                    sp.dma_start(v_raw[:], v_dram[bass.ts(batch, SEQ), bass.ts(group, SLOTS * HD)]
                                 .rearrange("(c p) d -> p c d", p=P)).then_inc(v_loaded, 16)
                cols = bass.ts(batch, SEQ)
                for part in range(4):
                    q_part, k_part = part % 2, part // 2
                    for dst, which, hl in ((qs, 0, q_part), (ks, 1, k_part)):
                        first = hl * 2 * DM + which * DM + s * HD
                        sp.dma_start(dst[part * HD:(part + 1) * HD, s, :].bitcast(FP32),
                                     qkt_dram[bass.ds(group * (SLOTS * HD) + first, HD), cols]).then_inc(qk_loaded[s], 16)

            def row(n, k, s):
                wait_apart(sp, c["ready"], (neg_ready, n + 1))
                sp.dma_start(qs[KS + 1:KS + 2, s, :].bitcast(FP32).rearrange("o (c q) -> o c q", c=NC),
                             neg_max[:, s % 2, :].bitcast(FP32)).then_inc(row_loaded[s], 16)

            def store(n, k, s):
                batch, group = place(k)
                wait_apart(sp, c["ready"], (att_ready, 2 * n + 2))
                sp.dma_start(headst_dram[bass.ds(group * (SLOTS * HD) + s * HD, HD), bass.ts(batch, SEQ)],
                             att[0:HD, s].rearrange("p h q -> p (h q)")).then_inc(stored[s], 16)
                sp.dma_start(sums_dram[bass.ds(group * SLOTS + s, 1), bass.ts(batch, SEQ)],
                             att[HD:VR, s].rearrange("p h q -> p (h q)")).then_inc(stored[s], 16)

            sp.wait_ge(filled, 6)
            pipeline(sp, heads, [load, nothing, row, nothing, store], SLOTS)
            for s in range(SLOTS):
                sp.wait_ge(stored[s], 32 * (heads // SLOTS))

        @block.gpsimd
        def _(pool):
            nc.gpsimd.memset(later[:], 0.0).then_inc(filled, 1)
            nc.gpsimd.memset(ident_b[:], 0.0).then_inc(filled, 1)
            nc.gpsimd.memset(maxes[:], -3.0e38).then_inc(filled, 1)
            nc.gpsimd.memset(vs[:], 1.0).then_inc(filled, 1)
            pool.wait_ge(filled, 4)
            nc.gpsimd.memset(ks[KS:KS + 2].bitcast(FP32), 1.0).then_inc(filled, 1)
            pool.wait_ge(filled, 5)
            nc.gpsimd.memset(qs[KS:KS + 1].bitcast(FP32), 0.0).then_inc(filled, 1)
            pool.wait_ge(filled, 6)
            nc.gpsimd.affine_select(out=later[:], in_=later[:], compare_op=ALU.is_ge, fill=-1.0e30, base=0,
                                    pattern=[[-1, P]], channel_multiplier=1).then_inc(set_up, 1)
            nc.gpsimd.affine_select(out=ident_b[:], in_=ident_b[:], compare_op=ALU.not_equal, fill=1.0, base=0,
                                    pattern=[[-1, P]], channel_multiplier=1).then_inc(set_up, 1)

            def values(n, k, s):
                wait_apart(pool, c["ready"], (v_loaded, 16 * k + 16), (av_done, NPK * (n - SLOTS) + NPK))
                nc.gpsimd.tensor_copy(vs[:, s, :, 0:HD], v_raw[:, :, s * HD:(s + 1) * HD]).then_inc(vs_ready, 1)

            def mask(n, k, s):
                for i, (half, base, width, pack) in enumerate(packs):
                    if diagonal[i]:
                        wait_apart(pool, c["ready"], (exp_ready, NPK * n + i + 1))
                        for kc, q0, w, off, col in pack:
                            if q0 == kc * P:
                                block_ = probs[:, col:col + P]
                                last = nc.gpsimd.affine_select(out=block_, in_=block_, compare_op=ALU.is_ge, fill=0.0, base=0,
                                                               pattern=[[1, P]], channel_multiplier=-1)
                        last.then_inc(masked, 1)

            pipeline(pool, heads, [values, nothing, mask], SLOTS)

        def ticks(eng, tick):
            def at(n, k, s, live):
                tick(lambda d: (n - d, k + (s - d) // SLOTS, (s - d) % SLOTS), live)

            for n in range(SLOTS):
                at(n, 0, n, lambda d: n >= d)
            with eng.Fori(1, heads // SLOTS) as turn:
                for s in range(SLOTS):
                    at(turn * SLOTS + s, turn, s, lambda d: True)
            for n in range(heads, heads + 3):
                at(n, heads // SLOTS, n - heads, lambda d: n - d < heads)

        @block.vector
        def _(dve):
            dve.wait_ge(filled, 6)

            def maximum(n, s, i):
                qc, k0, k1 = pieces[i]
                dve.wait_ge(s_done, NPC * n + i + 1)
                nc.vector.reduce_max(maxes[:, s % 2, qc, k0 // (4 * P):k0 // (4 * P) + 1], ps_s[i % 2][:, 0:k1 - k0],
                                     AXX).then_inc(piece_ready, 1)

            def outputs(n, k, s, half):
                dve.wait_ge(even_ready, 2 * n + half + 1)
                if half == 0:
                    wait(dve, stored[s], 32 * k)
                    nc.vector.tensor_copy(att[:, s, half, 0:P], even[:, 0:P])
                    nc.vector.tensor_tensor(att[:, s, half, P:], ps_o[32:32 + VR, P:], even[:, P:], ALU.add).then_inc(att_ready, 1)
                else:
                    nc.vector.tensor_tensor(att[:, s, half, :], ps_o[32:32 + VR, :], even[:], ALU.add).then_inc(att_ready, 1)

            def tick(ago, live):
                n, _, s = ago(0)
                for i in range(NPK):
                    if live(0):
                        maximum(n, s, 2 * i)
                        maximum(n, s, 2 * i + 1)
                    if i == 1 and live(3):
                        outputs(*ago(3), 1)
                    if i == 3 and live(2):
                        outputs(*ago(2), 0)
                if live(0):
                    wait(dve, maxt_done, n - 1)
                    dve.wait_ge(piece_ready, NPC * n + NPC)
                    nc.vector.reduce_max(row_max[:, s % 2, :], maxes[:, s % 2], AXX).then_inc(max_ready, 1)

            ticks(dve, tick)

        @block.scalar
        def _(act):
            def negate(n, k, s):
                act.wait_ge(maxt_done, n + 1)
                wait(act, row_loaded[(s - 2) % SLOTS], 16 * (k + 1 if s >= 2 else k))
                nc.scalar.activation(neg_max[:, s % 2, :], ps_max[:], ACT.Copy, scale=-1.0).then_inc(neg_ready, 1)

            def exponentials(n, i):
                half, base, width, pack = packs[i]
                act.wait_ge(st_done, NPK * n + i + 1)
                wait(act, av_done, NPK * (n - 1) + i + 1)
                nc.scalar.activation(probs[:, base:base + width], ps_st[i % 2][:, 0:width], ACT.Exp,
                                     scale=HD ** -0.5).then_inc(exp_ready, 1)

            def even_chunks(n, k, s, half):
                act.wait_ge(av_done, NPK * n + (NPK if half else NP0))
                wait(act, att_ready, 2 * n + half)
                nc.scalar.activation(even[:], ps_o[0:VR], ACT.Copy).then_inc(even_ready, 1)

            def tick(ago, live):
                for i in range(NPK):
                    if live(2):
                        exponentials(ago(2)[0], i)
                    if i == 0 and live(1):
                        negate(*ago(1))
                    if i == 1 and live(3):
                        even_chunks(*ago(3), 1)
                    if i == 3 and live(2):
                        even_chunks(*ago(2), 0)

            ticks(act, tick)

        @block.tensor
        def _(pe):
            pe.wait_ge(filled, 6)
            pe.wait_ge(set_up, 2)

            def piece(n, s, i):
                qc, k0, k1 = pieces[i]
                wait(pe, piece_ready, NPC * n + i - 1)
                diag = qc * P - k0
                inside = 0 <= diag < k1 - k0
                last = nc.tensor.matmul(ps_s[i % 2][:, 0:k1 - k0], qs[0:KS + 1, s, qc * P:(qc + 1) * P], ks[0:KS + 1, s, k0:k1],
                                        start=True, stop=not inside)
                if inside:
                    last = nc.tensor.matmul(ps_s[i % 2][:, diag:diag + P], ident_b[:], later[:], start=False, stop=True)
                last.then_inc(s_done, 1)

            def pack_scores(n, s, i):
                wait(pe, exp_ready, NPK * n + i - 1)
                for kc, q0, width, off, col in packs[i][3]:
                    last = nc.tensor.matmul(ps_st[i % 2][:, off:off + width], ks[:, s, kc * P:(kc + 1) * P], qs[:, s, q0:q0 + width],
                                            start=True, stop=True)
                last.then_inc(st_done, 1)

            def average(n, s, i):
                half, base, _, pack = packs[i]
                if diagonal[i]:
                    pe.wait_ge(masked, ND * n + sum(diagonal[:i + 1]))
                else:
                    pe.wait_ge(exp_ready, NPK * n + i + 1)
                if i == 0:
                    pe.wait_ge(vs_ready, n + 1)
                    wait(pe, att_ready, 2 * n)
                if i == NP0:
                    pe.wait_ge(att_ready, 2 * n + 1)
                for kc, q0, width, off, col in pack:
                    at = q0 - half * HALF * P
                    odd = kc % 2
                    last = nc.tensor.matmul(ps_o[32 * odd:32 * odd + VR, at:at + width], vs[:, s, kc, :], probs[:, col:col + width],
                                            start=(kc < 2), stop=(kc >= HALF * (half + 1) - 2))
                last.then_inc(av_done, 1)

            def tick(ago, live):
                n, k, s = ago(0)
                n2, k2, s2 = ago(2)
                if live(2):
                    pe.wait_ge(row_loaded[s2], 16 * k2 + 16)
                for i in range(NPK):
                    if live(2):
                        pack_scores(n2, s2, i)
                    if i == 0 and live(1):
                        n1, _, s1 = ago(1)
                        pe.wait_ge(max_ready, n1 + 1)
                        wait(pe, neg_ready, n1)
                        nc.tensor.transpose(ps_max[:], row_max[:, s1 % 2, :], ident[:]).then_inc(maxt_done, 1)
                    if live(0):
                        if i == 0:
                            pe.wait_ge(qk_loaded[s], 128 * k + 128)
                        piece(n, s, 2 * i)
                        piece(n, s, 2 * i + 1)
                    if i < 2 and live(3):
                        n3, _, s3 = ago(3)
                        average(n3, s3, NPK - 2 + i)
                    if i >= 2 and live(2):
                        average(n2, s2, i - 2)

            ticks(pe, tick)


FS = 256


def finish(nc, sb, pb, sem, c, x_dram, xn_dram, outputs, kept, sg_dram, su_dram, sd_dram, out_dram):
    ident = c["ident"]
    w_up = sb("f_w_up", [P, KD, 2 * FS])
    w_down = sb("f_w_down", [P, FS // P, DM])
    x_t = sb("f_x", [P, 2, DM])
    xn = sb("f_xn", [P, 2, DM])
    idx = sb("f_idx", [P, 2, 2], U32)
    prob = sb("f_prob", [P, 2, 2])
    ye = [sb(f"f_ye{i}", [P, 2, DM]) for i in range(2)]
    one_more = sb("f_one_more", [P, 2, DM])
    routed = sb("f_routed", [P, 2, DM])
    y = sb("f_y", [P, 2, DM])
    xnt = sb("f_xnt", [P, 2, KD, P])
    sig = sb("f_sig", [P, 2, FS])
    gated = sb("f_gated", [P, 2, FS])
    h = sb("f_h", [P, 2, FS])
    ht = sb("f_ht", [P, 2, FS // P, P])
    ps_x = pb("f_ps_x", [P, KD, P])
    ps_h = [pb(f"f_ps_h{s}", [P, 2 * FS]) for s in range(2)]
    ps_ht = pb("f_ps_ht", [P, FS // P, P])
    ps_y = pb("f_ps_y", [P, DM])
    w_loaded = sem("f_w_loaded")
    x_loaded = [sem(f"f_x_loaded{s}") for s in range(2)]
    gathered = c["moved"]["f_gathered"]
    stored = [sem(f"f_stored{s}") for s in range(2)]
    idx_ready, sum_steps, routed_ready, xt_done, xt_ready, h_done, sig_ready, gated_ready, h_ready, ht_done, ht_ready, \
        y_done, y_ready = (sem("f_" + n) for n in (
            "idx_ready", "sum_steps", "routed_ready", "xt_done", "xt_ready", "h_done", "sig_ready", "gated_ready", "h_ready",
            "ht_done", "ht_ready", "y_done", "y_ready"))

    def nothing(t, k, s):
        pass

    with nc.Block() as block:
        @block.sync
        def _(sp):
            sp.dma_start(w_up[:, :, 0:FS], sg_dram.rearrange("(k p) n -> p k n", p=P)).then_inc(w_loaded, 16)
            sp.dma_start(w_up[:, :, FS:2 * FS], su_dram.rearrange("(k p) n -> p k n", p=P)).then_inc(w_loaded, 16)
            sp.dma_start(w_down[:], sd_dram.rearrange("(k p) n -> p k n", p=P)).then_inc(w_loaded, 16)

            def load(t, k, s):
                wait_apart(sp, c["ready"], (xt_done, t - 1), (routed_ready, t - 1))
                sp.dma_start(xn[:, s, :], xn_dram[bass.ts(t, P), :]).then_inc(x_loaded[s], 16)
                sp.dma_start(x_t[:, s, :], x_dram[bass.ts(t, P), :]).then_inc(x_loaded[s], 16)

            def store(t, k, s):
                wait_apart(sp, c["ready"], (y_ready, t + 1))
                sp.dma_start(out_dram[bass.ts(t, P), :], y[:, s, :]).then_inc(stored[s], 16)

            pipeline(sp, NT, [load, nothing, nothing, nothing, store])
            for s in range(2):
                sp.wait_ge(stored[s], 16 * (NT // 2))

        @block.gpsimd
        def _(pool):
            def gather(t, k, s):
                wait(pool, routed_ready, t - 1)
                nc.gpsimd.tensor_copy(idx[:, s:s + 1, :], kept["pos"][:, bass.ds(t, 1), :]).then_inc(idx_ready, 1)
                nc.gpsimd.tensor_copy(prob[:, s:s + 1, :], kept["prob"][:, bass.ds(t, 1), :]).then_inc(idx_ready, 1)
                wait_apart(pool, c["ready"], (idx_ready, 2 * t + 2))
                for i in range(2):
                    nc.gpsimd.indirect_dma_start(
                        out=ye[i][:, s, :], out_offset=None, in_=outputs[:, :],
                        in_offset=bass.IndirectOffsetOnAxis(ap=idx[:, s, i:i + 1], axis=0)).then_inc(gathered[s], 16)

            pipeline(pool, NT, [gather])

        @block.vector
        def _(dve):
            def add_routed(t, k, s):
                dve.wait_ge(x_loaded[s], 32 * k + 32)
                dve.wait_ge(gathered[s], 32 * k + 32)
                wait(dve, y_ready, t - 1)
                nc.vector.scalar_tensor_tensor(out=one_more[:, s, :], in0=ye[0][:, s, :], scalar=prob[:, s, 0:1], in1=x_t[:, s, :],
                                               op0=ALU.mult, op1=ALU.add).then_inc(sum_steps, 1)
                dve.wait_ge(sum_steps, t + 1)
                nc.vector.scalar_tensor_tensor(out=routed[:, s, :], in0=ye[1][:, s, :], scalar=prob[:, s, 1:2], in1=one_more[:, s, :],
                                               op0=ALU.mult, op1=ALU.add).then_inc(routed_ready, 1)

            def gate(t, k, s):
                dve.wait_ge(sig_ready, t + 1)
                nc.vector.tensor_tensor(gated[:, s, :], ps_h[s][:, 0:FS], sig[:, s, :], ALU.mult).then_inc(gated_ready, 1)
                dve.wait_ge(gated_ready, t + 1)
                wait(dve, ht_done, t - 1)
                nc.vector.tensor_tensor(h[:, s, :], ps_h[s][:, FS:2 * FS], gated[:, s, :], ALU.mult).then_inc(h_ready, 1)

            def add_shared(t, k, s):
                dve.wait_ge(y_done, t + 1)
                dve.wait_ge(routed_ready, t + 1)
                wait(dve, stored[s], 16 * k)
                nc.vector.tensor_tensor(y[:, s, :], routed[:, s, :], ps_y[:], ALU.add).then_inc(y_ready, 1)

            def combine(t, k, s):
                gate(t, k, s)
                add_routed(t, k, s)

            pipeline(dve, NT, [nothing, combine, nothing, add_shared], order=(3, 1))

        @block.scalar
        def _(act):
            def copy_x(t, k, s):
                act.wait_ge(xt_done, t + 1)
                wait(act, h_done, t - 1)
                nc.scalar.activation(xnt[:, s], ps_x[:], ACT.Copy).then_inc(xt_ready, 1)

            def sigmoid(t, k, s):
                act.wait_ge(h_done, t + 1)
                wait(act, gated_ready, t - 1)
                nc.scalar.activation(sig[:, s, :], ps_h[s][:, 0:FS], ACT.Sigmoid).then_inc(sig_ready, 1)

            def copy_h(t, k, s):
                act.wait_ge(ht_done, t + 1)
                wait(act, y_done, t - 1)
                nc.scalar.activation(ht[:, s], ps_ht[:], ACT.Copy).then_inc(ht_ready, 1)

            pipeline(act, NT, [copy_x, sigmoid, copy_h])

        @block.tensor
        def _(pe):
            pe.wait_ge(w_loaded, 48)

            def go_up(t, k, s):
                pe.wait_ge(x_loaded[s], 32 * k + 32)
                wait(pe, xt_ready, t)
                for j in range(KD):
                    last = nc.tensor.transpose(ps_x[:, j, :], xn[:, s, j * P:(j + 1) * P], ident[:])
                last.then_inc(xt_done, 1)
                pe.wait_ge(xt_ready, t + 1)
                wait(pe, h_ready, t - 1)
                for j in range(KD):
                    last = nc.tensor.matmul(ps_h[s][:], xnt[:, s, j, :], w_up[:, j, :], start=(j == 0), stop=(j == KD - 1))
                last.then_inc(h_done, 1)

            def transpose_h(t, k, s):
                pe.wait_ge(h_ready, t + 1)
                wait(pe, ht_ready, t)
                for j in range(FS // P):
                    last = nc.tensor.transpose(ps_ht[:, j, :], h[:, s, j * P:(j + 1) * P], ident[:])
                last.then_inc(ht_done, 1)

            def go_down(t, k, s):
                pe.wait_ge(ht_ready, t + 1)
                wait(pe, y_ready, t)
                for j in range(FS // P):
                    last = nc.tensor.matmul(ps_y[:], ht[:, s, j, :], w_down[:, j, :], start=(j == 0), stop=(j == FS // P - 1))
                last.then_inc(y_done, 1)

            pipeline(pe, NT, [go_up, transpose_h, go_down])


def build(nc, x, w_in, w_abc, w_out, norm_w, gate_w, gate_b, w1, b1, w2, b2, w_qkv, w_o, rope, w_route, w_gu, w_d,
          sg, su, sd, out):
    E0, E1 = gate_w.shape[1], w_route.shape[1]
    H0, F1 = w1.shape[2], w_d.shape[1]
    flat = lambda a: a.rearrange("b t m -> (b t) m")

    def scratch(name, shape):
        return nc.dram_tensor(name, shape, FP32).ap()

    used = []

    def phase(build_it, *args, **more):
        with ExitStack() as own:
            def own_sem(n):
                s = own.enter_context(nc.semaphore(n))
                used.append(s.num)
                return s

            build_it(nc, lambda n, s, d=FP32: own.enter_context(nc.sbuf_tensor(n, s, d)),
                     lambda n, s, d=FP32: own.enter_context(nc.psum_tensor(n, s, d)),
                     own_sem, *args, **more)

    def router_keep(own, name, E):
        sb = lambda n, s, d=FP32: own.enter_context(nc.sbuf_tensor(name + n, s, d))
        return {"pos": sb("pos_all", [P, NT, 2], U32), "prob": sb("prob_all", [P, NT, 2]),
                "tiles": sb("tile_list", [1, 2, 2 * NT + E], U32)}

    xi_dram, abc_dram = scratch("xi_dram", [TOK, DI]), scratch("abc_dram", [TOK, 3 * NS])
    x1_dram, x2_dram, x3_dram = (scratch(n, [TOK, DM]) for n in ("x1_dram", "x2_dram", "x3_dram"))
    xn4_dram, v_dram = (scratch(n, [TOK, DM]) for n in ("xn4_dram", "v_dram"))
    headst_dram = scratch("headst_dram", [DM, TOK])
    sums_dram, inv_dram = scratch("sums_dram", [NH, TOK]), scratch("inv_dram", [NH, TOK])
    qkt_dram = scratch("qkt_dram", [4 * DM, TOK])
    gathered = [scratch(f"gathered{i}_dram", [E * (CAP + P), DM]) for i, E in enumerate((E0, E1))]
    outputs = [scratch(f"outputs{i}_dram", [(2 * NT + E) * P, DM]) for i, E in enumerate((E0, E1))]

    with ExitStack() as whole:
        keep = lambda n, s, d=FP32: whole.enter_context(nc.sbuf_tensor(n, s, d))
        sem = lambda n: whole.enter_context(nc.semaphore(n))
        c = constants(nc, keep, sem)
        c["moved"] = {n: [sem(f"{n}{s}") for s in range(2)] for n in ("r0_scattered", "d_gathered", "r1_scattered", "f_gathered")}
        x_in = flat(x)
        phase(ssm_project, c, x_in, xi_dram, abc_dram, w_in, w_abc)
        phase(ssm_scan, c, x_in, xi_dram, abc_dram, w_out, norm_w, x1_dram)
        with ExitStack() as layer:
            kept = router_keep(layer, "r0_", E0)
            phase(route, c, "r0_", E0, x1_dram, None, gathered[0], gate_w, gate_b, kept)
            with ExitStack() as weights:
                wsb = lambda n, s, d=FP32: weights.enter_context(nc.sbuf_tensor(n, s, d))
                w1_sb, w2_sb = wsb("w1_sb", [P, KD, E0 * H0]), wsb("w2_sb", [P, H0 // P, E0 * DM])
                b1_sb, b2_sb = wsb("b1_sb", [P, E0 * H0]), wsb("b2_sb", [P, E0 * DM])
                loaded = weights.enter_context(nc.semaphore("moe0_loaded"))
                load_moe0(nc, loaded, w1_sb, w1, w2_sb, w2, b1_sb, b1, b2_sb, b2)
                phase(run_experts, c, "m0_", E0, gathered[0], outputs[0], kept, (H0, w1_sb, b1_sb), (H0 // P, w2_sb, b2_sb))
            phase(project_qkv, c, x1_dram, outputs[0], kept, x2_dram, w_qkv, rope, qkt_dram, v_dram)
        with nc.Block() as block:
            @block.gpsimd
            def _(pool):
                pool.sem_clear(range(min(used), max(used) + 1))

        phase(attention, c, qkt_dram, v_dram, headst_dram, sums_dram)
        phase(invert, sums_dram, inv_dram)

        with ExitStack() as layer:
            kept = router_keep(layer, "r1_", E1)
            phase(route, c, "r1_", E1, None, xn4_dram, gathered[1], w_route, None, kept,
                  attn=(headst_dram, inv_dram, w_o, x2_dram, x3_dram))
            with ExitStack() as weights:
                wsb = lambda n, s, d=FP32: weights.enter_context(nc.sbuf_tensor(n, s, d))
                wgu_sb, wd_sb = wsb("wgu_sb", [P, KD, E1 * 2 * F1]), wsb("wd_sb", [P, F1 // P, E1 * DM])
                loaded = weights.enter_context(nc.semaphore("moe1_loaded"))
                load_moe1(nc, loaded, wgu_sb, w_gu, wd_sb, w_d)
                phase(run_experts, c, "m1_", E1, gathered[1], outputs[1], kept, (2 * F1, wgu_sb, None), (F1 // P, wd_sb, None))
            phase(finish, c, x3_dram, xn4_dram, outputs[1], kept, sg, su, sd, flat(out))


def invert(nc, sb, pb, sem, sums_dram, inv_dram):
    per = NH * TOK // P
    sums, inv = sb("i_sums", [P, per]), sb("i_inv", [P, per])
    sums_loaded, inv_ready, inv_stored = sem("i_sums_loaded"), sem("i_inv_ready"), sem("i_inv_stored")

    def spread(dram):
        return dram.rearrange("h (c t) -> (h c) t", t=per)

    with nc.Block() as block:
        @block.sync
        def _(sp):
            sp.dma_start(sums[:], spread(sums_dram)).then_inc(sums_loaded, 16)
            sp.wait_ge(inv_ready, 1)
            sp.dma_start(spread(inv_dram), inv[:]).then_inc(inv_stored, 16)
            sp.wait_ge(inv_stored, 16)

        @block.vector
        def _(dve):
            dve.wait_ge(sums_loaded, 16)
            nc.vector.reciprocal(inv[:], sums[:]).then_inc(inv_ready, 1)


def load_moe0(nc, loaded, w1_sb, w1, w2_sb, w2, b1_sb, b1, b2_sb, b2):
    E, _, H0 = w1.shape
    with nc.Block() as block:
        @block.sync
        def _(sp):
            n = 0
            for j in range(KD):
                sp.dma_start(w1_sb[:, j, :].rearrange("p (e h) -> p e h", e=E), w1[:, j * P:(j + 1) * P, :].rearrange("e p h -> p e h")).then_inc(loaded, 16)
                n += 16
            for j in range(H0 // P):
                sp.dma_start(w2_sb[:, j, :].rearrange("p (e h) -> p e h", e=E), w2[:, j * P:(j + 1) * P, :].rearrange("e p h -> p e h")).then_inc(loaded, 16)
                n += 16
            for dst, src in ((b1_sb, b1), (b2_sb, b2)):
                sp.dma_start(dst[:], src.rearrange("e h -> (e h)").partition_broadcast(P)).then_inc(loaded, 16)
                n += 16
            sp.wait_ge(loaded, n)


def load_moe1(nc, loaded, wgu_sb, w_gu, wd_sb, w_d):
    E = w_gu.shape[0]
    with nc.Block() as block:
        @block.sync
        def _(sp):
            for j in range(KD):
                sp.dma_start(wgu_sb[:, j, :].rearrange("p (e h) -> p e h", e=E), w_gu[:, j * P:(j + 1) * P, :].rearrange("e p h -> p e h")).then_inc(loaded, 16)
            sp.dma_start(wd_sb[:, 0, :].rearrange("p (e h) -> p e h", e=E), w_d.rearrange("e p h -> p e h")).then_inc(loaded, 16)
            sp.wait_ge(loaded, 16 * (KD + 1))


_OUTS = [((4, 1024, 256), 'float32')]


def kernel(**inputs):
    import numpy as _np
    import concourse.bacc as _bacc
    from concourse import mybir as _mybir
    from concourse.bass_utils import run_bass_kernel_spmd as _run

    a = inputs
    freq = 10000.0 ** (_np.arange(0, HD, 2, dtype=_np.float32) / _np.float32(HD))
    angle = _np.arange(SEQ, dtype=_np.float32)[:, None] / freq[None, :].astype(_np.float32)
    cos, sin = _np.cos(angle), _np.sin(angle)
    rope = _np.concatenate([_np.repeat(cos, 2, axis=1), _np.stack([-sin, sin], axis=-1).reshape(SEQ, HD)], axis=1)
    laid_out = {
        "x": a["L0_attn_x"], "w_in": a["L0_attn_W_in"],
        "w_abc": _np.concatenate([a["L0_attn_W_A"], a["L0_attn_W_B"], a["L0_attn_W_C"]], axis=1),
        "w_out": a["L0_attn_W_out"], "norm_w": _np.reshape(a["L0_attn_norm_w"], (KI, P)).T,
        "gate_w": a["L0_ffn_gate_w"].T, "gate_b": _np.reshape(a["L0_ffn_gate_b"], (1, -1)),
        "w1": a["L0_ffn_w1"], "b1": a["L0_ffn_b1"], "w2": a["L0_ffn_w2"], "b2": a["L0_ffn_b2"],
        "w_qkv": a["L1_attn_W_qkv"].T, "w_o": a["L1_attn_W_o"].T,
        "rope": _np.tile(rope.astype(_np.float32), (BATCH, 1)),
        "w_route": a["L1_ffn_Wr"], "w_gu": _np.concatenate([a["L1_ffn_Wg"], a["L1_ffn_Wu"]], axis=2),
        "w_d": a["L1_ffn_Wd"], "sg": a["L1_ffn_Sg"], "su": a["L1_ffn_Su"], "sd": a["L1_ffn_Sd"],
    }
    nc = _bacc.Bacc("TRN2", target_bir_lowering=False, num_devices=1)
    arrays, args = {}, []
    for name, value in laid_out.items():
        value = _np.ascontiguousarray(value)
        arrays[f"in_{name}_dram"] = value
        args.append(nc.dram_tensor(f"in_{name}_dram", value.shape, _mybir.dt.from_np(value.dtype), kind="ExternalInput").ap())
    for i, (shape, dtype) in enumerate(_OUTS):
        args.append(nc.dram_tensor(f"out_{i}_dram", shape, _mybir.dt.from_np(_np.dtype(dtype)), kind="ExternalOutput").ap())
    build(nc, *args)
    r = _run(nc, [arrays], core_ids=[0])
    return r.results[0]["out_0_dram"]
```

```python
import concourse.bass as bass
from concourse import mybir
from contextlib import ExitStack

FP32 = mybir.dt.float32
FP32R = mybir.dt.float32r
BF16 = mybir.dt.bfloat16
U32 = mybir.dt.uint32
ALU = mybir.AluOpType
ACT = mybir.ActivationFunctionType
AXX = mybir.AxisListType.X

P = 128
H = P // 2
BATCH, SEQ, DM = 4, 1024, 256
TOK = BATCH * SEQ
NT = TOK // P
TPB = SEQ // P
KD = DM // P
LN_EPS = 1e-5

DI, NS = 512, 16
KI = DI // P
NH, HD = 16, 16
RMS_EPS = 1.1920929e-07


class Chain:

    def __init__(self, eng, sem, per_tile):
        self.eng, self.sem, self.per, self.k, self.base = eng, sem, per_tile, 0, 0

    def at(self, t):
        assert self.k in (0, self.per), (self.k, self.per)
        self.base, self.k = t * self.per, 0

    def step(self, ins):
        ins.then_inc(self.sem, 1)
        self.k += 1
        return ins

    def wait(self):
        self.eng.wait_ge(self.sem, self.base + self.k)

    def link(self, ins):
        self.step(ins)
        self.wait()


def wait_apart(eng, const_ready, *waits):
    values = [(s, v if isinstance(v, int) else eng.compute_val(v)) for s, v in waits if not isinstance(v, int) or v > 0]
    eng.wait_ge(const_ready, 6)
    for s, v in values:
        eng.wait_ge(s, v)


def wait(eng, sem, value):
    if not isinstance(value, int) or value > 0:
        eng.wait_ge(sem, value)


def nothing(t, k, s):
    pass


def pipeline(eng, tiles, stages, unroll=2, order=None):
    interleaved(eng, tiles, [(s, stages[s]) for s in (order or range(len(stages)))], unroll)


def interleaved(eng, tiles, steps, unroll=2):
    lags = max(lag for lag, _ in steps)
    first = -(-(lags + 2) // unroll) * unroll

    def at(tau):
        for lag, step in steps:
            if 0 <= tau - lag < tiles:
                step(tau - lag, (tau - lag) // unroll, (tau - lag) % unroll)

    for tau in range(first):
        at(tau)
    with eng.Fori(first // unroll, tiles // unroll) as turn:
        for r in range(unroll):
            for lag, step in steps:
                d = r - lag
                step(turn * unroll + d, turn + d // unroll, d % unroll)
    for tau in range(tiles, tiles + lags):
        at(tau)




def constants(nc, sb, sem):
    c = {}
    c["ident"] = ident = sb("ident", [P, P])
    c["neg_tri"] = neg_tri = sb("neg_tri", [P, P])
    c["neg_suf"] = neg_suf = sb("neg_suf", [P, P])
    c["neg_mid0"] = neg_mid0 = sb("neg_mid0", [P, P])
    c["neg_mid1"] = neg_mid1 = sb("neg_mid1", [P, P])
    c["neg_own"] = neg_own = sb("neg_own", [P, P])
    c["neg_one"] = neg_one = sb("neg_one", [P, 1])
    c["one"] = one = sb("one", [P, 1])
    c["ones_row"] = ones_row = sb("ones_row", [1, P])
    c["mhalf"] = mhalf = sb("mhalf", [P, 4])
    c["causal4"] = causal4 = sb("causal4", [P, 4, P])
    made = sem("const_filled")
    ready = sem("const_ready")
    c["ready"] = ready
    with nc.Block() as block:
        @block.gpsimd
        def _(pool):
            fills = ((ident, 0.0), (neg_tri, -1.0), (neg_suf, -1.0), (neg_one, -1.0), (one, 1.0),
                     (ones_row, 1.0), (mhalf, -0.5), (causal4, 1.0), (neg_mid1, 0.0))
            for tile, value in fills:
                nc.gpsimd.memset(tile[:], value).then_inc(made, 1)
            pool.wait_ge(made, len(fills))
            nc.gpsimd.affine_select(out=ident[:], in_=ident[:], compare_op=ALU.not_equal, fill=1.0, base=0,
                                    pattern=[[-1, P]], channel_multiplier=1).then_inc(ready, 1)
            nc.gpsimd.affine_select(out=neg_tri[:], in_=neg_tri[:], compare_op=ALU.is_ge, fill=0.0, base=0,
                                    pattern=[[1, P]], channel_multiplier=-1).then_inc(ready, 1)
            nc.gpsimd.affine_select(out=neg_suf[:], in_=neg_suf[:], compare_op=ALU.is_gt, fill=0.0, base=0,
                                    pattern=[[-1, P]], channel_multiplier=1).then_inc(ready, 1)
            nc.gpsimd.affine_select(out=causal4[:], in_=causal4[:], compare_op=ALU.is_ge, fill=0.0, base=0,
                                    pattern=[[0, 4], [1, P]], channel_multiplier=-1).then_inc(ready, 1)
            pool.wait_ge(ready, 4)
            nc.gpsimd.tensor_copy(neg_mid0[:], neg_tri[:]).then_inc(made, 1)
            nc.gpsimd.tensor_copy(neg_mid1[:, H:P], neg_tri[:, H:P]).then_inc(made, 1)
            pool.wait_ge(made, len(fills) + 2)
            nc.gpsimd.tensor_scalar(neg_mid0[0:32, :], neg_tri[0:32, :], 1.0, None, ALU.add).then_inc(made, 1)
            for p0, p1 in ((0, 32), (32, 64), (64, 96)):
                nc.gpsimd.tensor_scalar(neg_mid1[p0:p1, H:P], neg_tri[p0:p1, H:P], 1.0, None, ALU.add).then_inc(made, 1)
            pool.wait_ge(made, len(fills) + 6)
            nc.gpsimd.tensor_copy(neg_own[:, 0:H], neg_mid0[:, 0:H]).then_inc(ready, 1)
            nc.gpsimd.tensor_copy(neg_own[:, H:P], neg_mid1[:, H:P]).then_inc(ready, 1)
            pool.wait_ge(ready, 6)
    return c


def ssm_project(nc, sb, pb, sem, c, x_in, xi_dram, abc_dram, w_in_dram, w_abc_dram, fetch):
    ident, mhalf = c["ident"], c["mhalf"]
    w_in = sb("w_in", [P, KD, 2 * DI])
    w_abc = sb("w_abc", [P, KI, 3 * NS])
    x_t = sb("x_t", [P, 2, DM])
    stats = sb("stats", [P, 2, 6])
    mean_var = sb("mean_var", [P, 2, 2])
    var_eps = sb("var_eps", [P, 2])
    rstd = sb("rstd", [P, 2])
    xn = sb("xn", [P, 2, DM])
    xnt = sb("xnt", [P, 2, KD, P])
    sig = sb("sig", [P, 2, 2 * DI])
    gated = sb("gated", [P, 2, DI])
    xi = sb("xi", [P, 2, DI])
    xit = sb("xit", [P, 2, KI, P])
    abc = sb("abc", [P, 2, 3 * NS])
    ps_xnt = [pb(f"ps_xnt{s}", [P, KD, P]) for s in range(2)]
    ps_xz = [pb(f"ps_xz{s}", [P, 2 * DI]) for s in range(2)]
    ps_xit = pb("ps_xit", [P, KI, P])
    ps_abc = pb("ps_abc", [P, 3 * NS])

    w_loaded = sem("a_w_loaded")
    x_loaded = [sem(f"a_x_loaded{s}") for s in range(2)]
    ln_steps, var_ready, rstd_ready, xn_ready = (sem("a_" + n) for n in ("ln_steps", "var_ready", "rstd_ready", "xn_ready"))
    xnt_done, xnt_ready, xz_done, sig_ready = (sem("a_" + n) for n in ("xnt_done", "xnt_ready", "xz_done", "sig_ready"))
    gated_ready, xi_ready, xit_done, xit_ready = (sem("a_" + n) for n in ("gated_ready", "xi_ready", "xit_done", "xit_ready"))
    abc_done, abc_ready = sem("a_abc_done"), sem("a_abc_ready")
    xi_stored = [sem(f"a_xi_stored{s}") for s in range(2)]
    abc_stored = [sem(f"a_abc_stored{s}") for s in range(2)]

    with nc.Block() as block:
        @block.sync
        def _(sp):
            sp.dma_start(w_in[:], w_in_dram.rearrange("(k p) n -> p k n", p=P)).then_inc(w_loaded, 16)
            sp.dma_start(w_abc[:], w_abc_dram.rearrange("(k p) n -> p k n", p=P)).then_inc(w_loaded, 16)

            def load(t, k, s):
                wait(sp, xn_ready, t - 1)
                sp.dma_start(x_t[:, s, :], x_in[bass.ts(t, P), :]).then_inc(x_loaded[s], 16)

            def store_xi(t, k, s):
                wait_apart(sp, c["ready"], (xi_ready, t + 1))
                sp.dma_start(xi_dram[bass.ts(t, P), :], xi[:, s, :]).then_inc(xi_stored[s], 16)

            def store_abc(t, k, s):
                wait_apart(sp, c["ready"], (abc_ready, t + 1))
                sp.dma_start(abc_dram[bass.ts(t, P), :], abc[:, s, :]).then_inc(abc_stored[s], 16)

            pipeline(sp, NT, [load, nothing, nothing, store_xi, nothing, store_abc])
            for s in range(2):
                sp.wait_ge(xi_stored[s], 16 * (NT // 2))
                sp.wait_ge(abc_stored[s], 16 * (NT // 2))

        @block.vector
        def _(dve):
            chain = Chain(dve, ln_steps, 2)

            def norm(t, k, s):
                dve.wait_ge(x_loaded[s], 16 * k + 16)
                chain.at(t)
                chain.step(nc.vector.bn_stats(stats[:, s, :], x_t[:, s, :]))
                wait_apart(dve, c["ready"], (ln_steps, chain.base + chain.k))
                chain.link(nc.vector.bn_aggr(mean_var[:, s, :], stats[:, s, :]))
                nc.vector.tensor_scalar(var_eps[:, s:s + 1], mean_var[:, s, 1:2], LN_EPS, None,
                                        ALU.add).then_inc(var_ready, 1)
                dve.wait_ge(rstd_ready, t + 1)
                wait(dve, xnt_done, t - 1)
                nc.vector.tensor_scalar(xn[:, s, :], x_t[:, s, :], mean_var[:, s, 0:1], rstd[:, s:s + 1],
                                        ALU.subtract, ALU.mult).then_inc(xn_ready, 1)

            def gate(t, k, s):
                dve.wait_ge(sig_ready, t + 1)
                wait(dve, xi_ready, t - 1)
                nc.vector.tensor_tensor(gated[:, s, :], ps_xz[s][:, 0:DI], sig[:, s, 0:DI],
                                        ALU.mult).then_inc(gated_ready, 1)

            pipeline(dve, NT, [norm, nothing, gate])

        @block.gpsimd
        def _(pool):
            def rsqrt(t, k, s):
                pool.wait_ge(var_ready, t + 1)
                nc.gpsimd.tensor_tensor(rstd[:, s:s + 1], var_eps[:, s:s + 1], mhalf[:, 0:1],
                                        ALU.pow).then_inc(rstd_ready, 1)

            def gate(t, k, s):
                pool.wait_ge(gated_ready, t + 1)
                wait(pool, xit_done, t - 1)
                wait(pool, xi_stored[s], 16 * k)
                nc.gpsimd.tensor_tensor(xi[:, s, :], gated[:, s, :], sig[:, s, DI:2 * DI],
                                        ALU.mult).then_inc(xi_ready, 1)

            pipeline(pool, NT, [rsqrt, nothing, gate])

        @block.tensor
        def _(pe):
            pe.wait_ge(w_loaded, 32)

            def transpose_x(t, k, s):
                pe.wait_ge(xn_ready, t + 1)
                wait(pe, xnt_ready, t - 1)
                for j in range(KD):
                    last = nc.tensor.transpose(ps_xnt[s][:, j, :], xn[:, s, j * P:(j + 1) * P], ident[:])
                last.then_inc(xnt_done, 1)

            def project(t, k, s):
                pe.wait_ge(xnt_ready, t + 1)
                wait(pe, gated_ready, t - 1)
                for h in range(2):
                    for j in range(KD):
                        last = nc.tensor.matmul(ps_xz[s][:, h * DI:(h + 1) * DI], xnt[:, s, j, :],
                                                w_in[:, j, h * DI:(h + 1) * DI], start=(j == 0), stop=(j == KD - 1))
                last.then_inc(xz_done, 1)

            def transpose_xi(t, k, s):
                pe.wait_ge(xi_ready, t + 1)
                wait(pe, xit_ready, t)
                for j in range(KI):
                    last = nc.tensor.transpose(ps_xit[:, j, :], xi[:, s, j * P:(j + 1) * P], ident[:])
                last.then_inc(xit_done, 1)

            def states(t, k, s):
                pe.wait_ge(xit_ready, t + 1)
                wait(pe, abc_ready, t)
                for j in range(KI):
                    last = nc.tensor.matmul(ps_abc[:], xit[:, s, j, :], w_abc[:, j, :], start=(j == 0), stop=(j == KI - 1))
                last.then_inc(abc_done, 1)

            pipeline(pe, NT, [nothing, transpose_x, project, transpose_xi, states], order=(1, 2, 4, 3))

        @block.scalar
        def _(act):
            act.wait_ge(x_loaded[1], 16)
            act.wait_ge(w_loaded, 32)
            fetch(act)

            def copy_x(t, k, s):
                act.wait_ge(xnt_done, t + 1)
                wait(act, xz_done, t - 1)
                nc.scalar.activation(xnt[:, s], ps_xnt[s][:], ACT.Copy).then_inc(xnt_ready, 1)

            def gate(t, k, s):
                act.wait_ge(xz_done, t + 1)
                wait(act, xi_ready, t - 1)
                nc.scalar.activation(sig[:, s, :], ps_xz[s][:], ACT.Sigmoid).then_inc(sig_ready, 1)

            def copy_xi(t, k, s):
                act.wait_ge(xit_done, t + 1)
                wait(act, abc_done, t - 1)
                nc.scalar.activation(xit[:, s], ps_xit[:], ACT.Copy).then_inc(xit_ready, 1)

            def copy_abc(t, k, s):
                act.wait_ge(abc_done, t + 1)
                wait(act, abc_stored[s], 16 * k)
                nc.scalar.activation(abc[:, s, :], ps_abc[:], ACT.Copy).then_inc(abc_ready, 1)

            pipeline(act, NT, [nothing, copy_x, gate, copy_xi, copy_abc], order=(1, 2, 4, 3))


def ssm_scan(nc, sb, pb, sem, c, x_in, xi_dram, abc_dram, w_out_dram, norm_w_dram, x1_dram):
    ident, mhalf, one, neg_one, causal4 = c["ident"], c["mhalf"], c["one"], c["neg_one"], c["causal4"]
    B4 = BATCH
    NP = P // B4
    xi = sb("b_xi", [P, 2, B4, DI])
    abc = sb("b_abc", [P, 2, B4, 3 * NS])
    x_t = sb("b_x", [P, 2, B4, DM])
    a_clip = sb("a_clip", [P, B4, NS])
    ea = sb("ea", [P, B4, NP])
    e_inv = sb("e_inv", [P, B4, NS])
    e_all = sb("e_all", [P, 4, B4, NS])
    decay = sb("decay", [P, 2])
    bx = sb("bx", [P, B4, NP])
    diag = {n: sb("diag_" + n, [P, B4 * (P + NP)]) for n in ("c0", "c1", "p")}
    bxt = sb("bxt", [P, P])
    c0t = sb("c0t", [P, B4, P])
    c1t = sb("c1t", [P, B4, H])
    cpt = sb("cpt", [P, 2, B4, P])
    bsm = sb("bsm", [P, 2, B4, NP])
    scores = sb("scores", [P, 2, B4, P])
    state = sb("state", [P, DI])
    ys = sb("ys", [P, 2, KI, P])
    sq = sb("sq", [P, 2, KI, P])
    sq_sum = sb("sq_sum", [P, 2, P])
    ms = sb("ms", [P, 2])
    rms = sb("rms", [P, 2])
    x1 = sb("x1", [P, 2, B4, DM])
    w_out = sb("w_out", [P, KI, DM])
    norm_w = sb("norm_w", [P, KI])
    ps_cum = pb("ps_cum", [P, 5 * B4 * NS + 1])
    ps_s = pb("ps_s", [P, B4, P])
    ps_tr = pb("ps_tr", [P, B4, P])
    ps_y = [pb(f"ps_y{i}", [P, KI, P]) for i in range(2)]
    ps_o = [pb(f"ps_o{i}", [P, DM + 1]) for i in range(2)]
    ps_st = pb("ps_st", [P, DI])

    w_loaded, w_steps, zeroed = sem("b_w_loaded"), sem("b_w_steps"), sem("b_zeroed")
    loaded = [sem(f"b_loaded{s}") for s in range(2)]
    (clipped, ea_ready, cum_done, exps_ready, bx_ready, bxt_done, bxt_ready, c0t_done, c0t_ready, c1t_done, c1t_ready, cpt_done,
     cpt_ready, s_done, scores_ready, y_done, ys_ready, sq_ready, sq_summed, o_done, ms_ready, rms_ready, x1_ready,
     st_done, state_ready) = (sem("b_" + n) for n in (
        "clipped", "ea_ready", "cum_done", "exps_ready", "bx_ready", "bxt_done", "bxt_ready", "c0t_done",
        "c0t_ready", "c1t_done", "c1t_ready", "cpt_done", "cpt_ready", "s_done", "scores_ready", "y_done", "ys_ready", "sq_ready", "sq_summed",
        "o_done", "ms_ready", "rms_ready", "x1_ready", "st_done", "state_ready"))
    stored = [sem(f"b_stored{s}") for s in range(2)]
    S4 = B4 * NS
    W = P + NP

    def own(tile):
        return tile.rearrange("p (b w) -> p b w", w=W)[:, :, 0:NS]

    def masked(tile, b):
        return tile[:, b * P:(b + 1) * P]

    with nc.Block() as block:
        @block.sync
        def _(sp):
            sp.dma_start(w_out[:], w_out_dram.rearrange("(k p) n -> p k n", p=P)).then_inc(w_loaded, 16)
            sp.dma_start(norm_w[:], norm_w_dram).then_inc(w_loaded, 16)

            def chunk(dram, ch):
                return dram.rearrange("(b t) n -> t b n", b=B4)[bass.ts(ch, P)]

            def load(ch, k, s):
                wait_apart(sp, c["ready"], (st_done, ch - 1), (x1_ready, B4 * (ch - 1)))
                sp.dma_start(xi[:, s], chunk(xi_dram, ch)).then_inc(loaded[s], 16)
                sp.dma_start(abc[:, s], chunk(abc_dram, ch)).then_inc(loaded[s], 16)
                sp.dma_start(x_t[:, s], chunk(x_in, ch)).then_inc(loaded[s], 16)

            def store(ch, k, s):
                wait_apart(sp, c["ready"], (x1_ready, B4 * (ch + 1)))
                sp.dma_start(chunk(x1_dram, ch), x1[:, s]).then_inc(stored[s], 16)

            pipeline(sp, TPB, [load, nothing, store])
            for s in range(2):
                sp.wait_ge(stored[s], 16 * (TPB // 2))

        @block.gpsimd
        def _(pool):
            nc.gpsimd.memset(ea[:], 0.0).then_inc(zeroed, 1)
            nc.gpsimd.memset(bx[:], 0.0).then_inc(zeroed, 1)
            nc.gpsimd.memset(diag["c0"][:], 0.0).then_inc(zeroed, 1)
            nc.gpsimd.memset(diag["c1"][:], 0.0).then_inc(zeroed, 1)
            nc.gpsimd.memset(diag["p"][:], 0.0).then_inc(zeroed, 1)
            nc.gpsimd.memset(bsm[:], 0.0).then_inc(zeroed, 1)
            nc.gpsimd.memset(scores[:], 0.0).then_inc(zeroed, 1)
            nc.gpsimd.memset(state[:], 0.0).then_inc(zeroed, 1)

            def rsqrt(ch, k, s):
                for b in range(B4):
                    pool.wait_ge(ms_ready, B4 * ch + b + 1)
                    nc.gpsimd.tensor_tensor(rms[:, b % 2:b % 2 + 1], ms[:, b % 2:b % 2 + 1], mhalf[:, 0:1],
                                            ALU.pow).then_inc(rms_ready, 1)

            pipeline(pool, TPB, [nothing, rsqrt])

        @block.vector
        def _(dve):
            dve.wait_ge(zeroed, 8)
            dve.wait_ge(w_loaded, 32)
            for j in range(KI):
                nc.vector.tensor_scalar(w_out[:, j, :], w_out[:, j, :], norm_w[:, j:j + 1], None,
                                        ALU.mult).then_inc(w_steps, 1)

            def clip(ch, k, s):
                dve.wait_ge(loaded[s], 48 * k + 48)
                wait(dve, ea_ready, ch)
                nc.vector.tensor_scalar(a_clip[:], abc[:, s, :, 0:NS], -5.0, 0.0, ALU.max,
                                        ALU.min).then_inc(clipped, 1)

            def operands(ch, k, s):
                dve.wait_ge(exps_ready, 3 * ch + 2)
                b_part, c_part = abc[:, s, :, NS:2 * NS], abc[:, s, :, 2 * NS:3 * NS]

                wait(dve, bxt_done, ch)
                nc.vector.tensor_tensor(bx[:, :, 0:NS], b_part, e_inv[:], ALU.mult).then_inc(bx_ready, 1)
                wait(dve, cpt_done, ch)
                for i, n in ((0, "c0"), (1, "c1"), (3, "p")):
                    nc.vector.tensor_tensor(own(diag[n][:]), c_part, e_all[:, i], ALU.mult).then_inc(bx_ready, 1)
                wait(dve, st_done, ch - 1)
                nc.vector.tensor_tensor(bsm[:, s, :, 0:NS], b_part, e_all[:, 2], ALU.mult).then_inc(bx_ready, 1)

            def keep_scores(ch, k, s):
                wait_apart(dve, c["ready"], (s_done, ch + 1))
                nc.vector.copy_predicated(scores[0:H, s], causal4[0:H].bitcast(U32), ps_s[0:H]).then_inc(scores_ready, 1)
                nc.vector.copy_predicated(scores[H:P, s, :, H:P], causal4[H:P, :, H:P].bitcast(U32),
                                          ps_s[H:P, :, H:P]).then_inc(scores_ready, 1)

            def copy_cpt(ch, k, s):
                dve.wait_ge(cpt_done, ch + 1)
                wait(dve, st_done, ch - 1)
                nc.vector.tensor_copy(cpt[:, s], ps_tr[:]).then_inc(cpt_ready, 1)

            def take(b):
                def step(ch, k, s):
                    n = B4 * ch + b
                    dve.wait_ge(y_done, n + 1)
                    wait(dve, o_done, n - 1)
                    nc.vector.tensor_copy(ys[:, b % 2], ps_y[b % 2][:]).then_inc(ys_ready, 1)
                return step

            def sum_squares(b):
                def step(ch, k, s):
                    n = B4 * ch + b
                    dve.wait_ge(sq_ready, n + 1)
                    wait(dve, o_done, n - 1)
                    nc.vector.reduce_sum(sq_sum[:, b % 2, :], sq[:, b % 2].rearrange("p j t -> p t j"), AXX).then_inc(sq_summed, 1)
                return step

            def finish(b):
                def step(ch, k, s):
                    n = B4 * ch + b
                    i = b % 2
                    dve.wait_ge(o_done, n + 1)
                    wait(dve, rms_ready, n - 1)
                    nc.vector.tensor_scalar(ms[:, i:i + 1], ps_o[i][:, DM:DM + 1], 1.0 / DI, RMS_EPS, ALU.mult,
                                            ALU.add).then_inc(ms_ready, 1)
                    dve.wait_ge(rms_ready, n + 1)
                    wait(dve, stored[s], 16 * k)
                    nc.vector.scalar_tensor_tensor(out=x1[:, s, b, :], in0=ps_o[i][:, 0:DM], scalar=rms[:, i:i + 1],
                                                   in1=x_t[:, s, b, :], op0=ALU.mult, op1=ALU.add).then_inc(x1_ready, 1)
                return step

            def update_state(ch, k, s):
                dve.wait_ge(st_done, ch + 1)
                nc.vector.scalar_tensor_tensor(out=state[:], in0=state[:], scalar=decay[:, s:s + 1], in1=ps_st[:],
                                               op0=ALU.mult, op1=ALU.add).then_inc(state_ready, 1)

            interleaved(dve, TPB, [(0, clip), (1, take(0)), (1, sum_squares(0)), (0, operands), (1, take(1)), (1, sum_squares(1)),
                                   (1, finish(0)), (1, take(2)), (1, sum_squares(2)), (1, finish(1)), (0, keep_scores),
                                   (1, take(3)), (1, sum_squares(3)), (0, copy_cpt), (1, update_state), (1, finish(2)), (1, finish(3))])

        @block.scalar
        def _(act):
            act.wait_ge(zeroed, 2)

            def exp_a(ch, k, s):
                act.wait_ge(clipped, ch + 1)
                wait(act, cum_done, ch)
                nc.scalar.activation(ea[:, :, 0:NS], a_clip[:], ACT.Exp).then_inc(ea_ready, 1)

            def exp_sums(ch, k, s):
                act.wait_ge(cum_done, ch + 1)
                wait(act, bx_ready, 5 * ch)
                wait(act, state_ready, ch - 1)
                nc.scalar.activation(e_inv[:].rearrange("p b n -> p (b n)"), ps_cum[:, 0:S4], ACT.Exp,
                                     scale=-1.0).then_inc(exps_ready, 1)
                nc.scalar.activation(e_all[:].rearrange("p i b n -> p (i b n)"), ps_cum[:, S4:5 * S4],
                                     ACT.Exp).then_inc(exps_ready, 1)
                nc.scalar.activation(decay[:, s:s + 1], ps_cum[:, 5 * S4:5 * S4 + 1], ACT.Exp).then_inc(exps_ready, 1)

            def copy_bxt(ch, k, s):
                act.wait_ge(bxt_done, ch + 1)
                wait(act, s_done, ch)
                nc.scalar.activation(bxt[:], ps_s[:, 0, :], ACT.Copy).then_inc(bxt_ready, 1)

            def copy_c0t(ch, k, s):
                act.wait_ge(c0t_done, ch + 1)
                nc.scalar.activation(c0t[:], ps_tr[:], ACT.Copy).then_inc(c0t_ready, 1)

            def copy_c1t(ch, k, s):
                act.wait_ge(c1t_done, ch + 1)
                nc.scalar.activation(c1t[:], ps_tr[:, :, H:P], ACT.Copy).then_inc(c1t_ready, 1)

            def square(b):
                def step(ch, k, s):
                    n = B4 * ch + b
                    act.wait_ge(ys_ready, n + 1)
                    wait(act, sq_summed, n - 1)
                    nc.scalar.activation(sq[:, b % 2], ys[:, b % 2], ACT.Square).then_inc(sq_ready, 1)
                return step

            interleaved(act, TPB, [(0, exp_a), (0, exp_sums), (1, square(0)), (0, copy_bxt), (1, square(1)), (0, copy_c0t),
                                   (1, square(2)), (0, copy_c1t), (1, square(3))])

        @block.tensor
        def _(pe):
            pe.wait_ge(w_steps, KI)
            pe.wait_ge(zeroed, 8)

            def cumulate(ch, k, s):
                pe.wait_ge(ea_ready, ch + 1)
                wait(pe, exps_ready, 3 * ch)
                for i, m in enumerate(("neg_own", "neg_mid0", "neg_mid1", "neg_suf", "neg_tri")):
                    nc.tensor.matmul(ps_cum[:, i * S4:(i + 1) * S4], c[m][:], ea[:, :, 0:NS], start=True, stop=True)
                nc.tensor.matmul(ps_cum[:, 5 * S4:5 * S4 + 1], ea[:].rearrange("p b n -> p (b n)"), neg_one[:],
                                 start=True, stop=True).then_inc(cum_done, 1)

            def transpose_bx(ch, k, s):
                pe.wait_ge(bx_ready, 5 * ch + 1)
                wait(pe, scores_ready, 2 * ch)
                nc.tensor.transpose(ps_s[:, 0, :], bx[:].rearrange("p b n -> p (b n)"), ident[:]).then_inc(bxt_done, 1)

            def transpose_c0(ch, k, s):
                pe.wait_ge(bx_ready, 5 * ch + 4)
                wait(pe, cpt_ready, ch)
                for b in range(B4):
                    last = nc.tensor.transpose(ps_tr[:, b, :], masked(diag["c0"], b), ident[:])
                last.then_inc(c0t_done, 1)

            def transpose_c1(ch, k, s):
                pe.wait_ge(c0t_ready, ch + 1)
                for b in range(B4):
                    last = nc.tensor.transpose(ps_tr[:, b, :], masked(diag["c1"], b), ident[:])
                last.then_inc(c1t_done, 1)

            def score(ch, k, s):
                pe.wait_ge(bxt_ready, ch + 1)
                nc.tensor.matmul(ps_s[0:H], bxt[:, 0:H], c0t[:], start=True, stop=True)
                pe.wait_ge(c1t_ready, ch + 1)
                nc.tensor.matmul(ps_s[H:P, :, H:P], bxt[:, H:P], c1t[:], start=True, stop=True).then_inc(s_done, 1)

            def transpose_cp(ch, k, s):
                for b in range(B4):
                    last = nc.tensor.transpose(ps_tr[:, b, :], masked(diag["p"], b), ident[:])
                last.then_inc(cpt_done, 1)

            def scan(b):
                def step(ch, k, s):
                    if b == 0:
                        pe.wait_ge(scores_ready, 2 * ch + 2)
                        pe.wait_ge(cpt_ready, ch + 1)
                        wait(pe, state_ready, ch)
                    wait(pe, ys_ready, B4 * ch + b - 1)
                    for j in range(KI):
                        d = slice(j * P, (j + 1) * P)
                        nc.tensor.matmul(ps_y[b % 2][:, j, :], xi[:, s, b, d], scores[:, s, b, :], start=True, stop=False)
                        last = nc.tensor.matmul(ps_y[b % 2][:, j, :], state[:, d], cpt[:, s, b, :], start=False, stop=True)
                    last.then_inc(y_done, 1)
                return step

            def project(b):
                def step(ch, k, s):
                    i = b % 2
                    pe.wait_ge(ys_ready, B4 * ch + b + 1)
                    wait(pe, x1_ready, B4 * ch + b - 1)
                    for j in range(KI):
                        nc.tensor.matmul(ps_o[i][:, 0:DM], ys[:, i, j, :], w_out[:, j, :], start=(j == 0), stop=(j == KI - 1))
                    pe.wait_ge(sq_summed, B4 * ch + b + 1)
                    nc.tensor.matmul(ps_o[i][:, DM:DM + 1], sq_sum[:, i, :], one[:], start=True, stop=True).then_inc(o_done, 1)
                return step

            def new_state(ch, k, s):
                for b in range(B4):
                    last = nc.tensor.matmul(ps_st[b * NP:(b + 1) * NP, :], bsm[:, s, b, :], xi[:, s, b, :], start=True, stop=True)
                last.then_inc(st_done, 1)

            interleaved(pe, TPB, [(0, cumulate), (1, scan(0)), (1, scan(1)), (0, transpose_bx), (1, project(0)), (0, transpose_c0),
                                  (1, scan(2)), (0, transpose_c1), (1, project(1)), (0, score), (1, scan(3)), (0, transpose_cp),
                                  (1, new_state), (1, project(2)), (1, project(3))])


CAP = TOK + P


G = 2
NG = NT // G


def route(nc, sb, pb, sem, c, name, E, x_dram, xn_dram, gathered, w_gate_dram, gate_b_dram, kept, attn=None):
    ident, mhalf, ones_row = c["ident"], c["mhalf"], c["ones_row"]
    pos_all, prob_all, tile_list = kept["pos"], kept["prob"], kept["tiles"]
    n_list = 2 * NT + E
    biased = gate_b_dram is not None
    w_gate = sb(name + "w_gate", [P, KD, E])
    gate_b = sb(name + "gate_b", [1, E])
    x_t = sb(name + "x_t", [P, 2, G, DM])
    stats = sb(name + "stats", [P, G, 6])
    mean_var = sb(name + "mean_var", [P, G, 2])
    var_eps = sb(name + "var_eps", [P, G])
    rstd = sb(name + "rstd", [P, G])
    xn = sb(name + "xn", [P, 2, G, DM])
    xs = sb(name + "xs", [P, 2, G, DM])
    xnt = sb(name + "xnt", [P, KD, G * P])
    top = sb(name + "top", [P, G])
    shifted = sb(name + "shifted", [P, G, E])
    expd = sb(name + "expd", [P, G, E])
    total = sb(name + "total", [P, G])
    inv = sb(name + "inv", [P, G])
    probs = sb(name + "probs", [P, G, E])
    best = sb(name + "best", [P, G, 8])
    best_at = sb(name + "best_at", [P, G, 8], U32)
    best_f = sb(name + "best_f", [P, G, 2])
    hot = sb(name + "hot", [P, 2, G, 2, E])
    both = sb(name + "both", [P, 2, G, E], BF16)
    free_row = sb(name + "free_row", [P, E])
    row = sb(name + "row", [P, G, E])
    hot_row = sb(name + "hot_row", [P, G, 2, E])
    pos_f = sb(name + "pos_f", [P, G, 2])
    pos = sb(name + "pos", [P, 2, G, 2], U32)
    experts = sb(name + "experts", [P, E])
    zeros = sb(name + "zeros", [P, DM])
    before = sb(name + "before", [P, P], BF16)
    all_ones = sb(name + "all_ones", [P, P], BF16)
    region = sb(name + "region", [P, E])
    count = sb(name + "count", [P, E])
    count_i = sb(name + "count_i", [P, E], U32)
    n_tiles = sb(name + "n_tiles", [P, E])
    one_e = sb(name + "one_e", [P, E])
    end = sb(name + "end", [P, E])
    moved = sb(name + "moved", [P, E])
    best_all = sb(name + "best_all", [P, NT, 2])
    pos_f_all = sb(name + "pos_f_all", [P, NT, 2])
    hot_all = sb(name + "hot_all", [P, 2 * NT, E])
    shift = sb(name + "shift", [P, NT, 2])
    index = sb(name + "index", [1, n_list])
    passed = sb(name + "passed", [1, n_list, E])
    passed_n = sb(name + "passed_n", [1, n_list, E])
    which = sb(name + "which", [1, n_list])
    start = sb(name + "start", [1, n_list])
    first_row = sb(name + "first_row", [1, n_list])
    pad_row = sb(name + "pad_row", [1, E], U32)
    if attn:
        headst_dram, inv_dram, wo_dram, res_dram, sum_dram = attn
        w_o = sb(name + "w_o", [P, KD, DM])
        headst = sb(name + "headst", [P, 2, KD, G * P])
        inv_t = sb(name + "inv_t", [P, 2, KD, G * P])
        scaled = sb(name + "scaled", [P, 2, KD, G * P])
        res = sb(name + "res", [P, 2, G, DM])
        ps_wo = pb(name + "ps_wo", [P, G, DM])
    ps_xnt = pb(name + "ps_xnt", [P, KD, G * P])
    ps_logits = pb(name + "ps_logits", [P, G, E])
    ps_rank = pb(name + "ps_rank", [P, G + 1, E])

    w_loaded, set_up = sem(name + "w_loaded"), sem(name + "set_up")
    x_loaded = [sem(f"{name}x_loaded{s}") for s in range(2)]
    (scaled_ready, wo_done, x_ready, ln_steps, var_ready, rstd_ready, xn_ready, xnt_done, xnt_ready,
     logits_done, shifted_ready, exp_ready, top_steps, both_ready, rank_done, row_ready, place_steps, pos_ready,
     kept_ready, xs_ready, list_steps, list_ready) = (sem(name + n) for n in (
        "scaled_ready", "wo_done", "x_ready", "ln_steps", "var_ready", "rstd_ready", "xn_ready",
        "xnt_done", "xnt_ready", "logits_done", "shifted_ready", "exp_ready", "top_steps", "both_ready", "rank_done",
        "row_ready", "place_steps", "pos_ready", "kept_ready", "xs_ready", "list_steps", "list_ready"))
    x_stored = [sem(f"{name}x_stored{s}") for s in range(2)]
    xn_stored = [sem(f"{name}xn_stored{s}") for s in range(2)]
    scattered = c["moved"][name + "scattered"]
    padded = sem(name + "padded")

    def rows(dram, g):
        return dram[bass.ts(g, G * P), :].rearrange("(j p) n -> p j n", p=P)

    with nc.Block() as block:
        @block.sync
        def _(sp):
            sp.dma_start(w_gate[:], w_gate_dram.rearrange("(k p) n -> p k n", p=P)).then_inc(w_loaded, 16)
            if biased:
                sp.dma_start(gate_b[:], gate_b_dram).then_inc(w_loaded, 16)
            if attn:
                sp.dma_start(w_o[:], wo_dram.rearrange("(k p) n -> p k n", p=P)).then_inc(w_loaded, 16)

            def load(g, k, s):
                wait_apart(sp, c["ready"], (xn_ready, g - 1))
                if attn:
                    for kd in range(KD):
                        sp.dma_start(inv_t[:, s, kd, :], inv_dram[kd * (P // HD):(kd + 1) * (P // HD), bass.ts(g, G * P)]
                                     .unsqueeze(1).broadcast_to([P // HD, HD, G * P])).then_inc(x_loaded[s], 16)
                    sp.dma_start(headst[:, s], headst_dram[:, bass.ts(g, G * P)].rearrange("(k p) t -> p k t", p=P)).then_inc(x_loaded[s], 16)
                    sp.dma_start(res[:, s], rows(res_dram, g)).then_inc(x_loaded[s], 16)
                else:
                    sp.dma_start(x_t[:, s], rows(x_dram, g)).then_inc(x_loaded[s], 16)

            def store(g, k, s):
                if attn:
                    wait_apart(sp, c["ready"], (x_ready, g + 1), (xn_ready, g + 1))
                    sp.dma_start(rows(sum_dram, g), x_t[:, s]).then_inc(x_stored[s], 16)
                    sp.dma_start(rows(xn_dram, g), xn[:, s]).then_inc(xn_stored[s], 16)

            pipeline(sp, NG, [load, nothing, store])
            if attn:
                for s in range(2):
                    sp.wait_ge(x_stored[s], 16 * (NG // 2))
                    sp.wait_ge(xn_stored[s], 16 * (NG // 2))
            sp.wait_ge(set_up, 9)
            for e in range(E):
                sp.dma_start(gathered[E * CAP + e * P:E * CAP + (e + 1) * P, :], zeros[:]).then_inc(padded, 16)
            sp.wait_ge(list_ready, 1)
            for e in range(E):
                at = sp.value_load(pad_row[0:1, e:e + 1], min_val=e * CAP, max_val=e * CAP + TOK)
                sp.dma_start(gathered[bass.ds(at, P), :], zeros[:]).then_inc(padded, 16)
            sp.wait_ge(padded, 32 * E)

        @block.gpsimd
        def _(pool):
            for tile, value in ((zeros, 0.0), (one_e, 1.0), (before, 1.0), (all_ones, 1.0)):
                nc.gpsimd.memset(tile[:], value).then_inc(set_up, 1)
            for tile, step, n in ((experts, 1, E), (free_row, CAP, E), (region, CAP, E), (index, 1, n_list)):
                nc.gpsimd.iota(tile[:], pattern=[[step, n]], base=0, channel_multiplier=0,
                               allow_small_or_imprecise_dtypes=True).then_inc(set_up, 1)
            pool.wait_ge(set_up, 8)
            nc.gpsimd.affine_select(out=before[:], in_=before[:], compare_op=ALU.is_gt, fill=0.0, base=0,
                                    pattern=[[1, P]], channel_multiplier=-1).then_inc(set_up, 1)

            def rsqrt(g, k, s):
                pool.wait_ge(var_ready, g + 1)
                nc.gpsimd.tensor_tensor(rstd[:], var_eps[:], mhalf[:, 0:G], ALU.pow).then_inc(rstd_ready, 1)

            def scatter(g, k, s):
                wait_apart(pool, c["ready"], (pos_ready, g + 1), (xs_ready, g + 1))
                for j in range(G):
                    for i in range(2):
                        nc.gpsimd.indirect_dma_start(
                            out=gathered[:, :], out_offset=bass.IndirectOffsetOnAxis(ap=pos[:, s, j, i:i + 1], axis=0),
                            in_=xs[:, s, j, :], in_offset=None).then_inc(scattered[s], 16)

            pipeline(pool, NG, [nothing, nothing, rsqrt, nothing, nothing, scatter])
            for s in range(2):
                pool.wait_ge(scattered[s], 32 * G * (NG // 2))

        @block.vector
        def _(dve):
            norm_chain = Chain(dve, ln_steps, 2 * G)
            top_chain = Chain(dve, top_steps, 2 * G + 6)
            place_chain = Chain(dve, place_steps, 2)

            def scale(g, k, s):
                if attn:
                    dve.wait_ge(x_loaded[s], 64 * k + 64)
                    wait(dve, wo_done, g - 1)
                    nc.vector.tensor_tensor(scaled[:, s], headst[:, s], inv_t[:, s], ALU.mult).then_inc(scaled_ready, 1)

            def normalise(g, k, s):
                if attn:
                    dve.wait_ge(wo_done, g + 1)
                    wait(dve, x_stored[s], 16 * k)
                    nc.vector.tensor_tensor(x_t[:, s], res[:, s], ps_wo[:], ALU.add).then_inc(x_ready, 1)
                    dve.wait_ge(x_ready, g + 1)
                else:
                    dve.wait_ge(x_loaded[s], 16 * k + 16)
                norm_chain.at(g)
                for j in range(G):
                    norm_chain.step(nc.vector.bn_stats(stats[:, j, :], x_t[:, s, j, :]))
                wait_apart(dve, c["ready"], (ln_steps, norm_chain.base + norm_chain.k))
                for j in range(G):
                    norm_chain.step(nc.vector.bn_aggr(mean_var[:, j, :], stats[:, j, :]))
                norm_chain.wait()
                nc.vector.tensor_scalar(var_eps[:], mean_var[:, :, 1], LN_EPS, None, ALU.add).then_inc(var_ready, 1)
                dve.wait_ge(rstd_ready, g + 1)
                wait(dve, xs_ready, g - 1)
                if xn_dram is not None:
                    wait(dve, xn_stored[s], 16 * k)
                for j in range(G):
                    last = nc.vector.tensor_scalar(xn[:, s, j, :], x_t[:, s, j, :], mean_var[:, j, 0:1], rstd[:, j:j + 1],
                                                   ALU.subtract, ALU.mult)
                last.then_inc(xn_ready, 1)

            def choose(g, k, s):
                top_chain.at(g)
                dve.wait_ge(logits_done, g + 1)
                top_chain.link(nc.vector.reduce_max(top[:], ps_logits[:], AXX))
                nc.vector.tensor_tensor(shifted[:], ps_logits[:], top[:].unsqueeze(2).broadcast_to([P, G, E]),
                                        ALU.subtract).then_inc(shifted_ready, 1)
                dve.wait_ge(exp_ready, g + 1)
                top_chain.link(nc.vector.reduce_sum(total[:], expd[:], AXX))
                top_chain.link(nc.vector.reciprocal(inv[:], total[:]))
                top_chain.step(nc.vector.tensor_tensor(probs[:], expd[:], inv[:].unsqueeze(2).broadcast_to([P, G, E]), ALU.mult))
                wait_apart(dve, c["ready"], (top_steps, top_chain.base + top_chain.k))
                for j in range(G):
                    top_chain.step(nc.vector.max(best[:, j, :], probs[:, j, :]))
                wait_apart(dve, c["ready"], (top_steps, top_chain.base + top_chain.k))
                for j in range(G):
                    top_chain.step(nc.vector.max_index(best_at[:, j, :], best[:, j, :], probs[:, j, :]))
                top_chain.wait()
                top_chain.link(nc.vector.tensor_copy(best_f[:], best_at[:, :, 0:2]))
                nc.vector.tensor_copy(prob_all[:, bass.ts(g, G), :], best[:, :, 0:2]).then_inc(kept_ready, 1)
                nc.vector.tensor_copy(best_all[:, bass.ts(g, G), :], best_f[:]).then_inc(kept_ready, 1)
                top_chain.link(nc.vector.tensor_tensor(hot[:, s].rearrange("p j i e -> p (j i) e"),
                                                       experts[:].unsqueeze(1).broadcast_to([P, 2 * G, E]),
                                                       best_f[:].rearrange("p j i -> p (j i)").unsqueeze(2).broadcast_to([P, 2 * G, E]),
                                                       ALU.is_equal))
                nc.vector.tensor_tensor(both[:, s], hot[:, s, :, 0, :], hot[:, s, :, 1, :], ALU.add).then_inc(both_ready, 1)

            def place(g, k, s):
                place_chain.at(g)
                dve.wait_ge(rank_done, g + 1)
                wait(dve, row_ready, 2 * g)
                nc.vector.tensor_tensor(row[:], free_row[:].unsqueeze(1).broadcast_to([P, G, E]), ps_rank[:, 0:G, :],
                                        ALU.add).then_inc(row_ready, 1)
                dve.wait_ge(row_ready, 2 * g + 1)
                nc.vector.tensor_tensor(free_row[:], free_row[:], ps_rank[:, G, :], ALU.add).then_inc(row_ready, 1)
                place_chain.link(nc.vector.tensor_tensor(hot_row[:], hot[:, s], row[:].unsqueeze(2).broadcast_to([P, G, 2, E]), ALU.mult))
                place_chain.link(nc.vector.reduce_sum(pos_f[:], hot_row[:], AXX))
                wait(dve, scattered[s], 32 * G * k)
                nc.vector.tensor_copy(pos[:, s], pos_f[:]).then_inc(pos_ready, 1)
                nc.vector.tensor_copy(pos_f_all[:, bass.ts(g, G), :], pos_f[:]).then_inc(kept_ready, 1)

            dve.wait_ge(set_up, 9)
            pipeline(dve, NG, [nothing, scale, normalise, nothing, choose, place], order=(5, 4, 2, 1))

            chain = Chain(dve, list_steps, 19)
            chain.at(0)
            dve.wait_ge(row_ready, 2 * NG)
            dve.wait_ge(kept_ready, 3 * NG)
            nc.vector.tensor_copy(pad_row[:], free_row[0:1, :]).then_inc(list_ready, 1)
            chain.link(nc.vector.tensor_tensor(count[:], free_row[:], region[:], ALU.subtract))
            chain.link(nc.vector.tensor_scalar(count_i[:], count[:], float(P - 1), None, ALU.add))
            chain.link(nc.vector.tensor_scalar(count_i[:], count_i[:], P.bit_length() - 1, None, ALU.logical_shift_right))
            chain.link(nc.vector.tensor_copy(n_tiles[:], count_i[:]))
            chain.link(nc.vector.tensor_tensor_scan(end[:], one_e[:], n_tiles[:], 0.0, ALU.mult, ALU.add))
            chain.link(nc.vector.tensor_tensor(passed[:], index[:].unsqueeze(2).broadcast_to([1, n_list, E]),
                                               end[0:1].unsqueeze(1).broadcast_to([1, n_list, E]), ALU.is_ge))
            chain.link(nc.vector.reduce_sum(which[:], passed[:], AXX))
            chain.link(nc.vector.tensor_tensor(passed_n[:], passed[:], n_tiles[0:1].unsqueeze(1).broadcast_to([1, n_list, E]), ALU.mult))
            chain.link(nc.vector.reduce_sum(start[:], passed_n[:], AXX))
            chain.link(nc.vector.tensor_tensor(start[:], index[:], start[:], ALU.subtract))
            chain.link(nc.vector.tensor_scalar(start[:], start[:], float(P), None, ALU.mult))
            chain.link(nc.vector.scalar_tensor_tensor(out=first_row[:], in0=which[:], scalar=float(CAP), in1=start[:],
                                                      op0=ALU.mult, op1=ALU.add))
            nc.vector.tensor_scalar(tile_list[0:1, 0, :], which[:], float(E - 1), None, ALU.min).then_inc(list_ready, 1)
            nc.vector.tensor_copy(tile_list[0:1, 1, :], first_row[:]).then_inc(list_ready, 1)
            chain.link(nc.vector.tensor_tensor(moved[:], end[:], n_tiles[:], ALU.subtract))
            chain.link(nc.vector.tensor_scalar(moved[:], moved[:], float(P), None, ALU.mult))
            chain.link(nc.vector.tensor_tensor(moved[:], moved[:], region[:], ALU.subtract))
            chain.link(nc.vector.tensor_tensor(hot_all[:], experts[:].unsqueeze(1).broadcast_to([P, 2 * NT, E]),
                                               best_all[:].rearrange("p t i -> p (t i)").unsqueeze(2).broadcast_to([P, 2 * NT, E]),
                                               ALU.is_equal))
            chain.link(nc.vector.tensor_tensor(hot_all[:], hot_all[:], moved[:].unsqueeze(1).broadcast_to([P, 2 * NT, E]), ALU.mult))
            chain.link(nc.vector.reduce_sum(shift[:].rearrange("p t i -> p (t i)"), hot_all[:], AXX))
            chain.link(nc.vector.tensor_tensor(shift[:], shift[:], pos_f_all[:], ALU.add))
            nc.vector.tensor_copy(pos_all[:], shift[:]).then_inc(list_ready, 1)
            dve.wait_ge(list_ready, 4)

        @block.tensor
        def _(pe):
            pe.wait_ge(set_up, 9)
            pe.wait_ge(w_loaded, 16 * (1 + biased + (attn is not None)))

            def attend(g, k, s):
                if attn:
                    pe.wait_ge(scaled_ready, g + 1)
                    wait(pe, x_ready, g)
                    for j in range(G):
                        for kd in range(KD):
                            last = nc.tensor.matmul(ps_wo[:, j, :], scaled[:, s, kd, j * P:(j + 1) * P], w_o[:, kd, :],
                                                    start=(kd == 0), stop=(kd == KD - 1))
                    last.then_inc(wo_done, 1)

            def gate(g, k, s):
                pe.wait_ge(xn_ready, g + 1)
                wait(pe, xnt_ready, g)
                for kd in range(KD):
                    for j in range(G):
                        last = nc.tensor.transpose(ps_xnt[:, kd, j * P:(j + 1) * P], xn[:, s, j, kd * P:(kd + 1) * P], ident[:])
                last.then_inc(xnt_done, 1)
                pe.wait_ge(xnt_ready, g + 1)
                wait(pe, shifted_ready, g)
                for j in range(G):
                    for kd in range(KD):
                        last = nc.tensor.matmul(ps_logits[:, j, :], xnt[:, kd, j * P:(j + 1) * P], w_gate[:, kd, :],
                                                start=(kd == 0), stop=(kd == KD - 1 and not biased))
                    if biased:
                        last = nc.tensor.matmul(ps_logits[:, j, :], ones_row[:], gate_b[:], start=False, stop=True)
                last.then_inc(logits_done, 1)

            def rank(g, k, s):
                pe.wait_ge(both_ready, g + 1)
                wait(pe, row_ready, 2 * g)
                for j in range(G + 1):
                    for i in range(min(j + 1, G)):
                        last = nc.tensor.matmul(ps_rank[:, j, :], before[:] if i == j else all_ones[:], both[:, s, i, :],
                                                start=(i == 0), stop=(i == min(j, G - 1)))
                last.then_inc(rank_done, 1)

            pipeline(pe, NG, [nothing, attend, nothing, gate, rank], order=(3, 4, 1))

        @block.scalar
        def _(act):
            def gate(g, k, s):
                act.wait_ge(xnt_done, g + 1)
                wait(act, logits_done, g)
                nc.scalar.activation(xnt[:], ps_xnt[:], ACT.Copy).then_inc(xnt_ready, 1)

            def soften(g, k, s):
                act.wait_ge(shifted_ready, g + 1)
                nc.scalar.activation(expd[:], shifted[:], ACT.Exp).then_inc(exp_ready, 1)
                wait(act, scattered[s], 32 * G * k)
                nc.scalar.activation(xs[:, s], xn[:, s], ACT.Copy).then_inc(xs_ready, 1)

            pipeline(act, NG, [nothing, nothing, nothing, gate, soften], order=(4, 3))


RING = 4


def run_experts(nc, sb, pb, sem, c, name, E, gathered, outputs, kept, up, down, weights):
    ident = c["ident"]
    n_list = 2 * NT + E
    width, w_up, b_up = up
    blocks, w_down, b_down = down
    hidden = blocks * P
    relu = b_up is not None
    tiles = kept["tiles"]
    x_t = sb(name + "x_t", [P, RING, DM])
    xt = sb(name + "xt", [P, 2, KD, P])
    h = sb(name + "h", [P, 2, hidden])
    ht = sb(name + "ht", [P, 2, blocks, P])
    y = sb(name + "y", [P, RING, DM])
    if not relu:
        sig = sb(name + "sig", [P, 2, hidden])
        act_g = sb(name + "act_g", [P, 2, hidden])
    ps_x = pb(name + "ps_x", [P, KD, P])
    ps_h = [pb(f"{name}ps_h{s}", [P, width]) for s in range(2)]
    ps_ht = pb(name + "ps_ht", [P, blocks, P])
    ps_y = pb(name + "ps_y", [P, DM])
    x_loaded = [sem(f"{name}x_loaded{s}") for s in range(RING)]
    stored = [sem(f"{name}stored{s}") for s in range(RING)]
    xt_done, xt_ready, h_done, sig_ready, gated, h_ready, ht_done, ht_ready, y_done, y_ready = (sem(name + n) for n in (
        "xt_done", "xt_ready", "h_done", "sig_ready", "gated", "h_ready", "ht_done", "ht_ready", "y_done", "y_ready"))

    def entry(eng, t, what, top):
        return eng.value_load(tiles[0:1, what, bass.ds(t, 1)], min_val=0, max_val=top)

    with nc.Block() as block:
        @block.sync
        def _(sp):
            def load(t, k, s):
                wait_apart(sp, c["ready"], (xt_done, t - RING + 1))
                row = entry(sp, t, 1, E * CAP + (E - 1) * P)
                sp.dma_start(x_t[:, s, :], gathered[bass.ds(row, P), :]).then_inc(x_loaded[s], 16)

            pipeline(sp, n_list, [load], RING)

        @block.tensor
        def _(pe):
            def transpose_x(t, k, s):
                pe.wait_ge(x_loaded[s], 16 * k + 16)
                wait(pe, xt_ready, t)
                for j in range(KD):
                    last = nc.tensor.transpose(ps_x[:, j, :], x_t[:, s, j * P:(j + 1) * P], ident[:])
                last.then_inc(xt_done, 1)

            at = {}

            def look_up(t, k, s):
                at["up"] = entry(pe, t, 0, E - 1)

            def look_down(t, k, s):
                at["down"] = entry(pe, t, 0, E - 1)

            def go_up(t, k, s):
                e = at["up"]
                pe.wait_ge(xt_ready, t + 1)
                wait(pe, h_ready, t - 1)
                for j in range(KD):
                    last = nc.tensor.matmul(ps_h[s % 2][:], xt[:, s % 2, j, :], w_up[:, j, bass.ts(e, width)], start=(j == 0), stop=(j == KD - 1))
                last.then_inc(h_done, 1)

            def transpose_h(t, k, s):
                pe.wait_ge(h_ready, t + 1)
                wait(pe, ht_ready, t)
                for j in range(blocks):
                    last = nc.tensor.transpose(ps_ht[:, j, :], h[:, s % 2, j * P:(j + 1) * P], ident[:])
                last.then_inc(ht_done, 1)

            def go_down(t, k, s):
                e = at["down"]
                pe.wait_ge(ht_ready, t + 1)
                wait(pe, y_ready, t)
                for j in range(blocks):
                    last = nc.tensor.matmul(ps_y[:], ht[:, s % 2, j, :], w_down[:, j, bass.ts(e, DM)], start=(j == 0), stop=(j == blocks - 1))
                last.then_inc(y_done, 1)

            pe.wait_ge(*weights)
            interleaved(pe, n_list, [(1, look_up), (3, look_down), (0, transpose_x), (1, go_up), (2, transpose_h), (3, go_down)], RING)

        @block.vector
        def _(dve):
            def hide(t, k, s):
                if relu:
                    e = entry(dve, t, 0, E - 1)
                dve.wait_ge(h_done, t + 1)
                wait(dve, ht_done, t - 1)
                if relu:
                    nc.vector.tensor_tensor(h[:, s % 2, :], ps_h[s % 2][:], b_up[:, bass.ts(e, width)], ALU.add).then_inc(h_ready, 1)
                else:
                    dve.wait_ge(sig_ready, t + 1)
                    nc.vector.tensor_tensor(act_g[:, s % 2, :], ps_h[s % 2][:, 0:hidden], sig[:, s % 2, :], ALU.mult).then_inc(gated, 1)
                    dve.wait_ge(gated, t + 1)
                    nc.vector.tensor_tensor(h[:, s % 2, :], ps_h[s % 2][:, hidden:2 * hidden], act_g[:, s % 2, :], ALU.mult).then_inc(h_ready, 1)

            def finish(t, k, s):
                if b_down is not None:
                    e = entry(dve, t, 0, E - 1)
                dve.wait_ge(y_done, t + 1)
                wait(dve, stored[s], 16 * k)
                if b_down is not None:
                    nc.vector.tensor_tensor(y[:, s, :], ps_y[:], b_down[:, bass.ts(e, DM)], ALU.add).then_inc(y_ready, 1)
                else:
                    nc.vector.tensor_copy(y[:, s, :], ps_y[:]).then_inc(y_ready, 1)

            dve.wait_ge(*weights)
            pipeline(dve, n_list, [nothing, hide, nothing, finish], RING)

        @block.scalar
        def _(act):
            def copy_x(t, k, s):
                act.wait_ge(xt_done, t + 1)
                wait(act, h_done, t - 1)
                nc.scalar.activation(xt[:, s % 2], ps_x[:], ACT.Copy).then_inc(xt_ready, 1)

            def sigmoid(t, k, s):
                if not relu:
                    act.wait_ge(h_done, t + 1)
                    wait(act, gated, t - 1)
                    nc.scalar.activation(sig[:, s % 2, :], ps_h[s % 2][:, 0:hidden], ACT.Sigmoid).then_inc(sig_ready, 1)

            def copy_h(t, k, s):
                act.wait_ge(ht_done, t + 1)
                wait(act, y_done, t - 1)
                nc.scalar.activation(ht[:, s % 2], ps_ht[:], ACT.Relu if relu else ACT.Copy).then_inc(ht_ready, 1)

            def store(t, k, s):
                act.wait_ge(y_ready, t + 1)
                act.dma_start(outputs[bass.ts(t, P), :], y[:, s, :]).then_inc(stored[s], 16)

            pipeline(act, n_list, [copy_x, sigmoid, copy_h, nothing, store], RING)
            for s in range(RING):
                act.wait_ge(stored[s], 16 * (n_list // RING))


SLOTS = 4


def project_qkv(nc, sb, pb, sem, c, x_dram, outputs, kept, sum_dram, w_qkv_dram, rope_dram, qkt_dram, v_dram, fetch):
    ident, mhalf = c["ident"], c["mhalf"]
    QK = 2 * DM
    w = sb("w_qkv", [P, KD, 3 * DM])
    x_t = sb("d_x", [P, 2, DM])
    idx = sb("d_idx", [P, 2, 2], U32)
    prob = sb("d_prob", [P, 2, 2])
    ye = [sb(f"d_ye{i}", [P, 2, DM]) for i in range(2)]
    part = sb("d_part", [P, 2, DM])
    x2 = sb("d_x2", [P, 2, DM])
    rope = sb("d_rope", [P, 2, 2, HD])
    stats = sb("d_stats", [P, 2, 6])
    mean_var = sb("d_mean_var", [P, 2, 2])
    var_eps = sb("d_var_eps", [P, 2])
    rstd = sb("d_rstd", [P, 2])
    xn = sb("d_xn", [P, 2, DM])
    xnt = sb("d_xnt", [P, 2, KD, P])
    by_cos = sb("d_by_cos", [P, 2, QK])
    by_sin = sb("d_by_sin", [P, 2, QK])
    qk = sb("d_qk", [P, 2, QK])
    hi = sb("d_hi", [P, 2, QK], FP32R)
    lo = sb("d_lo", [P, 2, QK])
    qkt = sb("d_qkt", [P, 2, 8, P])
    v_t = sb("d_v", [P, 2, DM])
    ps_xnt = pb("d_ps_xnt", [P, KD, P])
    ps_qkv = [pb(f"d_ps_qkv{s}", [P, 3 * DM]) for s in range(2)]
    ps_t = [pb(f"d_ps_t{i}", [P, 4, P]) for i in range(2)]
    w_loaded = sem("d_w_loaded")
    x_loaded = [sem(f"d_x_loaded{s}") for s in range(2)]
    (idx_ready, x2_steps, x2_ready, ln_steps, var_ready, rstd_ready, xn_ready, xnt_done, xnt_ready, qkv_done, roped,
     qk_ready, hi_ready, lo_ready, hit_done, lot_done, qkt_ready, v_ready) = (sem("d_" + n) for n in (
        "idx_ready", "x2_steps", "x2_ready", "ln_steps", "var_ready", "rstd_ready", "xn_ready", "xnt_done", "xnt_ready",
        "qkv_done", "roped", "qk_ready", "hi_ready", "lo_ready", "hit_done", "lot_done", "qkt_ready", "v_ready"))
    gathered = c["moved"]["d_gathered"]
    x2_stored = [sem(f"d_x2_stored{s}") for s in range(2)]
    qk_stored = [sem(f"d_qk_stored{s}") for s in range(2)]
    v_stored = [sem(f"d_v_stored{s}") for s in range(2)]
    rope_loaded = [sem(f"d_rope_loaded{s}") for s in range(2)]

    with nc.Block() as block:
        @block.sync
        def _(sp):
            sp.dma_start(w[:], w_qkv_dram.rearrange("(k p) n -> p k n", p=P)).then_inc(w_loaded, 16)

            def load(t, k, s):
                wait_apart(sp, c["ready"], (x2_ready, t - 1))
                sp.dma_start(x_t[:, s, :], x_dram[bass.ts(t, P), :]).then_inc(x_loaded[s], 16)

            def load_rope(t, k, s):
                wait_apart(sp, c["ready"], (roped, 3 * (t - 1)))
                sp.dma_start(rope[:, s], rope_dram[bass.ts(t, P), :].rearrange("p (a d) -> p a d", a=2)).then_inc(rope_loaded[s], 16)

            def store_x2(t, k, s):
                wait_apart(sp, c["ready"], (x2_ready, t + 1))
                sp.dma_start(sum_dram[bass.ts(t, P), :], x2[:, s, :]).then_inc(x2_stored[s], 16)

            def store_v(t, k, s):
                wait_apart(sp, c["ready"], (v_ready, t + 1))
                sp.dma_start(v_dram[bass.ts(t, P), :], v_t[:, s, :]).then_inc(v_stored[s], 16)

            def store_qk(t, k, s):
                wait_apart(sp, c["ready"], (qkt_ready, 2 * t + 2))
                sp.dma_start(qkt_dram[:, bass.ts(t, P)].rearrange("(j p) t -> p j t", p=P), qkt[:, s]).then_inc(qk_stored[s], 16)

            interleaved(sp, NT, [(1, load), (2, store_x2), (4, load_rope), (5, store_v), (7, store_qk)])
            for s in range(2):
                sp.wait_ge(x2_stored[s], 16 * (NT // 2))
                sp.wait_ge(v_stored[s], 16 * (NT // 2))
                sp.wait_ge(qk_stored[s], 16 * (NT // 2))

        @block.gpsimd
        def _(pool):
            def gather(t, k, s):
                wait(pool, x2_ready, t - 1)
                nc.gpsimd.tensor_copy(idx[:, s:s + 1, :], kept["pos"][:, bass.ds(t, 1), :]).then_inc(idx_ready, 1)
                nc.gpsimd.tensor_copy(prob[:, s:s + 1, :], kept["prob"][:, bass.ds(t, 1), :]).then_inc(idx_ready, 1)
                wait_apart(pool, c["ready"], (idx_ready, 2 * t + 2))
                for i in range(2):
                    nc.gpsimd.indirect_dma_start(
                        out=ye[i][:, s, :], out_offset=None, in_=outputs[:, :],
                        in_offset=bass.IndirectOffsetOnAxis(ap=idx[:, s, i:i + 1], axis=0)).then_inc(gathered[s], 16)

            def rsqrt(t, k, s):
                pool.wait_ge(var_ready, t + 1)
                nc.gpsimd.tensor_tensor(rstd[:, s:s + 1], var_eps[:, s:s + 1], mhalf[:, 0:1], ALU.pow).then_inc(rstd_ready, 1)

            def add_turned(t, k, s):
                pool.wait_ge(roped, 3 * t + 3)
                wait(pool, lo_ready, t - 1)
                wait(pool, hi_ready, t - 1)
                nc.gpsimd.tensor_tensor(qk[:, s, :], by_cos[:, s, :], by_sin[:, s, :], ALU.add).then_inc(qk_ready, 1)

            def rest(t, k, s):
                pool.wait_ge(hi_ready, t + 1)
                wait(pool, lot_done, t - 1)
                nc.gpsimd.tensor_tensor(lo[:, s, :], qk[:, s, :], hi[:, s, :].bitcast(FP32), ALU.subtract).then_inc(lo_ready, 1)

            interleaved(pool, NT, [(2, rsqrt), (0, gather), (5, add_turned), (6, rest)])

        @block.vector
        def _(dve):
            norm_chain = Chain(dve, ln_steps, 2)

            def norm(t, k, s):
                dve.wait_ge(x_loaded[s], 16 * k + 16)
                dve.wait_ge(gathered[s], 32 * k + 32)
                wait(dve, x2_stored[s], 16 * k)
                nc.vector.scalar_tensor_tensor(out=part[:, s, :], in0=ye[0][:, s, :], scalar=prob[:, s, 0:1], in1=x_t[:, s, :],
                                               op0=ALU.mult, op1=ALU.add).then_inc(x2_steps, 1)
                dve.wait_ge(x2_steps, t + 1)
                nc.vector.scalar_tensor_tensor(out=x2[:, s, :], in0=ye[1][:, s, :], scalar=prob[:, s, 1:2], in1=part[:, s, :],
                                               op0=ALU.mult, op1=ALU.add).then_inc(x2_ready, 1)
                dve.wait_ge(x2_ready, t + 1)
                norm_chain.at(t)
                norm_chain.step(nc.vector.bn_stats(stats[:, s, :], x2[:, s, :]))
                wait_apart(dve, c["ready"], (ln_steps, norm_chain.base + norm_chain.k))
                norm_chain.link(nc.vector.bn_aggr(mean_var[:, s, :], stats[:, s, :]))
                nc.vector.tensor_scalar(var_eps[:, s:s + 1], mean_var[:, s, 1:2], LN_EPS, None, ALU.add).then_inc(var_ready, 1)
                dve.wait_ge(rstd_ready, t + 1)
                wait(dve, xnt_done, t - 1)
                nc.vector.tensor_scalar(xn[:, s, :], x2[:, s, :], mean_var[:, s, 0:1], rstd[:, s:s + 1],
                                        ALU.subtract, ALU.mult).then_inc(xn_ready, 1)

            def turn(t, k, s):
                dve.wait_ge(qkv_done, t + 1)
                dve.wait_ge(rope_loaded[s], 16 * k + 16)
                wait(dve, qk_ready, t - 1)
                heads = ps_qkv[s][:, 0:QK].rearrange("p (h d) -> p h d", d=HD)
                pairs = ps_qkv[s][:, 0:QK].rearrange("p (h d two) -> p h d two", two=2, d=HD // 2)
                out = by_sin[:, s, :].rearrange("p (h d two) -> p h d two", two=2, d=HD // 2)
                sin = rope[:, s, 1, :].rearrange("p (d two) -> p d two", two=2)
                nc.vector.tensor_tensor(by_cos[:, s, :].rearrange("p (h d) -> p h d", d=HD), heads,
                                        rope[:, s, 0, :].unsqueeze(1).broadcast_to([P, 2 * NH, HD]), ALU.mult).then_inc(roped, 1)
                for i in range(2):
                    nc.vector.tensor_tensor(out[:, :, :, i], pairs[:, :, :, 1 - i],
                                            sin[:, :, i].unsqueeze(1).broadcast_to([P, 2 * NH, HD // 2]), ALU.mult).then_inc(roped, 1)

            def copy_lo(t, k, s):
                dve.wait_ge(lot_done, t + 1)
                wait(dve, qk_stored[s], 16 * k)
                nc.vector.tensor_copy(qkt[:, s, 4:8, :], ps_t[1][:]).then_inc(qkt_ready, 1)

            interleaved(dve, NT, [(2, norm), (5, turn), (7, copy_lo)])

        @block.scalar
        def _(act):
            act.wait_ge(x_loaded[1], 16)
            act.wait_ge(w_loaded, 16)
            fetch(act)

            def copy_xn(t, k, s):
                act.wait_ge(xnt_done, t + 1)
                wait(act, qkv_done, t - 1)
                nc.scalar.activation(xnt[:, s], ps_xnt[:], ACT.Copy).then_inc(xnt_ready, 1)

            def copy_v(t, k, s):
                act.wait_ge(qkv_done, t + 1)
                act.wait_ge(roped, 3 * t + 3)
                wait(act, v_stored[s], 16 * k)
                nc.scalar.activation(v_t[:, s, :], ps_qkv[s][:, QK:], ACT.Copy).then_inc(v_ready, 1)

            def round_qk(t, k, s):
                act.wait_ge(qk_ready, t + 1)
                wait(act, hit_done, t - 1)
                wait(act, lo_ready, t - 1)
                nc.scalar.activation(hi[:, s, :], qk[:, s, :], ACT.Copy).then_inc(hi_ready, 1)

            def copy_hi(t, k, s):
                act.wait_ge(hit_done, t + 1)
                wait(act, qk_stored[s], 16 * k)
                nc.scalar.activation(qkt[:, s, 0:4, :], ps_t[0][:], ACT.Copy).then_inc(qkt_ready, 1)

            interleaved(act, NT, [(3, copy_xn), (6, round_qk), (7, copy_hi), (5, copy_v)])

        @block.tensor
        def _(pe):
            pe.wait_ge(w_loaded, 16)

            def transpose_x(t, k, s):
                pe.wait_ge(xn_ready, t + 1)
                wait(pe, xnt_ready, t)
                for j in range(KD):
                    last = nc.tensor.transpose(ps_xnt[:, j, :], xn[:, s, j * P:(j + 1) * P], ident[:])
                last.then_inc(xnt_done, 1)

            def project(t, k, s):
                pe.wait_ge(xnt_ready, t + 1)
                wait(pe, roped, 3 * (t - 1))
                wait(pe, v_ready, t - 1)
                for n0, n1 in ((0, QK), (QK, 3 * DM)):
                    for j in range(KD):
                        last = nc.tensor.matmul(ps_qkv[s][:, n0:n1], xnt[:, s, j, :], w[:, j, n0:n1], start=(j == 0), stop=(j == KD - 1))
                last.then_inc(qkv_done, 1)

            def transpose_qk(t, k, s):
                pe.wait_ge(hi_ready, t + 1)
                wait(pe, qkt_ready, 2 * t)
                for j in range(4):
                    last = nc.tensor.transpose(ps_t[0][:, j, :], hi[:, s, j * P:(j + 1) * P].bitcast(FP32), ident[:])
                last.then_inc(hit_done, 1)
                pe.wait_ge(lo_ready, t + 1)
                for j in range(4):
                    last = nc.tensor.transpose(ps_t[1][:, j, :], lo[:, s, j * P:(j + 1) * P], ident[:])
                last.then_inc(lot_done, 1)

            interleaved(pe, NT, [(3, transpose_x), (7, transpose_qk), (4, project)])


def attention(nc, sb, pb, sem, c, qkt_dram, v_dram, headst_dram, sums_dram):
    ident = c["ident"]
    heads = BATCH * NH
    VR = HD + 1
    NC = SEQ // P
    KS = 4 * HD
    HALF = 4
    ks = sb("t_ks", [KS + 2, SLOTS, SEQ], FP32R)
    qs = sb("t_qs", [KS + 2, SLOTS, SEQ], FP32R)
    v_raw = sb("t_v_raw", [P, NC, SLOTS * HD])
    vs = sb("t_vs", [P, SLOTS, NC, VR])
    later = sb("t_later", [P, P], BF16)
    ident_b = sb("t_ident_b", [P, P], BF16)
    maxes = sb("t_maxes", [P, 2, NC, 2])
    row_max = sb("t_row_max", [P, 2, NC])
    neg_max = sb("t_neg_max", [NC, 2, P], FP32R)
    packs, at = [], 0
    for half in range(2):
        regions = [(kc, max(kc, HALF * half) * P, (HALF * (half + 1) - max(kc, HALF * half)) * P)
                   for kc in range(HALF * (half + 1))]
        for i in range(0, len(regions), 2):
            pack = []
            base = at
            for kc, q0, width in regions[i:i + 2]:
                pack.append((kc, q0, width, at - base, at))
                at += width
            packs.append((half, base, at - base, pack))
    probs = sb("t_probs", [P, at])
    att = sb("t_att", [VR, SLOTS, 2, HALF * P])
    ps_s = [pb(f"t_ps_s{i}", [P, 4 * P]) for i in range(2)]
    ps_st = [pb(f"t_ps_st{i}", [P, 8 * P]) for i in range(2)]
    ps_max = pb("t_ps_max", [NC, P])
    ps_o = pb("t_ps_o", [32 + VR, HALF * P])
    even = sb("t_even", [VR, HALF * P])
    pieces = [(qc, k0, min(k0 + 4 * P, (qc + 1) * P)) for qc in range(NC) for k0 in range(0, (qc + 1) * P, 4 * P)]
    NPC, NPK = len(pieces), len(packs)
    NP0 = sum(p[0] == 0 for p in packs)
    diagonal = [any(q0 == kc * P for kc, q0, *_ in p[3]) for p in packs]
    ND = sum(diagonal)
    filled, set_up = sem("t_filled"), sem("t_set_up")
    qk_loaded = [sem(f"t_qk_loaded{s}") for s in range(SLOTS)]
    row_loaded = [sem(f"t_row_loaded{s}") for s in range(SLOTS)]
    (v_loaded, vs_ready, s_done, piece_ready, max_ready, maxt_done, neg_ready, st_done, exp_ready, masked, av_done,
     even_ready, att_ready) = (sem("t_" + n) for n in (
        "v_loaded", "vs_ready", "s_done", "piece_ready", "max_ready", "maxt_done", "neg_ready", "st_done", "exp_ready",
        "masked", "av_done", "even_ready", "att_ready"))
    stored = [sem(f"t_stored{s}") for s in range(SLOTS)]

    with nc.Block() as block:
        @block.sync
        def _(sp):
            def place(k):
                if isinstance(k, int):
                    return k // (NH // SLOTS), k % (NH // SLOTS)
                batch = sp.snap(k // (NH // SLOTS))
                return batch, nc.s_assert_within(k - batch * (NH // SLOTS), 0, NH // SLOTS - 1,
                                                 skip_runtime_bounds_check_because="it is a remainder")

            def load(n, k, s):
                batch, group = place(k)
                wait_apart(sp, c["ready"], (st_done, NPK * (n - SLOTS) + NPK), (vs_ready, n if s == 0 else 0))
                if s == 0:
                    sp.dma_start(v_raw[:], v_dram[bass.ts(batch, SEQ), bass.ts(group, SLOTS * HD)]
                                 .rearrange("(c p) d -> p c d", p=P)).then_inc(v_loaded, 16)
                cols = bass.ts(batch, SEQ)
                for part in range(4):
                    q_part, k_part = part % 2, part // 2
                    for dst, which, hl in ((qs, 0, q_part), (ks, 1, k_part)):
                        first = hl * 2 * DM + which * DM + s * HD
                        sp.dma_start(dst[part * HD:(part + 1) * HD, s, :].bitcast(FP32),
                                     qkt_dram[bass.ds(group * (SLOTS * HD) + first, HD), cols]).then_inc(qk_loaded[s], 16)

            def row(n, k, s):
                wait_apart(sp, c["ready"], (neg_ready, n + 1))
                sp.dma_start(qs[KS + 1:KS + 2, s, :].bitcast(FP32).rearrange("o (c q) -> o c q", c=NC),
                             neg_max[:, s % 2, :].bitcast(FP32)).then_inc(row_loaded[s], 16)

            def store(n, k, s):
                batch, group = place(k)
                wait_apart(sp, c["ready"], (att_ready, 2 * n + 2))
                sp.dma_start(headst_dram[bass.ds(group * (SLOTS * HD) + s * HD, HD), bass.ts(batch, SEQ)],
                             att[0:HD, s].rearrange("p h q -> p (h q)")).then_inc(stored[s], 16)
                sp.dma_start(sums_dram[bass.ds(group * SLOTS + s, 1), bass.ts(batch, SEQ)],
                             att[HD:VR, s].rearrange("p h q -> p (h q)")).then_inc(stored[s], 16)

            sp.wait_ge(filled, 6)
            pipeline(sp, heads, [load, nothing, row, nothing, store], SLOTS)
            for s in range(SLOTS):
                sp.wait_ge(stored[s], 32 * (heads // SLOTS))

        @block.gpsimd
        def _(pool):
            nc.gpsimd.memset(later[:], 0.0).then_inc(filled, 1)
            nc.gpsimd.memset(ident_b[:], 0.0).then_inc(filled, 1)
            nc.gpsimd.memset(maxes[:], -3.0e38).then_inc(filled, 1)
            nc.gpsimd.memset(vs[:], 1.0).then_inc(filled, 1)
            pool.wait_ge(filled, 4)
            nc.gpsimd.memset(ks[KS:KS + 2].bitcast(FP32), 1.0).then_inc(filled, 1)
            pool.wait_ge(filled, 5)
            nc.gpsimd.memset(qs[KS:KS + 1].bitcast(FP32), 0.0).then_inc(filled, 1)
            pool.wait_ge(filled, 6)
            nc.gpsimd.affine_select(out=later[:], in_=later[:], compare_op=ALU.is_ge, fill=-1.0e30, base=0,
                                    pattern=[[-1, P]], channel_multiplier=1).then_inc(set_up, 1)
            nc.gpsimd.affine_select(out=ident_b[:], in_=ident_b[:], compare_op=ALU.not_equal, fill=1.0, base=0,
                                    pattern=[[-1, P]], channel_multiplier=1).then_inc(set_up, 1)

            def values(n, k, s):
                wait_apart(pool, c["ready"], (v_loaded, 16 * k + 16), (av_done, NPK * (n - SLOTS) + NPK))
                nc.gpsimd.tensor_copy(vs[:, s, :, 0:HD], v_raw[:, :, s * HD:(s + 1) * HD]).then_inc(vs_ready, 1)

            def mask(n, k, s):
                for i, (half, base, width, pack) in enumerate(packs):
                    if diagonal[i]:
                        wait_apart(pool, c["ready"], (exp_ready, NPK * n + i + 1))
                        for kc, q0, w, off, col in pack:
                            if q0 == kc * P:
                                block_ = probs[:, col:col + P]
                                last = nc.gpsimd.affine_select(out=block_, in_=block_, compare_op=ALU.is_ge, fill=0.0, base=0,
                                                               pattern=[[1, P]], channel_multiplier=-1)
                        last.then_inc(masked, 1)

            pipeline(pool, heads, [values, nothing, mask], SLOTS)

        def ticks(eng, tick):
            def at(n, k, s, live):
                tick(lambda d: (n - d, k + (s - d) // SLOTS, (s - d) % SLOTS), live)

            for n in range(SLOTS):
                at(n, 0, n, lambda d: n >= d)
            with eng.Fori(1, heads // SLOTS) as turn:
                for s in range(SLOTS):
                    at(turn * SLOTS + s, turn, s, lambda d: True)
            for n in range(heads, heads + 3):
                at(n, heads // SLOTS, n - heads, lambda d: n - d < heads)

        @block.vector
        def _(dve):
            dve.wait_ge(filled, 6)

            def maximum(n, s, i):
                qc, k0, k1 = pieces[i]
                dve.wait_ge(s_done, NPC * n + i + 1)
                nc.vector.reduce_max(maxes[:, s % 2, qc, k0 // (4 * P):k0 // (4 * P) + 1], ps_s[i % 2][:, 0:k1 - k0],
                                     AXX).then_inc(piece_ready, 1)

            def outputs(n, k, s, half):
                dve.wait_ge(even_ready, 2 * n + half + 1)
                if half == 0:
                    wait(dve, stored[s], 32 * k)
                    nc.vector.tensor_copy(att[:, s, half, 0:P], even[:, 0:P])
                    nc.vector.tensor_tensor(att[:, s, half, P:], ps_o[32:32 + VR, P:], even[:, P:], ALU.add).then_inc(att_ready, 1)
                else:
                    nc.vector.tensor_tensor(att[:, s, half, :], ps_o[32:32 + VR, :], even[:], ALU.add).then_inc(att_ready, 1)

            def tick(ago, live):
                n, _, s = ago(0)
                for i in range(NPK):
                    if live(0):
                        maximum(n, s, 2 * i)
                        maximum(n, s, 2 * i + 1)
                    if i == 1 and live(3):
                        outputs(*ago(3), 1)
                    if i == NP0 + 1 and live(2):
                        outputs(*ago(2), 0)
                if live(0):
                    wait(dve, maxt_done, n - 1)
                    dve.wait_ge(piece_ready, NPC * n + NPC)
                    nc.vector.reduce_max(row_max[:, s % 2, :], maxes[:, s % 2], AXX).then_inc(max_ready, 1)

            ticks(dve, tick)

        @block.scalar
        def _(act):
            def negate(n, k, s):
                act.wait_ge(maxt_done, n + 1)
                wait(act, row_loaded[(s - 2) % SLOTS], 16 * (k + 1 if s >= 2 else k))
                nc.scalar.activation(neg_max[:, s % 2, :], ps_max[:], ACT.Copy, scale=-1.0).then_inc(neg_ready, 1)

            def exponentials(n, i):
                half, base, width, pack = packs[i]
                act.wait_ge(st_done, NPK * n + i + 1)
                wait(act, av_done, NPK * (n - 1) + i + 1)
                nc.scalar.activation(probs[:, base:base + width], ps_st[i % 2][:, 0:width], ACT.Exp,
                                     scale=HD ** -0.5).then_inc(exp_ready, 1)

            def even_chunks(n, k, s, half):
                act.wait_ge(av_done, NPK * n + (NPK if half else NP0))
                wait(act, att_ready, 2 * n + half)
                nc.scalar.activation(even[:], ps_o[0:VR], ACT.Copy).then_inc(even_ready, 1)

            def tick(ago, live):
                for i in range(NPK):
                    if live(2):
                        exponentials(ago(2)[0], i)
                    if i == 0 and live(1):
                        negate(*ago(1))
                    if i == 1 and live(3):
                        even_chunks(*ago(3), 1)
                    if i == 3 and live(2):
                        even_chunks(*ago(2), 0)

            ticks(act, tick)

        @block.tensor
        def _(pe):
            pe.wait_ge(filled, 6)
            pe.wait_ge(set_up, 2)

            def piece(n, s, i):
                qc, k0, k1 = pieces[i]
                wait(pe, piece_ready, NPC * n + i - 1)
                diag = qc * P - k0
                inside = 0 <= diag < k1 - k0
                last = nc.tensor.matmul(ps_s[i % 2][:, 0:k1 - k0], qs[0:KS + 1, s, qc * P:(qc + 1) * P], ks[0:KS + 1, s, k0:k1],
                                        start=True, stop=not inside)
                if inside:
                    last = nc.tensor.matmul(ps_s[i % 2][:, diag:diag + P], ident_b[:], later[:], start=False, stop=True)
                last.then_inc(s_done, 1)

            def pack_scores(n, s, i):
                wait(pe, exp_ready, NPK * n + i - 1)
                for kc, q0, width, off, col in packs[i][3]:
                    last = nc.tensor.matmul(ps_st[i % 2][:, off:off + width], ks[:, s, kc * P:(kc + 1) * P], qs[:, s, q0:q0 + width],
                                            start=True, stop=True)
                last.then_inc(st_done, 1)

            def average(n, s, i):
                half, base, _, pack = packs[i]
                if diagonal[i]:
                    pe.wait_ge(masked, ND * n + sum(diagonal[:i + 1]))
                else:
                    pe.wait_ge(exp_ready, NPK * n + i + 1)
                if i == 0:
                    pe.wait_ge(vs_ready, n + 1)
                    wait(pe, att_ready, 2 * n)
                if i == NP0:
                    pe.wait_ge(att_ready, 2 * n + 1)
                for kc, q0, width, off, col in pack:
                    at = q0 - half * HALF * P
                    odd = kc % 2
                    last = nc.tensor.matmul(ps_o[32 * odd:32 * odd + VR, at:at + width], vs[:, s, kc, :], probs[:, col:col + width],
                                            start=(kc < 2), stop=(kc >= HALF * (half + 1) - 2))
                last.then_inc(av_done, 1)

            def tick(ago, live):
                n, k, s = ago(0)
                n2, k2, s2 = ago(2)
                if live(2):
                    pe.wait_ge(row_loaded[s2], 16 * k2 + 16)
                for i in range(NPK):
                    if live(2):
                        pack_scores(n2, s2, i)
                    if i == 0 and live(1):
                        n1, _, s1 = ago(1)
                        pe.wait_ge(max_ready, n1 + 1)
                        wait(pe, neg_ready, n1)
                        nc.tensor.transpose(ps_max[:], row_max[:, s1 % 2, :], ident[:]).then_inc(maxt_done, 1)

                    def pieces_of_step():
                        if live(0):
                            if i == 0:
                                pe.wait_ge(qk_loaded[s], 128 * k + 128)
                            piece(n, s, 2 * i)
                            piece(n, s, 2 * i + 1)

                    def average_of_step():
                        if i < 2 and live(3):
                            n3, _, s3 = ago(3)
                            average(n3, s3, NPK - 2 + i)
                        if i >= 2 and live(2):
                            average(n2, s2, i - 2)

                    pieces_of_step()
                    average_of_step()

            ticks(pe, tick)


FS = 256


def finish(nc, sb, pb, sem, c, x_dram, xn_dram, outputs, kept, sg_dram, su_dram, sd_dram, out_dram):
    ident = c["ident"]
    w_up = sb("f_w_up", [P, KD, 2 * FS])
    w_down = sb("f_w_down", [P, FS // P, DM])
    x_t = sb("f_x", [P, 2, DM])
    xn = sb("f_xn", [P, 2, DM])
    idx = sb("f_idx", [P, 2, 2], U32)
    prob = sb("f_prob", [P, 2, 2])
    ye = [sb(f"f_ye{i}", [P, 2, DM]) for i in range(2)]
    one_more = sb("f_one_more", [P, 2, DM])
    routed = sb("f_routed", [P, 2, DM])
    y = sb("f_y", [P, 2, DM])
    xnt = sb("f_xnt", [P, 2, KD, P])
    sig = sb("f_sig", [P, 2, FS])
    gated = sb("f_gated", [P, 2, FS])
    h = sb("f_h", [P, 2, FS])
    ht = sb("f_ht", [P, 2, FS // P, P])
    ps_x = pb("f_ps_x", [P, KD, P])
    ps_h = [pb(f"f_ps_h{s}", [P, 2 * FS]) for s in range(2)]
    ps_ht = pb("f_ps_ht", [P, FS // P, P])
    ps_y = pb("f_ps_y", [P, DM])
    w_loaded = sem("f_w_loaded")
    x_loaded = [sem(f"f_x_loaded{s}") for s in range(2)]
    xn_loaded = [sem(f"f_xn_loaded{s}") for s in range(2)]
    gathered = c["moved"]["f_gathered"]
    stored = [sem(f"f_stored{s}") for s in range(2)]
    idx_ready, sum_steps, routed_ready, xt_done, xt_ready, h_done, sig_ready, gated_ready, h_ready, ht_done, ht_ready, \
        y_done, y_ready = (sem("f_" + n) for n in (
            "idx_ready", "sum_steps", "routed_ready", "xt_done", "xt_ready", "h_done", "sig_ready", "gated_ready", "h_ready",
            "ht_done", "ht_ready", "y_done", "y_ready"))

    with nc.Block() as block:
        @block.sync
        def _(sp):
            sp.dma_start(w_up[:, :, 0:FS], sg_dram.rearrange("(k p) n -> p k n", p=P)).then_inc(w_loaded, 16)
            sp.dma_start(w_up[:, :, FS:2 * FS], su_dram.rearrange("(k p) n -> p k n", p=P)).then_inc(w_loaded, 16)
            sp.dma_start(w_down[:], sd_dram.rearrange("(k p) n -> p k n", p=P)).then_inc(w_loaded, 16)

            def load_xn(t, k, s):
                wait_apart(sp, c["ready"], (xt_done, t - 1))
                sp.dma_start(xn[:, s, :], xn_dram[bass.ts(t, P), :]).then_inc(xn_loaded[s], 16)

            def load_x(t, k, s):
                wait_apart(sp, c["ready"], (routed_ready, t - 1))
                sp.dma_start(x_t[:, s, :], x_dram[bass.ts(t, P), :]).then_inc(x_loaded[s], 16)

            def store(t, k, s):
                wait_apart(sp, c["ready"], (y_ready, t + 1))
                sp.dma_start(out_dram[bass.ts(t, P), :], y[:, s, :]).then_inc(stored[s], 16)

            pipeline(sp, NT, [load_xn, nothing, load_x, nothing, store])
            for s in range(2):
                sp.wait_ge(stored[s], 16 * (NT // 2))

        @block.gpsimd
        def _(pool):
            def gather(t, k, s):
                wait(pool, routed_ready, t - 1)
                nc.gpsimd.tensor_copy(idx[:, s:s + 1, :], kept["pos"][:, bass.ds(t, 1), :]).then_inc(idx_ready, 1)
                nc.gpsimd.tensor_copy(prob[:, s:s + 1, :], kept["prob"][:, bass.ds(t, 1), :]).then_inc(idx_ready, 1)
                wait_apart(pool, c["ready"], (idx_ready, 2 * t + 2))
                for i in range(2):
                    nc.gpsimd.indirect_dma_start(
                        out=ye[i][:, s, :], out_offset=None, in_=outputs[:, :],
                        in_offset=bass.IndirectOffsetOnAxis(ap=idx[:, s, i:i + 1], axis=0)).then_inc(gathered[s], 16)

            pipeline(pool, NT, [nothing, nothing, gather])

        @block.vector
        def _(dve):
            def add_routed(t, k, s):
                dve.wait_ge(x_loaded[s], 16 * k + 16)
                dve.wait_ge(gathered[s], 32 * k + 32)
                wait(dve, y_ready, t - 1)
                nc.vector.scalar_tensor_tensor(out=one_more[:, s, :], in0=ye[0][:, s, :], scalar=prob[:, s, 0:1], in1=x_t[:, s, :],
                                               op0=ALU.mult, op1=ALU.add).then_inc(sum_steps, 1)
                dve.wait_ge(sum_steps, t + 1)
                nc.vector.scalar_tensor_tensor(out=routed[:, s, :], in0=ye[1][:, s, :], scalar=prob[:, s, 1:2], in1=one_more[:, s, :],
                                               op0=ALU.mult, op1=ALU.add).then_inc(routed_ready, 1)

            def gate(t, k, s):
                dve.wait_ge(sig_ready, t + 1)
                nc.vector.tensor_tensor(gated[:, s, :], ps_h[s][:, 0:FS], sig[:, s, :], ALU.mult).then_inc(gated_ready, 1)
                dve.wait_ge(gated_ready, t + 1)
                wait(dve, ht_done, t - 1)
                nc.vector.tensor_tensor(h[:, s, :], ps_h[s][:, FS:2 * FS], gated[:, s, :], ALU.mult).then_inc(h_ready, 1)

            def add_shared(t, k, s):
                dve.wait_ge(y_done, t + 1)
                dve.wait_ge(routed_ready, t + 1)
                wait(dve, stored[s], 16 * k)
                nc.vector.tensor_tensor(y[:, s, :], routed[:, s, :], ps_y[:], ALU.add).then_inc(y_ready, 1)

            pipeline(dve, NT, [nothing, nothing, gate, add_routed, add_shared], order=(4, 3, 2))

        @block.scalar
        def _(act):
            def copy_x(t, k, s):
                act.wait_ge(xt_done, t + 1)
                wait(act, h_done, t - 1)
                nc.scalar.activation(xnt[:, s], ps_x[:], ACT.Copy).then_inc(xt_ready, 1)

            def sigmoid(t, k, s):
                act.wait_ge(h_done, t + 1)
                wait(act, gated_ready, t - 1)
                nc.scalar.activation(sig[:, s, :], ps_h[s][:, 0:FS], ACT.Sigmoid).then_inc(sig_ready, 1)

            def copy_h(t, k, s):
                act.wait_ge(ht_done, t + 1)
                wait(act, y_done, t - 1)
                nc.scalar.activation(ht[:, s], ps_ht[:], ACT.Copy).then_inc(ht_ready, 1)

            pipeline(act, NT, [nothing, copy_x, sigmoid, copy_h])

        @block.tensor
        def _(pe):
            pe.wait_ge(w_loaded, 48)

            def transpose_x(t, k, s):
                pe.wait_ge(xn_loaded[s], 16 * k + 16)
                wait(pe, xt_ready, t)
                for j in range(KD):
                    last = nc.tensor.transpose(ps_x[:, j, :], xn[:, s, j * P:(j + 1) * P], ident[:])
                last.then_inc(xt_done, 1)

            def go_up(t, k, s):
                pe.wait_ge(xt_ready, t + 1)
                wait(pe, h_ready, t - 1)
                for j in range(KD):
                    last = nc.tensor.matmul(ps_h[s][:], xnt[:, s, j, :], w_up[:, j, :], start=(j == 0), stop=(j == KD - 1))
                last.then_inc(h_done, 1)

            def transpose_h(t, k, s):
                pe.wait_ge(h_ready, t + 1)
                wait(pe, ht_ready, t)
                for j in range(FS // P):
                    last = nc.tensor.transpose(ps_ht[:, j, :], h[:, s, j * P:(j + 1) * P], ident[:])
                last.then_inc(ht_done, 1)

            def go_down(t, k, s):
                pe.wait_ge(ht_ready, t + 1)
                wait(pe, y_ready, t)
                for j in range(FS // P):
                    last = nc.tensor.matmul(ps_y[:], ht[:, s, j, :], w_down[:, j, :], start=(j == 0), stop=(j == FS // P - 1))
                last.then_inc(y_done, 1)

            pipeline(pe, NT, [nothing, transpose_x, go_up, transpose_h, go_down], order=(1, 4, 2, 3))


def build(nc, x, w_in, w_abc, w_out, norm_w, gate_w, gate_b, w1, b1, w2, b2, w_qkv, w_o, rope, w_route, w_gu, w_d,
          sg, su, sd, out):
    E0, E1 = gate_w.shape[1], w_route.shape[1]
    H0, F1 = w1.shape[2], w_d.shape[1]
    flat = lambda a: a.rearrange("b t m -> (b t) m")

    def scratch(name, shape):
        return nc.dram_tensor(name, shape, FP32).ap()

    used = []

    def phase(build_it, *args, **more):
        with ExitStack() as own:
            def own_sem(n):
                s = own.enter_context(nc.semaphore(n))
                used.append(s.num)
                return s

            build_it(nc, lambda n, s, d=FP32: own.enter_context(nc.sbuf_tensor(n, s, d)),
                     lambda n, s, d=FP32: own.enter_context(nc.psum_tensor(n, s, d)),
                     own_sem, *args, **more)

    def router_keep(own, name, E):
        sb = lambda n, s, d=FP32: own.enter_context(nc.sbuf_tensor(name + n, s, d))
        return {"pos": sb("pos_all", [P, NT, 2], U32), "prob": sb("prob_all", [P, NT, 2]),
                "tiles": sb("tile_list", [1, 2, 2 * NT + E], U32)}

    xi_dram, abc_dram = scratch("xi_dram", [TOK, DI]), scratch("abc_dram", [TOK, 3 * NS])
    x1_dram, x2_dram, x3_dram = (scratch(n, [TOK, DM]) for n in ("x1_dram", "x2_dram", "x3_dram"))
    xn4_dram, v_dram = (scratch(n, [TOK, DM]) for n in ("xn4_dram", "v_dram"))
    headst_dram = scratch("headst_dram", [DM, TOK])
    sums_dram, inv_dram = scratch("sums_dram", [NH, TOK]), scratch("inv_dram", [NH, TOK])
    qkt_dram = scratch("qkt_dram", [4 * DM, TOK])
    gathered = [scratch(f"gathered{i}_dram", [E * (CAP + P), DM]) for i, E in enumerate((E0, E1))]
    outputs = [scratch(f"outputs{i}_dram", [(2 * NT + E) * P, DM]) for i, E in enumerate((E0, E1))]

    with ExitStack() as whole:
        keep = lambda n, s, d=FP32: whole.enter_context(nc.sbuf_tensor(n, s, d))
        sem = lambda n: whole.enter_context(nc.semaphore(n))
        c = constants(nc, keep, sem)
        moe0_loaded, moe1_loaded = sem("moe0_loaded"), sem("moe1_loaded")
        c["moved"] = {n: [sem(f"{n}{s}") for s in range(2)] for n in ("r0_scattered", "d_gathered", "r1_scattered", "f_gathered")}
        x_in = flat(x)
        kept = router_keep(whole, "r0_", E0)
        with ExitStack() as weights:
            wsb = lambda n, s, d=FP32: weights.enter_context(nc.sbuf_tensor(n, s, d))
            w1_sb, w2_sb = wsb("w1_sb", [P, KD, E0 * H0]), wsb("w2_sb", [P, H0 // P, E0 * DM])
            b1_sb, b2_sb = wsb("b1_sb", [P, E0 * H0]), wsb("b2_sb", [P, E0 * DM])
            fetch = lambda eng: load_moe0(eng, moe0_loaded, w1_sb, w1, w2_sb, w2, b1_sb, b1, b2_sb, b2)
            phase(ssm_project, c, x_in, xi_dram, abc_dram, w_in, w_abc, fetch)
            phase(ssm_scan, c, x_in, xi_dram, abc_dram, w_out, norm_w, x1_dram)
            phase(route, c, "r0_", E0, x1_dram, None, gathered[0], gate_w, gate_b, kept)
            phase(run_experts, c, "m0_", E0, gathered[0], outputs[0], kept, (H0, w1_sb, b1_sb), (H0 // P, w2_sb, b2_sb),
                  (moe0_loaded, 16 * (KD + H0 // P + 2)))
        wsb = lambda n, s, d=FP32: whole.enter_context(nc.sbuf_tensor(n, s, d))
        wgu_sb, wd_sb = wsb("wgu_sb", [P, KD, E1 * 2 * F1]), wsb("wd_sb", [P, F1 // P, E1 * DM])
        fetch = lambda eng: load_moe1(eng, moe1_loaded, wgu_sb, w_gu, wd_sb, w_d)
        phase(project_qkv, c, x1_dram, outputs[0], kept, x2_dram, w_qkv, rope, qkt_dram, v_dram, fetch)
        with nc.Block() as block:
            @block.gpsimd
            def _(pool):
                pool.sem_clear(range(min(used), max(used) + 1))

        phase(attention, c, qkt_dram, v_dram, headst_dram, sums_dram)
        phase(invert, sums_dram, inv_dram)
        kept = router_keep(whole, "r1_", E1)
        phase(route, c, "r1_", E1, None, xn4_dram, gathered[1], w_route, None, kept,
              attn=(headst_dram, inv_dram, w_o, x2_dram, x3_dram))
        phase(run_experts, c, "m1_", E1, gathered[1], outputs[1], kept, (2 * F1, wgu_sb, None), (F1 // P, wd_sb, None),
              (moe1_loaded, 16 * (KD + 1)))
        phase(finish, c, x3_dram, xn4_dram, outputs[1], kept, sg, su, sd, flat(out))


def invert(nc, sb, pb, sem, sums_dram, inv_dram):
    per = NH * TOK // P
    sums, inv = sb("i_sums", [P, per]), sb("i_inv", [P, per])
    sums_loaded, inv_ready, inv_stored = sem("i_sums_loaded"), sem("i_inv_ready"), sem("i_inv_stored")

    def spread(dram):
        return dram.rearrange("h (c t) -> (h c) t", t=per)

    with nc.Block() as block:
        @block.sync
        def _(sp):
            sp.dma_start(sums[:], spread(sums_dram)).then_inc(sums_loaded, 16)
            sp.wait_ge(inv_ready, 1)
            sp.dma_start(spread(inv_dram), inv[:]).then_inc(inv_stored, 16)
            sp.wait_ge(inv_stored, 16)

        @block.vector
        def _(dve):
            dve.wait_ge(sums_loaded, 16)
            nc.vector.reciprocal(inv[:], sums[:]).then_inc(inv_ready, 1)


def load_moe0(eng, loaded, w1_sb, w1, w2_sb, w2, b1_sb, b1, b2_sb, b2):
    H0 = w1.shape[2]
    for j in range(KD):
        eng.dma_start(w1_sb[:, j, :].rearrange("p (e h) -> p e h", h=H0),
                     w1[:, j * P:(j + 1) * P, :].rearrange("e p h -> p e h")).then_inc(loaded, 16)
    for j in range(H0 // P):
        eng.dma_start(w2_sb[:, j, :].rearrange("p (e h) -> p e h", h=DM),
                     w2[:, j * P:(j + 1) * P, :].rearrange("e p h -> p e h")).then_inc(loaded, 16)
    for dst, src in ((b1_sb, b1), (b2_sb, b2)):
        eng.dma_start(dst[:], src.rearrange("e h -> (e h)").partition_broadcast(P)).then_inc(loaded, 16)
    return 16 * (KD + H0 // P + 2)


def load_moe1(eng, loaded, wgu_sb, w_gu, wd_sb, w_d):
    for j in range(KD):
        eng.dma_start(wgu_sb[:, j, :].rearrange("p (e h) -> p e h", h=w_gu.shape[2]),
                     w_gu[:, j * P:(j + 1) * P, :].rearrange("e p h -> p e h")).then_inc(loaded, 16)
    eng.dma_start(wd_sb[:, 0, :].rearrange("p (e h) -> p e h", h=DM), w_d.rearrange("e p h -> p e h")).then_inc(loaded, 16)
    return 16 * (KD + 1)


_OUTS = [((4, 1024, 256), 'float32')]


def kernel(**inputs):
    import numpy as _np
    import concourse.bacc as _bacc
    from concourse import mybir as _mybir
    from concourse.bass_utils import run_bass_kernel_spmd as _run

    a = inputs
    freq = 10000.0 ** (_np.arange(0, HD, 2, dtype=_np.float32) / _np.float32(HD))
    angle = _np.arange(SEQ, dtype=_np.float32)[:, None] / freq[None, :].astype(_np.float32)
    cos, sin = _np.cos(angle), _np.sin(angle)
    rope = _np.concatenate([_np.repeat(cos, 2, axis=1), _np.stack([-sin, sin], axis=-1).reshape(SEQ, HD)], axis=1)
    laid_out = {
        "x": a["L0_attn_x"], "w_in": a["L0_attn_W_in"],
        "w_abc": _np.concatenate([a["L0_attn_W_A"], a["L0_attn_W_B"], a["L0_attn_W_C"]], axis=1),
        "w_out": a["L0_attn_W_out"], "norm_w": _np.reshape(a["L0_attn_norm_w"], (KI, P)).T,
        "gate_w": a["L0_ffn_gate_w"].T, "gate_b": _np.reshape(a["L0_ffn_gate_b"], (1, -1)),
        "w1": a["L0_ffn_w1"], "b1": a["L0_ffn_b1"], "w2": a["L0_ffn_w2"], "b2": a["L0_ffn_b2"],
        "w_qkv": a["L1_attn_W_qkv"].T, "w_o": a["L1_attn_W_o"].T,
        "rope": _np.tile(rope.astype(_np.float32), (BATCH, 1)),
        "w_route": a["L1_ffn_Wr"], "w_gu": _np.concatenate([a["L1_ffn_Wg"], a["L1_ffn_Wu"]], axis=2),
        "w_d": a["L1_ffn_Wd"], "sg": a["L1_ffn_Sg"], "su": a["L1_ffn_Su"], "sd": a["L1_ffn_Sd"],
    }
    nc = _bacc.Bacc("TRN2", target_bir_lowering=False, num_devices=1)
    arrays, args = {}, []
    for name, value in laid_out.items():
        value = _np.ascontiguousarray(value)
        arrays[f"in_{name}_dram"] = value
        args.append(nc.dram_tensor(f"in_{name}_dram", value.shape, _mybir.dt.from_np(value.dtype), kind="ExternalInput").ap())
    for i, (shape, dtype) in enumerate(_OUTS):
        args.append(nc.dram_tensor(f"out_{i}_dram", shape, _mybir.dt.from_np(_np.dtype(dtype)), kind="ExternalOutput").ap())
    build(nc, *args)
    r = _run(nc, [arrays], core_ids=[0])
    return r.results[0]["out_0_dram"]
```
